# Optimizing a Trainium2 kernel written in Bass

```python
import numpy as np
import jax
import jax.numpy as jnp

def _softmax(x, axis=-1):
    return jax.nn.softmax(x, axis=axis)

def _gelu(x):
    return jax.nn.gelu(x, approximate=True)

def _silu(x):
    return jax.nn.silu(x)

def _sigmoid(x):
    return jax.nn.sigmoid(x)

def _layernorm(x, axis=-1, eps=1e-05):
    m = jnp.mean(x, axis=axis, keepdims=True)
    v = jnp.var(x, axis=axis, keepdims=True)
    return (x - m) / jnp.sqrt(v + eps)

def _scatter_add(tgt, idx, src, axis=0):
    return tgt.at[idx].add(src)

def _segment_sum(src, seg, n):
    return jax.ops.segment_sum(src, seg, n)
kernel_name = 'mk_seq_preln_d2_jaxref_r4_984b71'

def setup_inputs(seed: int=0):
    np.random.seed(seed)
    _w = jnp.asarray

    def _L0_attn_setup():
        import jax, jax.numpy as jnp
        import numpy as np
        EPS_LN = 1e-06
        STAB = 0.001

        def layer_norm(x, gamma, beta):
            mu = jnp.mean(x, axis=-1, keepdims=True)
            var = jnp.mean(jnp.square(x - mu), axis=-1, keepdims=True)
            return (x - mu) * jax.lax.rsqrt(var + EPS_LN) * gamma + beta
        key = jax.random.key(seed)
        B, L, E, H, F = (8, 512, 256, 16, 1024)
        dh = E // H
        ks = jax.random.split(key, 12)
        s_attn = 1.0 / np.sqrt(E)
        s_ffn1 = 1.0 / np.sqrt(E)
        s_ffn2 = 1.0 / np.sqrt(F)
        return {'x': jax.random.normal(ks[0], (B, L, E), jnp.float32), 'gamma1': jnp.ones((E,), jnp.float32), 'beta1': jnp.zeros((E,), jnp.float32), 'wq': jax.random.normal(ks[1], (E, H, dh), jnp.float32) * s_attn, 'wk': jax.random.normal(ks[2], (E, H, dh), jnp.float32) * s_attn, 'wv': jax.random.normal(ks[3], (E, H, dh), jnp.float32) * s_attn, 'wo': jax.random.normal(ks[4], (H, dh, E), jnp.float32) * s_attn, 'w1': jax.random.normal(ks[5], (E, F), jnp.float32) * s_ffn1, 'b1': jnp.zeros((F,), jnp.float32), 'w2': jax.random.normal(ks[6], (F, E), jnp.float32) * s_ffn2, 'b2': jnp.zeros((E,), jnp.float32)}
    _L0_attn_in = _L0_attn_setup()

    def _L0_ffn_setup():
        import jax, jax.numpy as jnp
        import numpy as np
        D_MODEL = 256
        M = 64
        INNER = 16
        key = jax.random.key(seed)
        ks = jax.random.split(key, 9)

        def init(k, shape, fan_in):
            bound = 1.0 / np.sqrt(fan_in)
            return jax.random.uniform(k, shape, jnp.float32, -bound, bound)
        x = jax.random.normal(ks[0], (16, 1024, D_MODEL), dtype=jnp.float32)
        Win = init(ks[1], (D_MODEL, M), D_MODEL)
        bin_ = init(ks[2], (M,), D_MODEL)
        W1 = init(ks[3], (M, INNER), 1)
        b1 = init(ks[4], (M, INNER), 1)
        W2 = init(ks[5], (M, INNER), INNER)
        b2 = init(ks[6], (M,), INNER)
        Wout = init(ks[7], (M, D_MODEL), M)
        bout = init(ks[8], (D_MODEL,), M)
        return {'x': x, 'Win': Win, 'bin_': bin_, 'W1': W1, 'b1': b1, 'W2': W2, 'b2': b2, 'Wout': Wout, 'bout': bout}
    _L0_ffn_in = _L0_ffn_setup()

    def _L1_attn_setup():
        import jax, jax.numpy as jnp
        import numpy as np
        DIM = 256
        HEADS = 16
        DIM_HEAD = DIM // HEADS
        LATENT = DIM // 4
        SCALE = DIM_HEAD ** (-0.5)
        key = jax.random.key(seed)
        ks = jax.random.split(key, 8)
        B, S = (2, 512)
        init = lambda k, shape, fan_in: jax.random.normal(k, shape, jnp.float32) * fan_in ** (-0.5)
        return {'x': jax.random.normal(ks[0], (B, S, DIM), jnp.float32), 'Wq': init(ks[1], (DIM, DIM), DIM), 'bq': jnp.zeros((DIM,), jnp.float32), 'Wl': init(ks[2], (DIM, LATENT), DIM), 'bl': jnp.zeros((LATENT,), jnp.float32), 'Wk': init(ks[3], (LATENT, DIM), LATENT), 'bk': jnp.zeros((DIM,), jnp.float32), 'Wv': init(ks[4], (LATENT, DIM), LATENT), 'bv': jnp.zeros((DIM,), jnp.float32), 'Wo': init(ks[5], (DIM, DIM), DIM), 'bo': jnp.zeros((DIM,), jnp.float32)}
    _L1_attn_in = _L1_attn_setup()

    def _L1_ffn_setup():
        import jax, jax.numpy as jnp
        import numpy as np
        import math
        GOLDEN_CENTER = 1.0 / math.e
        GOLDEN_LOWER = 0.5 - math.log(4.0 / 3.0)
        GOLDEN_UPPER = 0.5
        B, T, D = (4, 512, 256)
        E = 8
        I = 1024 // (E // 2)

        def _routing_weights(x, Wr, temperature):
            inh = jax.nn.sigmoid(x @ Wr / temperature)
            in_zone = (inh >= GOLDEN_LOWER) & (inh <= GOLDEN_UPPER)
            dist = jnp.abs(inh - GOLDEN_CENTER)
            w = jnp.exp(-dist / 0.1) * in_zone.astype(x.dtype)
            wsum = w.sum(axis=-1, keepdims=True)
            no_expert = wsum < 1e-08
            fb = jnp.exp(-dist / 0.3)
            _, top2 = jax.lax.top_k(fb, 2)
            fb_mask = jax.nn.one_hot(top2, E, dtype=x.dtype).sum(axis=-2)
            fb_w = fb * fb_mask
            fb_w = fb_w / jnp.clip(fb_w.sum(axis=-1, keepdims=True), 1e-08)
            w = jnp.where(no_expert, fb_w, w)
            wsum = w.sum(axis=-1, keepdims=True)
            return w / jnp.clip(wsum, 1e-08)
        key = jax.random.key(seed)
        k = jax.random.split(key, 6)
        s_d = 1.0 / math.sqrt(D)
        s_i = 1.0 / math.sqrt(I)
        return {'x': jax.random.normal(k[0], (B, T, D), jnp.float32), 'Wg': jax.random.normal(k[1], (E, D, I), jnp.float32) * s_d, 'Wu': jax.random.normal(k[2], (E, D, I), jnp.float32) * s_d, 'Wd': jax.random.normal(k[3], (E, I, D), jnp.float32) * s_i, 'Wr': jax.random.normal(k[4], (D, E), jnp.float32) * s_d, 'temperature': jnp.ones((1,), jnp.float32)}
    _L1_ffn_in = _L1_ffn_setup()
    _d = {'L0_attn_x': _L0_attn_in['x'], 'L0_attn_gamma1': _L0_attn_in['gamma1'], 'L0_attn_beta1': _L0_attn_in['beta1'], 'L0_attn_wq': _L0_attn_in['wq'], 'L0_attn_wk': _L0_attn_in['wk'], 'L0_attn_wv': _L0_attn_in['wv'], 'L0_attn_wo': _L0_attn_in['wo'], 'L0_attn_w1': _L0_attn_in['w1'], 'L0_attn_b1': _L0_attn_in['b1'], 'L0_attn_w2': _L0_attn_in['w2'], 'L0_attn_b2': _L0_attn_in['b2'], 'L0_ffn_Win': _L0_ffn_in['Win'], 'L0_ffn_bin_': _L0_ffn_in['bin_'], 'L0_ffn_W1': _L0_ffn_in['W1'], 'L0_ffn_b1': _L0_ffn_in['b1'], 'L0_ffn_W2': _L0_ffn_in['W2'], 'L0_ffn_b2': _L0_ffn_in['b2'], 'L0_ffn_Wout': _L0_ffn_in['Wout'], 'L0_ffn_bout': _L0_ffn_in['bout'], 'L1_attn_Wq': _L1_attn_in['Wq'], 'L1_attn_bq': _L1_attn_in['bq'], 'L1_attn_Wl': _L1_attn_in['Wl'], 'L1_attn_bl': _L1_attn_in['bl'], 'L1_attn_Wk': _L1_attn_in['Wk'], 'L1_attn_bk': _L1_attn_in['bk'], 'L1_attn_Wv': _L1_attn_in['Wv'], 'L1_attn_bv': _L1_attn_in['bv'], 'L1_attn_Wo': _L1_attn_in['Wo'], 'L1_attn_bo': _L1_attn_in['bo'], 'L1_ffn_Wg': _L1_ffn_in['Wg'], 'L1_ffn_Wu': _L1_ffn_in['Wu'], 'L1_ffn_Wd': _L1_ffn_in['Wd'], 'L1_ffn_Wr': _L1_ffn_in['Wr'], 'L1_ffn_temperature': _L1_ffn_in['temperature']}
    _x0 = _d['L0_attn_x']
    _d['L0_attn_x'] = jax.random.normal(jax.random.fold_in(jax.random.key(seed), 1), (8, 1024, 256), dtype=_x0.dtype)
    del _x0
    return _d

def reference(L0_attn_x, L0_attn_gamma1, L0_attn_beta1, L0_attn_wq, L0_attn_wk, L0_attn_wv, L0_attn_wo, L0_attn_w1, L0_attn_b1, L0_attn_w2, L0_attn_b2, L0_ffn_Win, L0_ffn_bin_, L0_ffn_W1, L0_ffn_b1, L0_ffn_W2, L0_ffn_b2, L0_ffn_Wout, L0_ffn_bout, L1_attn_Wq, L1_attn_bq, L1_attn_Wl, L1_attn_bl, L1_attn_Wk, L1_attn_bk, L1_attn_Wv, L1_attn_bv, L1_attn_Wo, L1_attn_bo, L1_ffn_Wg, L1_ffn_Wu, L1_ffn_Wd, L1_ffn_Wr, L1_ffn_temperature):

    def _L0_attn_ref(x, gamma1, beta1, wq, wk, wv, wo, w1, b1, w2, b2):
        import jax, jax.numpy as jnp
        import numpy as np
        EPS_LN = 1e-06
        STAB = 0.001

        def layer_norm(x, gamma, beta):
            mu = jnp.mean(x, axis=-1, keepdims=True)
            var = jnp.mean(jnp.square(x - mu), axis=-1, keepdims=True)
            return (x - mu) * jax.lax.rsqrt(var + EPS_LN) * gamma + beta
        ln1 = layer_norm(x, gamma1, beta1)
        q = jnp.einsum('ble,ehd->blhd', ln1, wq)
        k = jnp.einsum('ble,ehd->blhd', ln1, wk)
        v = jnp.einsum('ble,ehd->blhd', ln1, wv)
        qp = jax.nn.relu(q) + STAB
        kp = jax.nn.relu(k) + STAB
        kvs = jnp.einsum('blhm,blhd->bhmd', kp, v)
        num = jnp.einsum('blhm,bhmd->blhd', qp, kvs)
        ksum = jnp.sum(kp, axis=1)
        den = jnp.einsum('blhm,bhm->blh', qp, ksum)
        att = num / den[..., None]
        attn_out = jnp.einsum('blhd,hde->ble', att, wo)
        add1 = attn_out + x
        ln2 = layer_norm(add1, gamma1, beta1)
        h = jax.nn.gelu(jnp.einsum('ble,ef->blf', ln2, w1) + b1, approximate=False)
        out2 = jax.nn.gelu(jnp.einsum('blf,fe->ble', h, w2) + b2, approximate=False)
        return out2 + add1

    def _L0_ffn_ref(x, Win, bin_, W1, b1, W2, b2, Wout, bout):
        import jax, jax.numpy as jnp
        import numpy as np
        D_MODEL = 256
        M = 64
        INNER = 16
        s = jnp.einsum('btd,dm->btm', x, Win) + bin_
        h = jax.nn.relu(s[..., None] * W1 + b1)
        g = jnp.einsum('btmh,mh->btm', h, W2) + b2
        out = jnp.einsum('btm,md->btd', g, Wout) + bout
        return out

    def _L1_attn_ref(x, Wq, bq, Wl, bl, Wk, bk, Wv, bv, Wo, bo):
        import jax, jax.numpy as jnp
        import numpy as np
        DIM = 256
        HEADS = 16
        DIM_HEAD = DIM // HEADS
        LATENT = DIM // 4
        SCALE = DIM_HEAD ** (-0.5)
        B, S, D = x.shape
        H, Dh = (HEADS, DIM_HEAD)
        q = (x @ Wq + bq).reshape(B, S, H, Dh)
        latent = x @ Wl + bl
        k = (latent @ Wk + bk).reshape(B, S, H, Dh)
        v = (latent @ Wv + bv).reshape(B, S, H, Dh)
        scores = jnp.einsum('bihd,bjhd->bhij', q, k) * SCALE
        attn = jax.nn.softmax(scores, axis=-1)
        out = jnp.einsum('bhij,bjhd->bihd', attn, v).reshape(B, S, D)
        out = out @ Wo + bo
        return out

    def _L1_ffn_ref(x, Wg, Wu, Wd, Wr, temperature):
        import jax, jax.numpy as jnp
        import numpy as np
        import math
        GOLDEN_CENTER = 1.0 / math.e
        GOLDEN_LOWER = 0.5 - math.log(4.0 / 3.0)
        GOLDEN_UPPER = 0.5
        B, T, D = (4, 512, 256)
        E = 8
        I = 1024 // (E // 2)

        def _routing_weights(x, Wr, temperature):
            inh = jax.nn.sigmoid(x @ Wr / temperature)
            in_zone = (inh >= GOLDEN_LOWER) & (inh <= GOLDEN_UPPER)
            dist = jnp.abs(inh - GOLDEN_CENTER)
            w = jnp.exp(-dist / 0.1) * in_zone.astype(x.dtype)
            wsum = w.sum(axis=-1, keepdims=True)
            no_expert = wsum < 1e-08
            fb = jnp.exp(-dist / 0.3)
            _, top2 = jax.lax.top_k(fb, 2)
            fb_mask = jax.nn.one_hot(top2, E, dtype=x.dtype).sum(axis=-2)
            fb_w = fb * fb_mask
            fb_w = fb_w / jnp.clip(fb_w.sum(axis=-1, keepdims=True), 1e-08)
            w = jnp.where(no_expert, fb_w, w)
            wsum = w.sum(axis=-1, keepdims=True)
            return w / jnp.clip(wsum, 1e-08)
        weights = _routing_weights(x, Wr, temperature)
        gate = jnp.einsum('btd,edi->beti', x, Wg)
        up = jnp.einsum('btd,edi->beti', x, Wu)
        h = jax.nn.silu(gate) * up
        e_out = jnp.einsum('beti,eid->betd', h, Wd)
        out = jnp.einsum('bte,betd->btd', weights, e_out)
        return out
    x = L0_attn_x
    x = x + _L0_attn_ref(_layernorm(x, axis=-1), L0_attn_gamma1, L0_attn_beta1, L0_attn_wq, L0_attn_wk, L0_attn_wv, L0_attn_wo, L0_attn_w1, L0_attn_b1, L0_attn_w2, L0_attn_b2)
    x = x + _L0_ffn_ref(_layernorm(x, axis=-1), L0_ffn_Win, L0_ffn_bin_, L0_ffn_W1, L0_ffn_b1, L0_ffn_W2, L0_ffn_b2, L0_ffn_Wout, L0_ffn_bout)
    x = x + _L1_attn_ref(_layernorm(x, axis=-1), L1_attn_Wq, L1_attn_bq, L1_attn_Wl, L1_attn_bl, L1_attn_Wk, L1_attn_bk, L1_attn_Wv, L1_attn_bv, L1_attn_Wo, L1_attn_bo)
    x = x + _L1_ffn_ref(_layernorm(x, axis=-1), L1_ffn_Wg, L1_ffn_Wu, L1_ffn_Wd, L1_ffn_Wr, L1_ffn_temperature)
    return x

_drawn_inputs = setup_inputs


def setup_inputs(seed=0):
    import zlib

    import numpy as np

    out = dict(_drawn_inputs(seed))
    spreads = {'L0_attn_gamma1': (1.0, 0.2),
     'L0_attn_beta1': (0.0, 0.1),
     'L0_attn_b1': (0.0, 0.1),
     'L0_attn_b2': (0.0, 0.1),
     'L1_attn_bq': (0.0, 0.502),
     'L1_attn_bl': (0.0, 0.1),
     'L1_attn_bk': (0.0, 0.8),
     'L1_attn_bv': (0.0, 0.1),
     'L1_attn_bo': (0.0, 0.1)}
    factors = {'L0_ffn_bin_': 8.0}
    for name, (base, spread) in spreads.items():
        noise = np.random.default_rng([zlib.crc32(name.encode()), seed]).standard_normal(out[name].shape)
        drawn = base * np.exp(spread * noise) if base else spread * noise
        out[name] = jnp.asarray(drawn.astype(out[name].dtype))
    for name, factor in factors.items():
        out[name] = (out[name] * factor).astype(out[name].dtype)
    return out
```

```python
import math
from contextlib import ExitStack

import concourse.bass as bass
from concourse import mybir

ALU = mybir.AluOpType
ACT = mybir.ActivationFunctionType
F32 = mybir.dt.float32
F16 = mybir.dt.float16
AX_X = mybir.AxisListType.X

P = 128
BATCH, TOKENS, D = 8, 1024, 256
TT = TOKENS // P
NB = 512
IB = TOKENS // NB
KC = D // P
HEADS, DH = 16, 16
FF = 1024
FT = FF // P
M0, INNER = 64, 16
PAIRS = INNER // 2
LATENT = 64
EXPERTS, EI = 8, 256
ET = EI // P
GROUPS, GH = 4, 4
HALF = 64
SPLIT_ROWS = 3 * DH
STACK_ROWS = SPLIT_ROWS + 2
MAX_UNIT = 256.0
P_SLOTS = 8
BURST = GH
BURSTS = TT * IB
MAX_TILES = TT * GH * IB
AHEAD = MAX_TILES + 12
NORMS = 6
ROUTE_STEPS = 28
SCALE = DH ** -0.5
ZONE_CENTER = 1.0 / math.e
ZONE_LOWER = 0.5 - math.log(4.0 / 3.0)
ZONE_UPPER = 0.5


class Signal:

    def __init__(self, sem, per_batch, at_start=0):
        self.sem, self.per_batch, self.at_start = sem, per_batch, at_start

    def at(self, b, n):
        return b * self.per_batch + self.at_start + n


def build(nc, a, out):
    nc.disable_value_cache = True
    ctx = ExitStack()
    with ctx:
        def sb(name, shape, dt=F32):
            return ctx.enter_context(nc.sbuf_tensor(name, shape, dt))

        def signal(name, per_batch=1, at_start=0):
            return Signal(ctx.enter_context(nc.semaphore(name)), per_batch, at_start)

        def split_weight(name, shape):
            return sb(name + "_hi", shape, F16), sb(name + "_lo", shape, F16)

        wq0 = split_weight("wq0", [P, KC, D])
        wkv0 = split_weight("wkv0", [P, KC, 2 * D])
        w1 = split_weight("w1", [P, KC, FF])
        win = split_weight("win", [P, KC, 2 * M0])
        wl = split_weight("wl", [P, KC, LATENT])
        wq1 = split_weight("wq1", [P, KC, D])
        wk1 = split_weight("wk1", [LATENT, D])
        wv1 = split_weight("wv1", [LATENT, D])
        wr = split_weight("wr", [P, KC, EXPERTS])
        wg = split_weight("wg", [P, EXPERTS, KC, EI])
        wu = split_weight("wu", [P, EXPERTS, KC, EI])
        wo0 = sb("wo0", [P, KC, D])
        w2 = sb("w2", [P, FT, D])
        wout = sb("wout", [P, D])
        wo1 = sb("wo1", [P, GROUPS, D])
        wd = sb("wd", [P, EXPERTS, ET, D])
        gamma = sb("gamma", [P, KC])
        beta = sb("beta", [P, KC])
        b1 = sb("b1", [P, FT])
        bin2 = sb("bin2", [P, 1])
        w1p = sb("w1p", [P, PAIRS])
        b1p = sb("b1p", [P, PAIRS])
        w2p = sb("w2p", [P, PAIRS])
        b2p = sb("b2p", [P, 1])
        bq = sb("bq", [P, KC])
        bk = sb("bk", [P, KC])
        bl = sb("bl", [LATENT, 1])
        b2_all = sb("b2_all", [P, D])
        bout_all = sb("bout_all", [P, D])
        bv_all = sb("bv_all", [P, D])
        temp_all = sb("temp_all", [P, 1])
        rtemp = sb("rtemp", [P, 1])
        ident = sb("ident", [P, P])
        ident16 = sb("ident16", [P, P], F16)
        head_mask = sb("head_mask", [P, 2, P])
        ones_tok = sb("ones_tok", [P, P])
        before = sb("before", [P, EXPERTS, EXPERTS])
        eps = sb("eps", [P, 2, TT // 2])
        neg_half = sb("neg_half", [P, TT // 2])
        x_tok = sb("x_tok", [P, TT, D])
        r0 = sb("r0", [P, 2 * TT * D])
        r1 = sb("r1", [P, 4096])
        r2 = sb("r2", [P, 4096])
        r3 = sb("r3", [P, 4096])
        xT = (sb("xT_hi", [P, KC, TOKENS], F16), sb("xT_lo", [P, KC, TOKENS], F16))
        qs = sb("q_stack", [P, 2, GH, TOKENS], F16)
        ks = sb("k_stack", [P, 2, GH, TOKENS], F16)
        bn = sb("bn", [P, TT, 6])
        mv = sb("mv", [P, TT, 2])
        var_eps = sb("var_eps", [P, TT])
        rstd = sb("rstd", [P, TT])
        row_max = sb("row_max", [P, 2, TT, GH, IB])
        head_max = sb("head_max", [P, TT, GH])
        m16 = sb("m16", [P, TT, GH, 2], F16)
        mT = sb("mT", [2 * GH, TOKENS], F16)
        rt = sb("route", [P, 12, TT, EXPERTS])
        rt1 = sb("route_sums", [P, 6, TT])

        def view(region, start, size, pattern, **kw):
            return region[:, start:start + size].rearrange(pattern, **kw)

        y_tok = view(r0, 0, TT * D, "p (t d) -> p t d", d=D)
        n_tok = view(r0, TT * D, TT * D, "p (t d) -> p t d", d=D)
        probs = view(r0, 0, P_SLOTS * NB, "p (s n) -> p s n", n=NB)
        kv_tok = view(r1, 0, TT * 2 * D, "p (t n) -> p t n", n=2 * D)
        v_aug = view(r1, 0, TT * HEADS * 32, "p (t h c) -> p t h c", h=HEADS, c=32)
        h_ff = view(r2, 0, FT * NB, "p (f n) -> p f n", n=NB)
        attT0 = view(r2, 0, KC * TOKENS, "p (c n) -> p c n", c=KC)
        den0 = view(r2, 2048, 2 * NB, "p (s n) -> p s n", n=NB)
        gtmp = view(r2, 3072, 2 * NB, "p (s n) -> p s n", n=NB)
        s_dup = r2[:, 0:TOKENS]
        relu_s = view(r2, 1024, 2 * TOKENS, "p (s n) -> p s n", s=2)
        g_acc = r2[:, 3072:4096]
        qkT = [r2[:, 1024 * k:1024 * (k + 1)].bitcast(F16).rearrange("p (c n) -> p c n", c=KC)
               for k in range(4)]
        qT_hi, qT_lo, kT_hi, kT_lo = qkT
        den1 = view(r2, 0, 2 * TOKENS, "p (s n) -> p s n", s=2)
        h_moe = view(r2, 0, 2 * ET * TOKENS, "p (s m n) -> p s m n", s=2, m=ET)
        qpT = view(r3, 0, KC * TOKENS, "p (c n) -> p c n", c=KC)
        t1 = view(r3, 0, TT * D, "p (t d) -> p t d", d=D)
        add1 = view(r3, 2048, TT * D, "p (t d) -> p t d", d=D)
        latT = [r3[0:LATENT, 512 * k:512 * (k + 1)].bitcast(F16) for k in range(2)]
        oT = view(r3, 0, GROUPS * TOKENS, "p (g n) -> p g n", g=GROUPS)
        moe_acc = view(r3, 0, TT * D, "p (t d) -> p t d", d=D)
        silu = view(r3, 2048, 2 * NB, "p (s n) -> p s n", n=NB)
        pairs = [view(r3, 3072 + 512 * k, 512, "p (t e f) -> p t e f", e=EXPERTS, f=EXPERTS)
                 for k in range(2)]
        wait_cell = sb("wait_cell", [P, 3])
        kvsB = view(r3, 2048, KC * 2 * P, "p (c a n) -> p c a n", c=KC, a=2)

        bank = [ctx.enter_context(nc.psum_tensor(f"bank{k}", [P, NB], F32)) for k in range(8)]

        weights_loaded = signal("weights_loaded")
        hi_split = signal("hi_split")
        lo_split = signal("lo_split")
        setup_step = signal("setup_step")
        consts_made = signal("consts_made")
        x_loaded = signal("x_loaded", 32)
        bn_done = signal("bn_done", NORMS * TT)
        stats_done = signal("stats_done", NORMS * TT)
        eps_added = signal("eps_added", NORMS * 2)
        rstd_done = signal("rstd_done", NORMS * 2)
        norm_done = signal("norm_done", NORMS * TT)
        xT_full = signal("xT_full", 5 * 4)
        xT_hi_done = signal("xT_hi_done", 5 * 4)
        xT_affine = signal("xT_affine", 2 * 4)
        xT_lo_done = signal("xT_lo_done", 5 * 4)
        kv_full = signal("kv_full", TT)
        kv_done = signal("kv_done", TT)
        q_full = signal("q_full", 4)
        q_done = signal("q_done", 4)
        kvs_full = signal("kvs_full", KC)
        kvs_done = signal("kvs_done", KC)
        numden_full = signal("numden_full", 4)
        rden_done = signal("rden_done", 4)
        att0_done = signal("att0_done", 4)
        wo_full = signal("wo_full", 4)
        add1_done = signal("add1_done", 4)
        h_full = signal("h_full", 2 * FT)
        h_done = signal("h_done", 2 * FT)
        w2_full = signal("w2_full", 4)
        t1_done = signal("t1_done", 4)
        gelu_done = signal("gelu_done", 4)
        x_add1_done = signal("x_add1_done", 1)
        x1_done = signal("x1_done", 4)
        s_full = signal("s_full", 2)
        s_done = signal("s_done", 2)
        relu_done = signal("relu_done", PAIRS)
        g_done = signal("g_done", PAIRS)
        x_bout_done = signal("x_bout_done", 1)
        fo_full = signal("fo_full", 4)
        x2_done = signal("x2_done", 4)
        lat_full = signal("lat_full", 2)
        lat_hi_done = signal("lat_hi_done", 2)
        lat_lo_done = signal("lat_lo_done", 2)
        k1_full = signal("k1_full", 4)
        k1_hi_done = signal("k1_hi_done", 4)
        k1_lo_done = signal("k1_lo_done", 4)
        q1_full = signal("q1_full", 4)
        q1_hi_done = signal("q1_hi_done", 4)
        q1_lo_done = signal("q1_lo_done", 4)
        v1_full = signal("v1_full", 4)
        v1_done = signal("v1_done", 4)
        v_ones_done = signal("v_ones_done", 1)
        stack_loaded = [signal(f"stack_loaded{s}", 16 * 6 * GH) for s in range(2)]
        rows_full = signal("rows_full", GROUPS * MAX_TILES)
        rows_max_done = signal("rows_max_done", GROUPS * MAX_TILES)
        max_step = signal("max_step", 2 * GROUPS)
        m16_done = signal("m16_done", GROUPS)
        mT_full = signal("mT_full", GROUPS)
        mT_done = signal("mT_done", GROUPS)
        m_loaded = signal("m_loaded", 16 * GH * GROUPS)
        cols_full = signal("cols_full", GROUPS * BURSTS * BURST)
        exp_done = signal("exp_done", GROUPS * BURSTS * BURST)
        av_done = signal("av_done", GROUPS * BURSTS)
        o_done = signal("o_done", 2 * GROUPS)
        den_step = signal("den_step", 2 * GROUPS)
        att1_done = signal("att1_done", GROUPS)
        o1_full = signal("o1_full", 4)
        x3_done = signal("x3_done", 4)
        route_full = signal("route_full", 1)
        route_step = signal("route_step", ROUTE_STEPS)
        route_exp = signal("route_exp", 3)
        gate_full = signal("gate_full", EXPERTS * 4)
        up_full = signal("up_full", EXPERTS * 4)
        silu_done = signal("silu_done", EXPERTS * 4)
        hmoe_done = signal("hmoe_done", EXPERTS * 4)
        down_full = signal("down_full", EXPERTS * 4)
        moe_done = signal("moe_done", EXPERTS * TT, at_start=1)
        stored = signal("stored", 64, at_start=1)

        def stage(region, start, rows, shape):
            n = math.prod(shape)
            names = "abc"[:len(shape)]
            v = region[0:rows, start:start + n]
            if len(shape) == 1:
                return v
            return v.rearrange(f"p ({' '.join(names)}) -> p {' '.join(names)}", **dict(zip(names, shape)))

        dr = {k: v for k, v in a.items()}
        chunk = "(c p) n -> p c n"
        st_kv = stage(r3, 2048, P, [KC, 2 * D])
        st_win = stage(r0, 0, P, [KC, 2 * M0])
        split_plan = [
            ([(stage(r1, 0, P, [EXPERTS, KC, EI]), dr["L1_ffn_Wg"].rearrange("e (c p) n -> p e c n", p=P))],
             stage(r1, 0, P, [EXPERTS, KC, EI]), wg),
            ([(stage(r2, 0, P, [EXPERTS, KC, EI]), dr["L1_ffn_Wu"].rearrange("e (c p) n -> p e c n", p=P))],
             stage(r2, 0, P, [EXPERTS, KC, EI]), wu),
            ([(stage(r3, 0, P, [KC, FF]), dr["L0_attn_w1"].rearrange(chunk, p=P))],
             stage(r3, 0, P, [KC, FF]), w1),
            ([(st_kv[:, :, 0:D], dr["L0_attn_wk"].rearrange("(c p) h d -> p c (h d)", p=P)),
              (st_kv[:, :, D:2 * D], dr["L0_attn_wv"].rearrange("(c p) h d -> p c (h d)", p=P))],
             st_kv, wkv0),
            ([(stage(r3, 3072, P, [KC, D]), dr["L0_attn_wq"].rearrange("(c p) h d -> p c (h d)", p=P))],
             stage(r3, 3072, P, [KC, D]), wq0),
            ([(stage(r3, 3584, P, [KC, D]), dr["L1_attn_Wq"].rearrange(chunk, p=P))],
             stage(r3, 3584, P, [KC, D]), wq1),
            ([(st_win[:, :, s * M0:(s + 1) * M0], dr["L0_ffn_Win"].rearrange(chunk, p=P)) for s in range(2)],
             st_win, win),
            ([(stage(r0, 256, P, [KC, LATENT]), dr["L1_attn_Wl"].rearrange(chunk, p=P))],
             stage(r0, 256, P, [KC, LATENT]), wl),
            ([(stage(r0, 512, LATENT, [D]), dr["L1_attn_Wk"])], stage(r0, 512, LATENT, [D]), wk1),
            ([(stage(r0, 768, LATENT, [D]), dr["L1_attn_Wv"])], stage(r0, 768, LATENT, [D]), wv1),
            ([(stage(r0, 1024, P, [KC, EXPERTS]), dr["L1_ffn_Wr"].rearrange(chunk, p=P))],
             stage(r0, 1024, P, [KC, EXPERTS]), wr),
        ]

        def column(vec, rows):
            return vec.rearrange("(c p) -> p c", p=rows)

        def halves(t, m):
            return m.rearrange("m (k two) -> two m k", two=2)

        def row_for_all(vec):
            return vec.partition_broadcast(P)

        plain_loads = [
            (wo0[:], dr["L0_attn_wo"].rearrange("(c h) d n -> (h d) c n", c=KC)),
            (w2[:], dr["L0_attn_w2"].rearrange(chunk, p=P)),
            (wout[0:M0, :], dr["L0_ffn_Wout"]), (wout[M0:P, :], dr["L0_ffn_Wout"]),
            (wd[:, 0:4], dr["L1_ffn_Wd"][0:4].rearrange("e (m p) n -> p e m n", p=P)),
            (wd[:, 4:8], dr["L1_ffn_Wd"][4:8].rearrange("e (m p) n -> p e m n", p=P)),
            (gamma[:], column(dr["L0_attn_gamma1"], P)), (beta[:], column(dr["L0_attn_beta1"], P)),
            (b1[:], column(dr["L0_attn_b1"], P)), (bq[:], column(dr["L1_attn_bq"], P)),
            (bk[:], column(dr["L1_attn_bk"], P)), (bl[:], column(dr["L1_attn_bl"], LATENT)),
            (b2_all[:], row_for_all(dr["L0_attn_b2"])), (bout_all[:], row_for_all(dr["L0_ffn_bout"])),
            (bv_all[:], row_for_all(dr["L1_attn_bv"])), (temp_all[:], row_for_all(dr["L1_ffn_temperature"])),
        ]
        for s in range(2):
            rows = slice(s * M0, (s + 1) * M0)
            plain_loads += [
                (bin2[rows, :], column(dr["L0_ffn_bin_"], M0)),
                (w1p[rows, :], halves(w1p, dr["L0_ffn_W1"])[s]), (b1p[rows, :], halves(b1p, dr["L0_ffn_b1"])[s]),
                (w2p[rows, :], halves(w2p, dr["L0_ffn_W2"])[s]),
            ]
        zeroed_loads = [(wo1[32 * c:32 * c + DH, :, :],
                         dr["L1_attn_Wo"].rearrange("(g c r) n -> c r g n", g=GROUPS, c=GH)[c])
                        for c in range(GH)]
        zeroed_loads.append((wo1[DH:DH + 1, 0, :], dr["L1_attn_bo"].rearrange("(a n) -> a n", a=1)))
        zeroed_loads.append((b2p[0:M0, :], column(dr["L0_ffn_b2"], M0)))
        N_LOADS = sum(len(x[0]) for x in split_plan) + len(plain_loads) + len(zeroed_loads)
        N_SPLIT = len(split_plan)

        x_view = dr["L0_attn_x"].rearrange("b (t p) d -> b p t d", p=P)
        out_view = out.rearrange("b (t p) d -> b p t d", p=P)

        block = ctx.enter_context(nc.Block())

        @block.sync
        def _(sp):
            for loads, _, _ in split_plan:
                for dst, src in loads:
                    sp.dma_start(dst, src).then_inc(weights_loaded.sem, 16)
            with nc.allow_non_contiguous_dma(reason="a few KB of per-partition vectors, once"):
                for dst, src in plain_loads:
                    sp.dma_start(dst, src).then_inc(weights_loaded.sem, 16)
            sp.wait_ge(setup_step.sem, 2)
            with nc.allow_non_contiguous_dma(reason="one of them is a per-partition vector"):
                for dst, src in zeroed_loads:
                    sp.dma_start(dst, src).then_inc(weights_loaded.sem, 16)

            with sp.Fori(0, BATCH) as b:
                sp.wait_ge(q1_lo_done.sem, q1_lo_done.at(b, 4))
                sp.wait_ge(k1_lo_done.sem, k1_lo_done.at(b, 4))
                for s in range(2):
                    for hh in range(GH):
                        rows = slice(HALF * s + DH * hh, HALF * s + DH * (hh + 1))
                        for part, (q_src, k_src) in enumerate(((qT_hi, kT_hi), (qT_lo, kT_hi), (qT_hi, kT_lo))):
                            at = slice(HALF * s + DH * part, HALF * s + DH * (part + 1))
                            sp.dma_start(qs[at, :, hh, :], q_src[rows, :, :]).then_inc(stack_loaded[s].sem, 16)
                            sp.dma_start(ks[at, :, hh, :], k_src[rows, :, :]).then_inc(stack_loaded[s].sem, 16)
                for g in range(GROUPS):
                    sp.wait_ge(mT_done.sem, mT_done.at(b, g + 1))
                    for hh in range(GH):
                        at = HALF * (g % 2) + SPLIT_ROWS
                        sp.dma_start(qs[at:at + 2, g // 2, hh, :], mT[2 * hh:2 * hh + 2, :])\
                          .then_inc(m_loaded.sem, 16)
                for tp in range(4):
                    sp.wait_ge(moe_done.sem, moe_done.at(b, (EXPERTS - 1) * TT + 2 * tp + 2))
                    sp.dma_start(out_view[b, :, 2 * tp:2 * tp + 2, :], moe_acc[:, 2 * tp:2 * tp + 2, :])\
                      .then_inc(stored.sem, 16)
            sp.wait_ge(stored.sem, BATCH * stored.per_batch + stored.at_start)

        @block.gpsimd
        def _(pool):
            pool.memset(wo1[:], 0.0).then_inc(setup_step.sem, 1)
            pool.memset(b2p[:], 0.0).then_inc(setup_step.sem, 1)
            pool.memset(ident[:], 0.0).then_inc(setup_step.sem, 1)
            pool.memset(head_mask[:], 1.0).then_inc(setup_step.sem, 1)
            pool.memset(before[:], 0.0).then_inc(setup_step.sem, 1)
            pool.memset(ks[:], MAX_UNIT).then_inc(setup_step.sem, 1)
            pool.memset(qs[:], 0.0).then_inc(setup_step.sem, 1)
            pool.memset(ones_tok[:], 1.0).then_inc(setup_step.sem, 1)
            pool.memset(eps[:, 0, :], 1e-5).then_inc(setup_step.sem, 1)
            pool.memset(eps[:, 1, :], 1e-6).then_inc(setup_step.sem, 1)
            pool.memset(neg_half[:], -0.5).then_inc(setup_step.sem, 1)
            pool.wait_ge(setup_step.sem, 11)
            pool.affine_select(out=ident[:], in_=ident[:], compare_op=ALU.not_equal, fill=1.0, base=0,
                               pattern=[[-1, P]], channel_multiplier=1).then_inc(setup_step.sem, 1)
            pool.affine_select(out=before[:], in_=before[:], compare_op=ALU.is_ge, fill=1.0, base=0,
                               pattern=[[-1, EXPERTS], [1, EXPERTS]], channel_multiplier=0)\
                .then_inc(setup_step.sem, 1)
            mask = head_mask[:].rearrange("p a (h d) -> p a h d", d=DH)
            pool.affine_select(out=mask, in_=mask, compare_op=ALU.is_ge, fill=0.0, base=0,
                               pattern=[[0, 2], [-DH, P // DH], [0, DH]], channel_multiplier=1)\
                .then_inc(setup_step.sem, 1)
            pool.wait_ge(setup_step.sem, 14)
            pool.affine_select(out=mask, in_=mask, compare_op=ALU.is_ge, fill=0.0, base=DH - 1,
                               pattern=[[0, 2], [DH, P // DH], [0, DH]], channel_multiplier=-1)\
                .then_inc(setup_step.sem, 1)
            pool.tensor_copy(ident16[:], ident[:]).then_inc(setup_step.sem, 1)
            pool.wait_ge(setup_step.sem, 16)
            pool.wait_ge(weights_loaded.sem, 16 * N_LOADS)
            pool.memset(eps[:, 0, :], 1e-5).then_inc(consts_made.sem, 1)

            def rstds(b, norm, which_eps):
                for s in range(2):
                    half = slice(s * TT // 2, (s + 1) * TT // 2)
                    pool.wait_ge(stats_done.sem, stats_done.at(b, norm * TT + (s + 1) * TT // 2))
                    pool.tensor_tensor(var_eps[:, half], mv[:, half, 1], eps[:, which_eps, :], ALU.add)\
                        .then_inc(eps_added.sem, 1)
                    pool.wait_ge(eps_added.sem, eps_added.at(b, norm * 2 + s + 1))
                    pool.tensor_tensor(rstd[:, half], var_eps[:, half], neg_half[:], ALU.pow)\
                        .then_inc(rstd_done.sem, 1)

            with pool.Fori(0, BATCH) as b:
                pool.wait_ge(moe_done.sem, moe_done.at(b, 0))
                for s in range(2):
                    half = slice(s * TT // 2, (s + 1) * TT // 2)
                    pool.dma_start(x_tok[:, half, :], x_view[b, :, half, :]).then_inc(x_loaded.sem, 16)
                rstds(b, 0, 0)
                rstds(b, 1, 1)
                rstds(b, 2, 1)
                pool.wait_ge(add1_done.sem, add1_done.at(b, 4))
                pool.tensor_tensor(x_tok[:], x_tok[:], add1, ALU.add).then_inc(x_add1_done.sem, 1)
                pool.memset(v_aug[:, :, :, DH:32], 1.0).then_inc(v_ones_done.sem, 1)
                rstds(b, 3, 0)
                pool.wait_ge(norm_done.sem, norm_done.at(b, 4 * TT))
                pool.tensor_tensor(x_tok[:], x_tok[:], bout_all[:].unsqueeze(1).to_broadcast([P, TT, D]),
                                   ALU.add).then_inc(x_bout_done.sem, 1)
                rstds(b, 4, 0)
                rstds(b, 5, 0)

        @block.scalar
        def _(act):
            act.wait_ge(weights_loaded.sem, 16 * N_LOADS)
            for _, staged, (hi, _) in split_plan:
                act.activation(hi[:], staged, ACT.Copy).then_inc(hi_split.sem, 1)

            def xT_his(b, n, affine):
                for k in range(4):
                    i, c = divmod(k, KC)
                    dst = xT[0][:, c, i * NB:(i + 1) * NB]
                    act.wait_ge(xT_full.sem, xT_full.at(b, 4 * n + k + 1))
                    if affine:
                        act.activation(dst, bank[XT_BANK[n] + k][:], ACT.Identity, bias=beta[:, c:c + 1],
                                       scale=gamma[:, c:c + 1]).then_inc(xT_hi_done.sem, 1)
                    else:
                        act.activation(dst, bank[XT_BANK[n] + k][:], ACT.Copy).then_inc(xT_hi_done.sem, 1)

            with act.Fori(0, BATCH) as b:
                xT_his(b, 0, True)
                xT_his(b, 1, True)
                for i in range(IB):
                    for f in range(FT):
                        n = i * FT + f
                        act.wait_ge(h_full.sem, h_full.at(b, n + 1))
                        if i and f == 0:
                            act.wait_ge(w2_full.sem, w2_full.at(b, 2))
                        act.activation(h_ff[:, f, :], bank[4 + f % 4][:], ACT.Gelu, bias=b1[:, f:f + 1])\
                            .then_inc(h_done.sem, 1)
                    for tp in range(2):
                        n = 2 * i + tp
                        act.wait_ge(t1_done.sem, t1_done.at(b, n + 1))
                        act.activation(t1[:, 2 * n:2 * n + 2, :], t1[:, 2 * n:2 * n + 2, :], ACT.Gelu)\
                            .then_inc(gelu_done.sem, 1)
                xT_his(b, 2, False)
                for i in range(IB):
                    act.wait_ge(s_full.sem, s_full.at(b, i + 1))
                    act.activation(s_dup[:, i * NB:(i + 1) * NB], bank[4 + i][:], ACT.Identity, bias=bin2[:])\
                        .then_inc(s_done.sem, 1)
                act.wait_ge(s_done.sem, s_done.at(b, 2))
                for k in range(PAIRS):
                    if k >= 2:
                        act.wait_ge(g_done.sem, g_done.at(b, k - 1))
                    act.activation(relu_s[:, k % 2, :], s_dup, ACT.Relu, bias=b1p[:, k:k + 1],
                                   scale=w1p[:, k:k + 1]).then_inc(relu_done.sem, 1)
                xT_his(b, 3, False)
                for i in range(IB):
                    act.wait_ge(lat_full.sem, lat_full.at(b, i + 1))
                    act.activation(latT[0][:, i * NB:(i + 1) * NB], bank[i][0:LATENT, :], ACT.Identity,
                                   bias=bl[:]).then_inc(lat_hi_done.sem, 1)
                for k in range(4):
                    m, i = divmod(k, IB)
                    act.wait_ge(k1_full.sem, k1_full.at(b, k + 1))
                    act.activation(kT_hi[:, m, i * NB:(i + 1) * NB], bank[4 + k][:], ACT.Identity,
                                   bias=bk[:, m:m + 1]).then_inc(k1_hi_done.sem, 1)
                for k in range(4):
                    m, i = divmod(k, IB)
                    act.wait_ge(q1_full.sem, q1_full.at(b, k + 1))
                    act.activation(qT_hi[:, m, i * NB:(i + 1) * NB], bank[k][:], ACT.Identity,
                                   bias=bq[:, m:m + 1]).then_inc(q1_hi_done.sem, 1)

                def maxima_to_rows(g):
                    act.wait_ge(mT_full.sem, mT_full.at(b, g + 1))
                    if g:
                        act.wait_ge(m_loaded.sem, m_loaded.at(b, 16 * GH * g))
                    act.activation(mT[:], bank[5][:].bitcast(F16)[0:2 * GH, :], ACT.Copy)\
                        .then_inc(mT_done.sem, 1)

                def out_of_group(g):
                    for i in range(IB):
                        act.wait_ge(av_done.sem, av_done.at(b, BURSTS * (g + 1)))
                        act.activation(oT[:, g, i * NB:(i + 1) * NB], bank[6 + i][:], ACT.Copy)\
                            .then_inc(o_done.sem, 1)

                maxima_to_rows(0)
                for n in range(GROUPS * BURSTS):
                    g, r = divmod(n, BURSTS)
                    if r == BURSTS - 2 and g + 1 < GROUPS:
                        maxima_to_rows(g + 1)
                    for hh in range(GH):
                        tile = n * BURST + hh
                        act.wait_ge(cols_full.sem, cols_full.at(b, tile + 1))
                        if n >= 2 and hh == 0:
                            act.wait_ge(av_done.sem, av_done.at(b, n - 1))
                        act.activation(probs[:, tile % P_SLOTS, :], bank[2 + tile % 3][:], ACT.Exp,
                                       scale=SCALE).then_inc(exp_done.sem, 1)
                    if r == 0 and g:
                        out_of_group(g - 1)
                out_of_group(GROUPS - 1)
                xT_his(b, 4, False)
                act.wait_ge(route_step.sem, route_step.at(b, ROUTE_Z))
                act.activation(rt[:, 1], rt[:, 0], ACT.Exp, scale=-1.0).then_inc(route_exp.sem, 1)
                act.wait_ge(route_step.sem, route_step.at(b, ROUTE_DIST))
                act.activation(rt[:, 6], rt[:, 5], ACT.Exp, scale=-1.0 / 0.1).then_inc(route_exp.sem, 1)
                act.activation(rt[:, 7], rt[:, 5], ACT.Exp, scale=-1.0 / 0.3).then_inc(route_exp.sem, 1)
                for j in range(EXPERTS * 4):
                    act.wait_ge(gate_full.sem, gate_full.at(b, j + 1))
                    if j >= 2:
                        act.wait_ge(hmoe_done.sem, hmoe_done.at(b, j - 1))
                    act.activation(silu[:, j % 2, :], bank[4 + 2 * (j % 2)][:], ACT.Silu)\
                        .then_inc(silu_done.sem, 1)

        @block.tensor
        def _(pe):
            pe.wait_ge(lo_split.sem, N_SPLIT)
            pe.wait_ge(consts_made.sem, 1)

            def split_product(out_ap, stationary, moving):
                chunks = stationary[1]
                terms = [(c, ps, pm) for c in range(chunks) for ps, pm in ((0, 0), (1, 0), (0, 1))]
                for k, (c, ps, pm) in enumerate(terms):
                    last = pe.matmul(out_ap, stationary[0](ps, c), moving(pm, c),
                                     start=(k == 0), stop=(k == len(terms) - 1))
                return last

            def transposes(b, norm, n):
                for k in range(4):
                    i, c = divmod(k, KC)
                    pe.wait_ge(norm_done.sem, norm_done.at(b, norm * TT + 4 * (i + 1)))
                    for t in range(4):
                        last = pe.transpose(bank[XT_BANK[n] + k][:, t * P:(t + 1) * P],
                                            n_tok[:, 4 * i + t, c * P:(c + 1) * P], ident[:])
                    last.then_inc(xT_full.sem, 1)

            def cols(w, lo, hi):
                return (lambda part, c: w[part][:, c, lo:hi], KC)

            def x_cols(lo, hi):
                return lambda part, c: xT[part][:, c, lo:hi]

            with pe.Fori(0, BATCH) as b:
                transposes(b, 1, 0)
                for t in range(TT):
                    pe.wait_ge(xT_lo_done.sem, xT_lo_done.at(b, 2 * (t // 4 + 1)))
                    if t >= 4:
                        pe.wait_ge(kv_done.sem, kv_done.at(b, t - 3))
                    split_product(bank[4 + t % 4][:],
                                  (lambda part, c: xT[part][:, c, t * P:(t + 1) * P], KC),
                                  lambda part, c: wkv0[part][:, c, :]).then_inc(kv_full.sem, 1)
                for k in range(4):
                    m, i = divmod(k, IB)
                    split_product(bank[k][:], cols(wq0, m * P, (m + 1) * P),
                                  x_cols(i * NB, (i + 1) * NB)).then_inc(q_full.sem, 1)
                pe.wait_ge(kv_done.sem, kv_done.at(b, TT))
                for m in range(KC):
                    for t in range(TT):
                        pe.matmul(bank[4 + m][:, 0:P], kv_tok[:, t, m * P:(m + 1) * P],
                                  kv_tok[:, t, D + m * P:D + (m + 1) * P], start=(t == 0), stop=(t == TT - 1))
                    for t in range(TT):
                        last = pe.matmul(bank[4 + m][:, P:2 * P], kv_tok[:, t, m * P:(m + 1) * P],
                                         ones_tok[:], start=(t == 0), stop=(t == TT - 1))
                    last.then_inc(kvs_full.sem, 1)
                for k in range(4):
                    m, i = divmod(k, IB)
                    pe.wait_ge(kvs_done.sem, kvs_done.at(b, m + 1))
                    pe.wait_ge(q_done.sem, q_done.at(b, 4 if k == 0 else k + 1))
                    if k >= 2:
                        pe.wait_ge(att0_done.sem, att0_done.at(b, k - 1))
                    for part in range(2):
                        last = pe.matmul(bank[2 * (k % 2) + part][:], kvsB[:, m, part, :],
                                         qpT[:, m, i * NB:(i + 1) * NB], start=True, stop=True)
                    last.then_inc(numden_full.sem, 1)
                pe.wait_ge(att0_done.sem, att0_done.at(b, 4))
                for tp in range(4):
                    for t in range(2):
                        for c in range(KC):
                            at = (2 * tp + t) * P
                            last = pe.matmul(bank[4 + tp][:, t * D:(t + 1) * D], attT0[:, c, at:at + P],
                                             wo0[:, c, :], start=(c == 0), stop=(c == KC - 1))
                    last.then_inc(wo_full.sem, 1)
                transposes(b, 2, 1)
                pe.wait_ge(add1_done.sem, add1_done.at(b, 4))
                for i in range(IB):
                    pe.wait_ge(xT_lo_done.sem, xT_lo_done.at(b, 8))
                    for f in range(FT):
                        n = i * FT + f
                        if n >= 4:
                            pe.wait_ge(h_done.sem, h_done.at(b, n - 3))
                        split_product(bank[4 + f % 4][:], cols(w1, f * P, (f + 1) * P),
                                      x_cols(i * NB, (i + 1) * NB)).then_inc(h_full.sem, 1)
                    pe.wait_ge(h_done.sem, h_done.at(b, (i + 1) * FT))
                    for tp in range(2):
                        for t in range(2):
                            for f in range(FT):
                                at = (2 * tp + t) * P
                                last = pe.matmul(bank[2 * i + tp][:, t * D:(t + 1) * D], h_ff[:, f, at:at + P],
                                                 w2[:, f, :], start=(f == 0), stop=(f == FT - 1))
                        last.then_inc(w2_full.sem, 1)
                pe.wait_ge(t1_done.sem, t1_done.at(b, 4))
                transposes(b, 3, 2)
                for i in range(IB):
                    pe.wait_ge(xT_lo_done.sem, xT_lo_done.at(b, 8 + 2 * (i + 1)))
                    split_product(bank[4 + i][:], cols(win, 0, 2 * M0),
                                  x_cols(i * NB, (i + 1) * NB)).then_inc(s_full.sem, 1)
                pe.wait_ge(g_done.sem, g_done.at(b, PAIRS))
                for tp in range(4):
                    for t in range(2):
                        at = (2 * tp + t) * P
                        last = pe.matmul(bank[tp][:, t * D:(t + 1) * D], g_acc[:, at:at + P], wout[:],
                                         start=True, stop=True)
                    last.then_inc(fo_full.sem, 1)
                transposes(b, 4, 3)
                pe.wait_ge(x2_done.sem, x2_done.at(b, 4))
                for i in range(IB):
                    pe.wait_ge(xT_lo_done.sem, xT_lo_done.at(b, 12 + 2 * (i + 1)))
                    split_product(bank[i][0:LATENT, :], (lambda part, c: wl[part][:, c, :], KC),
                                  x_cols(i * NB, (i + 1) * NB)).then_inc(lat_full.sem, 1)
                pe.wait_ge(lat_lo_done.sem, lat_lo_done.at(b, 2))
                for k in range(4):
                    m, i = divmod(k, IB)
                    split_product(bank[4 + k][:], (lambda part, c: wk1[part][:, m * P:(m + 1) * P], 1),
                                  lambda part, c: latT[part][:, i * NB:(i + 1) * NB]).then_inc(k1_full.sem, 1)
                for k in range(4):
                    m, i = divmod(k, IB)
                    split_product(bank[k][:], cols(wq1, m * P, (m + 1) * P),
                                  x_cols(i * NB, (i + 1) * NB)).then_inc(q1_full.sem, 1)
                for tp in range(4):
                    pe.wait_ge(k1_lo_done.sem, k1_lo_done.at(b, tp + 1))
                    for t in range(2):
                        at = (2 * tp + t) * P
                        last = split_product(bank[4 + tp][:, t * D:(t + 1) * D],
                                             (lambda part, c: latT[part][:, at:at + P], 1),
                                             lambda part, c: wv1[part][:])
                    last.then_inc(v1_full.sem, 1)
                pe.wait_ge(q1_lo_done.sem, q1_lo_done.at(b, 4))
                pe.wait_ge(v1_done.sem, v1_done.at(b, 4))
                pe.wait_ge(v_ones_done.sem, v_ones_done.at(b, 1))

                def row_tile(n):
                    g, r = divmod(n, MAX_TILES)
                    it, hh, jb = r // (GH * IB), (r // IB) % GH, r % IB
                    lo = HALF * (g % 2)
                    if r == 0 and g < 2:
                        pe.wait_ge(stack_loaded[g % 2].sem, stack_loaded[g % 2].at(b, 16 * 6 * GH))
                    if n >= 2:
                        pe.wait_ge(rows_max_done.sem, rows_max_done.at(b, n - 1))
                    pe.matmul(bank[n % 2][:], qs[lo:lo + SPLIT_ROWS, g // 2, hh, it * P:(it + 1) * P],
                              ks[lo:lo + SPLIT_ROWS, g // 2, hh, jb * NB:(jb + 1) * NB],
                              start=True, stop=True).then_inc(rows_full.sem, 1)

                def maxima(g):
                    pe.wait_ge(m16_done.sem, m16_done.at(b, g + 1))
                    if g:
                        pe.wait_ge(mT_done.sem, mT_done.at(b, g))
                    for it in range(TT):
                        last = pe.transpose(bank[5][:].bitcast(F16)[0:2 * GH, it * P:(it + 1) * P],
                                            m16[:, it].rearrange("p h s -> p (h s)"), ident16[:])
                    last.then_inc(mT_full.sem, 1)

                def column_tile(n, hh):
                    g, r = divmod(n, BURSTS)
                    jt, ib = divmod(r, IB)
                    lo = HALF * (g % 2)
                    tile = n * BURST + hh
                    if tile >= 3:
                        pe.wait_ge(exp_done.sem, exp_done.at(b, tile - 2))
                    pe.matmul(bank[2 + tile % 3][:], ks[lo:lo + STACK_ROWS, g // 2, hh, jt * P:(jt + 1) * P],
                              qs[lo:lo + STACK_ROWS, g // 2, hh, ib * NB:(ib + 1) * NB],
                              start=True, stop=True).then_inc(cols_full.sem, 1)

                def values(n):
                    g, r = divmod(n, BURSTS)
                    jt, ib = divmod(r, IB)
                    if r == 0 and g:
                        pe.wait_ge(o_done.sem, o_done.at(b, 2 * g))
                    pe.wait_ge(exp_done.sem, exp_done.at(b, (n + 1) * BURST))
                    for hh in range(GH):
                        last = pe.matmul(bank[6 + ib][32 * hh:32 * hh + 32, :], v_aug[:, jt, GH * g + hh, :],
                                         probs[:, (n * BURST + hh) % P_SLOTS, :], start=(jt == 0),
                                         stop=(jt == TT - 1))
                    last.then_inc(av_done.sem, 1)

                for n in range(AHEAD):
                    row_tile(n)
                    if n == MAX_TILES + 5:
                        maxima(0)
                for n in range(GROUPS * BURSTS):
                    g, r = divmod(n, BURSTS)
                    if r == 0:
                        pe.wait_ge(m_loaded.sem, m_loaded.at(b, 16 * GH * (g + 1)))
                    if r == BURSTS - 2 and g + 1 < GROUPS:
                        maxima(g + 1)
                    for hh in range(GH):
                        column_tile(n, hh)
                        if AHEAD + 4 * n + hh < GROUPS * MAX_TILES:
                            row_tile(AHEAD + 4 * n + hh)
                    if n:
                        values(n - 1)
                values(GROUPS * BURSTS - 1)
                pe.wait_ge(rows_max_done.sem, rows_max_done.at(b, GROUPS * MAX_TILES))
                pe.wait_ge(exp_done.sem, exp_done.at(b, GROUPS * BURSTS * BURST))
                pe.wait_ge(att1_done.sem, att1_done.at(b, GROUPS))
                for tp in range(4):
                    for t in range(2):
                        for g in range(GROUPS):
                            at = (2 * tp + t) * P
                            last = pe.matmul(bank[tp][:, t * D:(t + 1) * D], oT[:, g, at:at + P], wo1[:, g, :],
                                             start=(g == 0), stop=(g == GROUPS - 1))
                    last.then_inc(o1_full.sem, 1)
                transposes(b, 5, 4)
                pe.wait_ge(x3_done.sem, x3_done.at(b, 4))
                for t in range(TT):
                    pe.wait_ge(xT_lo_done.sem, xT_lo_done.at(b, 16 + 2 * (t // 4 + 1)))
                    last = split_product(bank[0][:, t * EXPERTS:(t + 1) * EXPERTS],
                                         (lambda part, c: xT[part][:, c, t * P:(t + 1) * P], KC),
                                         lambda part, c: wr[part][:, c, :])
                last.then_inc(route_full.sem, 1)

                def gate_up(e):
                    for k in range(4):
                        m, i = divmod(k, IB)
                        j = 4 * e + k
                        if j >= 2:
                            pe.wait_ge(hmoe_done.sem, hmoe_done.at(b, j - 1))
                        for w, at, sig in ((wg, 4, gate_full), (wu, 5, up_full)):
                            split_product(bank[at + 2 * (j % 2)][:],
                                          (lambda part, c: w[part][:, e, c, m * P:(m + 1) * P], KC),
                                          x_cols(i * NB, (i + 1) * NB)).then_inc(sig.sem, 1)

                def down(e):
                    pe.wait_ge(hmoe_done.sem, hmoe_done.at(b, 4 * e + 4))
                    for tp in range(4):
                        if e:
                            pe.wait_ge(moe_done.sem, moe_done.at(b, (e - 1) * TT + 2 * tp + 2))
                        elif tp == 0:
                            pe.wait_ge(route_step.sem, route_step.at(b, ROUTE_Z))
                        for t in range(2):
                            for m in range(ET):
                                at = (2 * tp + t) * P
                                last = pe.matmul(bank[tp][:, t * D:(t + 1) * D],
                                                 h_moe[:, e % 2, m, at:at + P], wd[:, e, m, :],
                                                 start=(m == 0), stop=(m == ET - 1))
                        last.then_inc(down_full.sem, 1)

                gate_up(0)
                for e in range(1, EXPERTS):
                    gate_up(e)
                    down(e - 1)
                down(EXPERTS - 1)

        @block.vector
        def _(dve):
            dve.wait_ge(consts_made.sem, 1)
            for k, (_, staged, (hi, lo)) in enumerate(split_plan):
                dve.wait_ge(hi_split.sem, k + 1)
                dve.tensor_tensor(lo[:], staged, hi[:], ALU.subtract).then_inc(lo_split.sem, 1)
            dve.memset(wait_cell[:, 1:2], 0.0).then_inc(moe_done.sem, moe_done.at_start)
            dve.memset(wait_cell[:, 2:3], 0.0).then_inc(stored.sem, stored.at_start)
            dve.reciprocal(rtemp[:], temp_all[:]).then_inc(setup_step.sem, 1)
            dve.wait_ge(lo_split.sem, N_SPLIT)
            dve.wait_ge(setup_step.sem, 17)

            def carry_wait():
                dve.memset(wait_cell[:, 0:1], 0.0)

            def norm(b, n, src, dst, ready, per_tile):
                for s in range(2):
                    half = range(s * TT // 2, (s + 1) * TT // 2)
                    for t in half:
                        dve.wait_ge(ready.sem, ready.at(b, math.ceil((t + 1) * per_tile)))
                        dve.bn_stats(bn[:, t, :], src[:, t, :]).then_inc(bn_done.sem, 1)
                    dve.wait_ge(bn_done.sem, bn_done.at(b, n * TT + half[-1] + 1))
                    carry_wait()
                    for t in half:
                        dve.bn_aggr(mv[:, t, :], bn[:, t, :]).then_inc(stats_done.sem, 1)
                for t in range(TT):
                    if t % 4 == 0:
                        dve.wait_ge(rstd_done.sem, rstd_done.at(b, n * 2 + t // 4 + 1))
                    dve.tensor_scalar(dst[:, t, :], src[:, t, :], mv[:, t, 0:1], rstd[:, t:t + 1],
                                      ALU.subtract, ALU.mult).then_inc(norm_done.sem, 1)

            def xT_los(b, n, affine):
                for k in range(4):
                    i, c = divmod(k, KC)
                    src = bank[XT_BANK[n] + k][:]
                    at = slice(i * NB, (i + 1) * NB)
                    dve.wait_ge(xT_hi_done.sem, xT_hi_done.at(b, 4 * n + k + 1))
                    if affine:
                        if k >= 2:
                            dve.wait_ge(xT_lo_done.sem, xT_lo_done.at(b, 4 * n + k - 1))
                        dve.tensor_scalar(gtmp[:, k % 2, :], src, gamma[:, c:c + 1], beta[:, c:c + 1],
                                          ALU.mult, ALU.add).then_inc(xT_affine.sem, 1)
                        dve.wait_ge(xT_affine.sem, xT_affine.at(b, 4 * n + k + 1))
                        src = gtmp[:, k % 2, :]
                    dve.tensor_tensor(xT[1][:, c, at], src, xT[0][:, c, at], ALU.subtract)\
                       .then_inc(xT_lo_done.sem, 1)

            with dve.Fori(0, BATCH) as b:
                dve.wait_ge(x_loaded.sem, x_loaded.at(b, 32))
                norm(b, 0, x_tok, y_tok, x_loaded, 4)
                norm(b, 1, y_tok, n_tok, norm_done, 1)
                xT_los(b, 0, True)
                for t in range(TT):
                    dve.wait_ge(kv_full.sem, kv_full.at(b, t + 1))
                    dve.tensor_scalar(kv_tok[:, t, 0:D], bank[4 + t % 4][:, 0:D], 0.0, 1e-3, ALU.max, ALU.add)
                    dve.tensor_copy(kv_tok[:, t, D:2 * D], bank[4 + t % 4][:, D:2 * D]).then_inc(kv_done.sem, 1)
                dve.wait_ge(stored.sem, stored.at(b, 0))
                for k in range(4):
                    m, i = divmod(k, IB)
                    dve.wait_ge(q_full.sem, q_full.at(b, k + 1))
                    dve.tensor_scalar(qpT[:, m, i * NB:(i + 1) * NB], bank[k][:], 0.0, 1e-3, ALU.max, ALU.add)\
                       .then_inc(q_done.sem, 1)
                for m in range(KC):
                    dve.wait_ge(kvs_full.sem, kvs_full.at(b, m + 1))
                    dve.tensor_tensor(kvsB[:, m], bank[4 + m][:, 0:2 * P].rearrange("p (a n) -> p a n", a=2),
                                      head_mask[:], ALU.mult).then_inc(kvs_done.sem, 1)
                for k in range(4):
                    m, i = divmod(k, IB)
                    dve.wait_ge(numden_full.sem, numden_full.at(b, k + 1))
                    if k >= 2:
                        dve.wait_ge(att0_done.sem, att0_done.at(b, k - 1))
                    dve.reciprocal(den0[:, k % 2, :], bank[2 * (k % 2) + 1][:]).then_inc(rden_done.sem, 1)
                    dve.wait_ge(rden_done.sem, rden_done.at(b, k + 1))
                    dve.tensor_tensor(attT0[:, m, i * NB:(i + 1) * NB], bank[2 * (k % 2)][:],
                                      den0[:, k % 2, :], ALU.mult).then_inc(att0_done.sem, 1)
                for tp in range(4):
                    dve.wait_ge(wo_full.sem, wo_full.at(b, tp + 1))
                    dve.tensor_tensor(add1[:, 2 * tp:2 * tp + 2, :],
                                      bank[4 + tp][:].rearrange("p (t d) -> p t d", d=D),
                                      y_tok[:, 2 * tp:2 * tp + 2, :], ALU.add).then_inc(add1_done.sem, 1)
                norm(b, 2, add1, n_tok, add1_done, 0.5)
                xT_los(b, 1, True)
                for n in range(4):
                    dve.wait_ge(w2_full.sem, w2_full.at(b, n + 1))
                    dve.tensor_tensor(t1[:, 2 * n:2 * n + 2, :], bank[n][:].rearrange("p (t d) -> p t d", d=D),
                                      b2_all[:].unsqueeze(1).to_broadcast([P, 2, D]), ALU.add)\
                       .then_inc(t1_done.sem, 1)
                dve.wait_ge(x_add1_done.sem, x_add1_done.at(b, 1))
                for n in range(4):
                    pair = slice(2 * n, 2 * n + 2)
                    dve.wait_ge(gelu_done.sem, gelu_done.at(b, n + 1))
                    dve.tensor_tensor(x_tok[:, pair, :], x_tok[:, pair, :], t1[:, pair, :], ALU.add)\
                       .then_inc(x1_done.sem, 1)
                norm(b, 3, x_tok, n_tok, x1_done, 0.5)
                xT_los(b, 2, False)
                for k in range(PAIRS):
                    dve.wait_ge(relu_done.sem, relu_done.at(b, k + 1))
                    if k == 0:
                        dve.tensor_scalar(g_acc, relu_s[:, 0, :], w2p[:, 0:1], b2p[:], ALU.mult, ALU.add)\
                           .then_inc(g_done.sem, 1)
                        continue
                    dve.wait_ge(g_done.sem, g_done.at(b, k))
                    dve.scalar_tensor_tensor(out=g_acc, in0=relu_s[:, k % 2, :], scalar=w2p[:, k:k + 1],
                                             in1=g_acc, op0=ALU.mult, op1=ALU.add).then_inc(g_done.sem, 1)
                dve.wait_ge(x_bout_done.sem, x_bout_done.at(b, 1))
                for tp in range(4):
                    pair = slice(2 * tp, 2 * tp + 2)
                    dve.wait_ge(fo_full.sem, fo_full.at(b, tp + 1))
                    dve.tensor_tensor(x_tok[:, pair, :], bank[tp][:].rearrange("p (t d) -> p t d", d=D),
                                      x_tok[:, pair, :], ALU.add).then_inc(x2_done.sem, 1)
                norm(b, 4, x_tok, n_tok, x2_done, 0.5)
                xT_los(b, 3, False)
                for i in range(IB):
                    at = slice(i * NB, (i + 1) * NB)
                    dve.wait_ge(lat_hi_done.sem, lat_hi_done.at(b, i + 1))
                    dve.scalar_tensor_tensor(out=latT[1][:, at], in0=bank[i][0:LATENT, :], scalar=bl[:],
                                             in1=latT[0][:, at], op0=ALU.add, op1=ALU.subtract)\
                       .then_inc(lat_lo_done.sem, 1)
                for hi, lo, bias, first, hi_done, lo_done in ((kT_hi, kT_lo, bk, 4, k1_hi_done, k1_lo_done),
                                                              (qT_hi, qT_lo, bq, 0, q1_hi_done, q1_lo_done)):
                    for k in range(4):
                        m, i = divmod(k, IB)
                        at = slice(i * NB, (i + 1) * NB)
                        dve.wait_ge(hi_done.sem, hi_done.at(b, k + 1))
                        dve.scalar_tensor_tensor(out=lo[:, m, at], in0=bank[first + k][:], scalar=bias[:, m:m + 1],
                                                 in1=hi[:, m, at], op0=ALU.add, op1=ALU.subtract)\
                           .then_inc(lo_done.sem, 1)
                for tp in range(4):
                    dve.wait_ge(v1_full.sem, v1_full.at(b, tp + 1))
                    dve.tensor_tensor(v_aug[:, 2 * tp:2 * tp + 2, :, 0:DH],
                                      bank[4 + tp][:].rearrange("p (t h c) -> p t h c", t=2, c=DH),
                                      bv_all[:].rearrange("p (h c) -> p h c", c=DH).unsqueeze(1)
                                      .to_broadcast([P, 2, HEADS, DH]), ALU.add).then_inc(v1_done.sem, 1)

                def group_maxima(g):
                    dve.wait_ge(rows_max_done.sem, rows_max_done.at(b, MAX_TILES * (g + 1)))
                    if g:
                        dve.wait_ge(mT_full.sem, mT_full.at(b, g))
                    dve.tensor_reduce(head_max[:], row_max[:, g % 2], AX_X, ALU.max).then_inc(max_step.sem, 1)
                    dve.wait_ge(max_step.sem, max_step.at(b, 2 * g + 1))
                    dve.tensor_scalar(m16[:, :, :, 0], head_max[:], -1.0 / MAX_UNIT, None, ALU.mult)\
                       .then_inc(max_step.sem, 1)
                    dve.wait_ge(max_step.sem, max_step.at(b, 2 * g + 2))
                    dve.scalar_tensor_tensor(out=m16[:, :, :, 1], in0=head_max[:], scalar=-1.0 / MAX_UNIT,
                                             in1=m16[:, :, :, 0], op0=ALU.mult, op1=ALU.subtract)\
                       .then_inc(m16_done.sem, 1)

                def normalise(g):
                    dve.wait_ge(o_done.sem, o_done.at(b, 2 * g + 2))
                    if g:
                        dve.wait_ge(att1_done.sem, att1_done.at(b, g))
                    carry_wait()
                    dve.stream_shuffle(den1[:, 0, :], oT[:, g, :], mask=[DH] * 32).then_inc(den_step.sem, 1)
                    dve.wait_ge(den_step.sem, den_step.at(b, 2 * g + 1))
                    dve.reciprocal(den1[:, 1, :], den1[:, 0, :]).then_inc(den_step.sem, 1)
                    dve.wait_ge(den_step.sem, den_step.at(b, 2 * g + 2))
                    dve.tensor_tensor(oT[:, g, :], oT[:, g, :], den1[:, 1, :], ALU.mult)\
                       .then_inc(att1_done.sem, 1)

                for s in range(2):
                    dve.wait_ge(stack_loaded[s].sem, stack_loaded[s].at(b, 16 * 6 * GH))
                for n in range(GROUPS * MAX_TILES):
                    g, r = divmod(n, MAX_TILES)
                    it, hh, jb = r // (GH * IB), (r // IB) % GH, r % IB
                    dve.wait_ge(rows_full.sem, rows_full.at(b, n + 1))
                    if r == 0 and g >= 2:
                        dve.wait_ge(m16_done.sem, m16_done.at(b, g - 1))
                    dve.tensor_reduce(row_max[:, g % 2, it, hh, jb:jb + 1], bank[n % 2][:], AX_X, ALU.max)\
                       .then_inc(rows_max_done.sem, 1)
                    if r == MAX_TILES - 1:
                        group_maxima(g)
                    for done in range(GROUPS):
                        if n == AHEAD + 4 * (BURSTS * (done + 1) + 2):
                            normalise(done)
                for g in range(GROUPS):
                    if AHEAD + 4 * (BURSTS * (g + 1) + 2) >= GROUPS * MAX_TILES:
                        normalise(g)
                for tp in range(4):
                    pair = slice(2 * tp, 2 * tp + 2)
                    dve.wait_ge(o1_full.sem, o1_full.at(b, tp + 1))
                    dve.tensor_tensor(x_tok[:, pair, :], bank[tp][:].rearrange("p (t d) -> p t d", d=D),
                                      x_tok[:, pair, :], ALU.add).then_inc(x3_done.sem, 1)
                norm(b, 5, x_tok, n_tok, x3_done, 0.5)
                xT_los(b, 4, False)
                steps = 0

                def step(instruction):
                    nonlocal steps
                    steps += 1
                    instruction.then_inc(route_step.sem, 1)
                    dve.wait_ge(route_step.sem, route_step.at(b, steps))

                def per_expert(v):
                    return v.unsqueeze(2).to_broadcast([P, TT, EXPERTS])

                z, inh, zone, low, dist, w, fb = rt[:, 0], rt[:, 2], rt[:, 3], rt[:, 4], rt[:, 5], rt[:, 6], rt[:, 7]
                rank, chosen, none, rsum = rt[:, 8], rt[:, 9], rt1[:, 0], rt1[:, 1]
                dve.wait_ge(route_full.sem, route_full.at(b, 1))
                step(dve.tensor_scalar(z, bank[0][:, 0:TT * EXPERTS].rearrange("p (t e) -> p t e", e=EXPERTS),
                                       rtemp[:], None, ALU.mult))
                assert steps == ROUTE_Z
                dve.wait_ge(route_exp.sem, route_exp.at(b, 1))
                step(dve.tensor_scalar(rt[:, 10], rt[:, 1], 1.0, None, ALU.add))
                step(dve.reciprocal(inh, rt[:, 10]))
                step(dve.tensor_scalar(low, inh, ZONE_LOWER, None, ALU.is_ge))
                step(dve.scalar_tensor_tensor(out=zone, in0=inh, scalar=ZONE_UPPER, in1=low,
                                              op0=ALU.is_le, op1=ALU.mult))
                step(dve.tensor_scalar(rt[:, 11], inh, ZONE_CENTER, None, ALU.subtract))
                step(dve.scalar_tensor_tensor(out=dist, in0=rt[:, 11], scalar=-1.0, in1=rt[:, 11],
                                              op0=ALU.mult, op1=ALU.max))
                assert steps == ROUTE_DIST
                dve.wait_ge(route_exp.sem, route_exp.at(b, 3))
                step(dve.tensor_tensor(rt[:, 10], w, zone, ALU.mult))
                step(dve.tensor_reduce(rsum, rt[:, 10], AX_X, ALU.add))
                step(dve.tensor_scalar(none, rsum, 1e-8, None, ALU.is_lt))
                ahead, equal = pairs
                mine = fb.unsqueeze(3).to_broadcast([P, TT, EXPERTS, EXPERTS])
                other = fb.unsqueeze(2).to_broadcast([P, TT, EXPERTS, EXPERTS])
                step(dve.tensor_tensor(ahead, other, mine, ALU.is_gt))
                step(dve.tensor_tensor(equal, other, mine, ALU.is_equal))
                step(dve.tensor_tensor(equal, equal, before[:].unsqueeze(1).to_broadcast(
                    [P, TT, EXPERTS, EXPERTS]), ALU.mult))
                step(dve.tensor_tensor(ahead, ahead, equal, ALU.add))
                step(dve.tensor_reduce(rank, ahead, AX_X, ALU.add))
                step(dve.scalar_tensor_tensor(out=chosen, in0=rank, scalar=2.0, in1=fb,
                                              op0=ALU.is_lt, op1=ALU.mult))
                step(dve.tensor_reduce(rt1[:, 2], chosen, AX_X, ALU.add))
                step(dve.tensor_scalar(rt1[:, 3], rt1[:, 2], 1e-8, None, ALU.max))
                step(dve.reciprocal(rt1[:, 4], rt1[:, 3]))
                step(dve.tensor_tensor(chosen, chosen, per_expert(rt1[:, 4]), ALU.mult))
                step(dve.tensor_tensor(chosen, chosen, per_expert(none), ALU.mult))
                step(dve.tensor_scalar(rt1[:, 5], none, -1.0, 1.0, ALU.mult, ALU.add))
                step(dve.tensor_tensor(rt[:, 11], rt[:, 10], per_expert(rt1[:, 5]), ALU.mult))
                step(dve.tensor_tensor(rt[:, 11], rt[:, 11], chosen, ALU.add))
                step(dve.tensor_reduce(rt1[:, 2], rt[:, 11], AX_X, ALU.add))
                step(dve.tensor_scalar(rt1[:, 3], rt1[:, 2], 1e-8, None, ALU.max))
                step(dve.reciprocal(rt1[:, 4], rt1[:, 3]))
                step(dve.tensor_tensor(rt[:, 10], rt[:, 11], per_expert(rt1[:, 4]), ALU.mult))
                route_w = rt[:, 10]
                assert steps == ROUTE_STEPS, steps

                def hidden(e):
                    for k in range(4):
                        m, i = divmod(k, IB)
                        j = 4 * e + k
                        dve.wait_ge(silu_done.sem, silu_done.at(b, j + 1))
                        dve.wait_ge(up_full.sem, up_full.at(b, j + 1))
                        dve.tensor_tensor(h_moe[:, e % 2, m, i * NB:(i + 1) * NB], silu[:, j % 2, :],
                                          bank[5 + 2 * (j % 2)][:], ALU.mult).then_inc(hmoe_done.sem, 1)

                def weigh(e):
                    for t in range(TT):
                        if t % 2 == 0:
                            dve.wait_ge(down_full.sem, down_full.at(b, 4 * e + t // 2 + 1))
                        if e:
                            dve.wait_ge(moe_done.sem, moe_done.at(b, (e - 1) * TT + t + 1))
                        dve.scalar_tensor_tensor(out=moe_acc[:, t, :], in0=bank[t // 2][:, (t % 2) * D:(t % 2 + 1) * D],
                                                 scalar=route_w[:, t, e:e + 1],
                                                 in1=(moe_acc if e else x_tok)[:, t, :],
                                                 op0=ALU.mult, op1=ALU.add).then_inc(moe_done.sem, 1)

                hidden(0)
                for e in range(1, EXPERTS):
                    hidden(e)
                    weigh(e - 1)
                weigh(EXPERTS - 1)


XT_BANK = [0, 0, 0, 4, 4]
ROUTE_Z = 1
ROUTE_DIST = 7

_INS = ['L0_attn_x', 'L0_attn_gamma1', 'L0_attn_beta1', 'L0_attn_wq', 'L0_attn_wk', 'L0_attn_wv', 'L0_attn_wo',
        'L0_attn_w1', 'L0_attn_b1', 'L0_attn_w2', 'L0_attn_b2', 'L0_ffn_Win', 'L0_ffn_bin_', 'L0_ffn_W1',
        'L0_ffn_b1', 'L0_ffn_W2', 'L0_ffn_b2', 'L0_ffn_Wout', 'L0_ffn_bout', 'L1_attn_Wq', 'L1_attn_bq',
        'L1_attn_Wl', 'L1_attn_bl', 'L1_attn_Wk', 'L1_attn_bk', 'L1_attn_Wv', 'L1_attn_bv', 'L1_attn_Wo',
        'L1_attn_bo', 'L1_ffn_Wg', 'L1_ffn_Wu', 'L1_ffn_Wd', 'L1_ffn_Wr', 'L1_ffn_temperature']


def kernel(**inputs):
    import numpy as _np
    import concourse.bacc as _bacc
    from concourse import mybir as _mybir
    from concourse.bass_utils import run_bass_kernel_spmd as _run

    nc = _bacc.Bacc("TRN2", target_bir_lowering=False, num_devices=1)
    arrays, args = {}, {}
    for name in _INS:
        a = _np.ascontiguousarray(inputs[name])
        arrays[f"in_{name}_dram"] = a
        args[name] = nc.dram_tensor(f"in_{name}_dram", a.shape, _mybir.dt.from_np(a.dtype),
                                    kind="ExternalInput").ap()
    out = nc.dram_tensor("out_0_dram", (BATCH, TOKENS, D), F32, kind="ExternalOutput").ap()
    build(nc, args, out)
    r = _run(nc, [arrays], core_ids=[0])
    return r.results[0]["out_0_dram"]
```

```python
import math
import struct
from contextlib import ExitStack

import concourse.bass as bass
from concourse import mybir

ALU = mybir.AluOpType
ACT = mybir.ActivationFunctionType
F32 = mybir.dt.float32
F16 = mybir.dt.float16
AX_X = mybir.AxisListType.X

P = 128
BATCH, TOKENS, D = 8, 1024, 256
TT = TOKENS // P
NB = 512
IB = TOKENS // NB
KC = D // P
HEADS, DH = 16, 16
FF = 1024
FT = FF // P
M0, INNER = 64, 16
PAIRS = INNER // 2
LATENT = 64
EXPERTS, EI = 8, 256
ET = EI // P
GROUPS, GH = 4, 4
HALF = 64
SPLIT_ROWS = 3 * DH
MAX_UNIT = 256.0
PAIR_OF_UNITS = 0x5C005C00
UNITS = GROUPS * IB
P_SLOTS = 8
BURSTS = TT
MAX_TILES = (TT // IB) * GH * IB
AHEAD = MAX_TILES + 12
NORMS = 6
ROUTE_STEPS = 28
SCALE = DH ** -0.5
ZONE_CENTER = 1.0 / math.e
ZONE_LOWER = 0.5 - math.log(4.0 / 3.0)
ZONE_UPPER = 0.5


class Signal:

    def __init__(self, sem, per_batch, at_start=0):
        self.sem, self.per_batch, self.at_start = sem, per_batch, at_start

    def at(self, b, n):
        return b * self.per_batch + self.at_start + n


def build(nc, a, out):
    nc.disable_value_cache = True
    ctx = ExitStack()
    with ctx:
        def sb(name, shape, dt=F32):
            return ctx.enter_context(nc.sbuf_tensor(name, shape, dt))

        def signal(name, per_batch=1, at_start=0):
            return Signal(ctx.enter_context(nc.semaphore(name)), per_batch, at_start)

        def split_weight(name, shape):
            return sb(name + "_hi", shape, F16), sb(name + "_lo", shape, F16)

        wq0 = split_weight("wq0", [P, KC, D])
        wkv0 = split_weight("wkv0", [P, KC, 2 * D])
        w1 = split_weight("w1", [P, KC, FF])
        win = split_weight("win", [P, KC, 2 * M0])
        wl = split_weight("wl", [P, KC, LATENT])
        wq1 = split_weight("wq1", [P, KC, D])
        wk1 = split_weight("wk1", [LATENT, D])
        wv1 = split_weight("wv1", [LATENT, D])
        wr = split_weight("wr", [P, KC, EXPERTS])
        wg = split_weight("wg", [P, EXPERTS, KC, EI])
        wu = split_weight("wu", [P, EXPERTS, KC, EI])
        wo0 = sb("wo0", [P, KC, D])
        w2 = sb("w2", [P, FT, D])
        wout = sb("wout", [P, D])
        wo1 = sb("wo1", [P, GROUPS, D])
        wd = sb("wd", [P, EXPERTS, ET, D])
        gamma = sb("gamma", [P, KC])
        beta = sb("beta", [P, KC])
        b1 = sb("b1", [P, FT])
        bin2 = sb("bin2", [P, 1])
        w1p = sb("w1p", [P, PAIRS])
        b1p = sb("b1p", [P, PAIRS])
        w2p = sb("w2p", [P, PAIRS])
        b2p = sb("b2p", [P, 1])
        bq = sb("bq", [P, KC])
        bk = sb("bk", [P, KC])
        bl = sb("bl", [LATENT, 1])
        b2_all = sb("b2_all", [P, D])
        bout_all = sb("bout_all", [P, D])
        bv_all = sb("bv_all", [P, D])
        temp_all = sb("temp_all", [P, 1])
        rtemp = sb("rtemp", [P, 1])
        ident = sb("ident", [P, P])
        ident16 = sb("ident16", [P, P], F16)
        head_mask = sb("head_mask", [P, 2, P])
        ones_tok = sb("ones_tok", [P, P])
        before = sb("before", [P, EXPERTS, EXPERTS])
        eps = sb("eps", [P, 2, TT // 2])
        neg_half = sb("neg_half", [P, TT // 2])
        x_tok = sb("x_tok", [P, TT, D])
        r0 = sb("r0", [P, 2 * TT * D])
        r1 = sb("r1", [P, 4096])
        r2 = sb("r2", [P, 4096])
        r3 = sb("r3", [P, 4096])
        xT_both = sb("xT", [P, 2, KC, TOKENS], F16)
        xT = (xT_both[:, 0], xT_both[:, 1])
        qs = sb("q_stack", [P, 2, GH, TOKENS], F16)
        ks = sb("k_stack", [P, 2, GH, TOKENS], F16)
        bn = sb("bn", [P, TT, 6])
        mv = sb("mv", [P, TT, 2])
        var_eps = sb("var_eps", [P, TT])
        rstd = sb("rstd", [P, TT])
        row_max = sb("row_max", [P, 2, TT // IB, GH, IB])
        head_max = sb("head_max", [P, TT // IB, GH])
        m16 = sb("m16", [P, TT // IB, GH, 2], F16)
        mT = sb("mT", [2 * GH, NB], F16)
        max_rows = sb("max_rows", [P, GH])
        zero_cell = sb("zero_cell", [P, 1])
        rt = sb("route", [P, 12, TT, EXPERTS])
        rt1 = sb("route_sums", [P, 6, TT])

        def view(region, start, size, pattern, **kw):
            return region[:, start:start + size].rearrange(pattern, **kw)

        y_tok = view(r0, 0, TT * D, "p (t d) -> p t d", d=D)
        n_tok = view(r0, TT * D, TT * D, "p (t d) -> p t d", d=D)
        probs = view(r0, 0, P_SLOTS * NB, "p (s n) -> p s n", n=NB)
        kv_tok = view(r1, 0, TT * 2 * D, "p (t n) -> p t n", n=2 * D)
        v_aug = view(r1, 0, TT * HEADS * 32, "p (t h c) -> p t h c", h=HEADS, c=32)
        h_ff = view(r2, 0, FT * NB, "p (f n) -> p f n", n=NB)
        attT0 = view(r2, 0, KC * TOKENS, "p (c n) -> p c n", c=KC)
        den0 = view(r2, 2048, 2 * NB, "p (s n) -> p s n", n=NB)
        gtmp = view(r2, 3072, 2 * NB, "p (s n) -> p s n", n=NB)
        s_dup = r2[:, 0:TOKENS]
        relu_s = view(r2, 1024, 2 * TOKENS, "p (s n) -> p s n", s=2)
        g_acc = r2[:, 3072:4096]
        qT_hi, qT_lo, kT_hi, kT_lo = [r3[:, 1024 * k:1024 * (k + 1)].bitcast(F16)
                                      .rearrange("p (c n) -> p c n", c=KC) for k in range(4)]
        latT = [r2[0:LATENT, 512 * k:512 * (k + 1)].bitcast(F16) for k in range(2)]
        den1 = view(r2, 0, 2 * NB, "p (s n) -> p s n", s=2)
        late_words = {2: xT_both[:].bitcast(F32).rearrange("p a c n -> p (a c n)"), 3: r2[:, 2048:4096]}
        k_stack = [ks[:, 0], ks[:, 1]] + [late_words[g].bitcast(F16).rearrange("p (h n) -> p h n", h=GH)
                                          for g in (2, 3)]
        h_moe = view(r2, 0, 2 * ET * TOKENS, "p (s m n) -> p s m n", s=2, m=ET)
        qpT = view(r3, 0, KC * TOKENS, "p (c n) -> p c n", c=KC)
        t1 = view(r3, 0, TT * D, "p (t d) -> p t d", d=D)
        add1 = view(r3, 2048, TT * D, "p (t d) -> p t d", d=D)
        oT = view(r3, 0, GROUPS * TOKENS, "p (g n) -> p g n", g=GROUPS)
        moe_acc = view(r3, 0, TT * D, "p (t d) -> p t d", d=D)
        silu = view(r3, 2048, 2 * NB, "p (s n) -> p s n", n=NB)
        pairs = [view(r3, 3072 + 512 * k, 512, "p (t e f) -> p t e f", e=EXPERTS, f=EXPERTS)
                 for k in range(2)]
        wait_cell = sb("wait_cell", [P, 4])
        kvsB = view(r3, 2048, KC * 2 * P, "p (c a n) -> p c a n", c=KC, a=2)

        bank = [ctx.enter_context(nc.psum_tensor(f"bank{k}", [P, NB], F32)) for k in range(8)]

        weights_loaded = signal("weights_loaded")
        hi_split = signal("hi_split")
        lo_split = signal("lo_split")
        setup_step = signal("setup_step")
        consts_made = signal("consts_made")
        x_loaded = signal("x_loaded", 32)
        bn_done = signal("bn_done", NORMS * TT)
        stats_done = signal("stats_done", NORMS * TT)
        eps_added = signal("eps_added", NORMS * 2)
        rstd_done = signal("rstd_done", NORMS * 2)
        norm_done = signal("norm_done", NORMS * TT)
        xT_full = signal("xT_full", 5 * 4)
        xT_hi_done = signal("xT_hi_done", 5 * 4)
        xT_affine = signal("xT_affine", 2 * 4)
        xT_lo_done = signal("xT_lo_done", 5 * 4)
        kv_full = signal("kv_full", TT)
        kv_done = signal("kv_done", TT)
        q_full = signal("q_full", 4)
        q_done = signal("q_done", 4)
        kvs_full = signal("kvs_full", KC)
        kvs_done = signal("kvs_done", KC)
        numden_full = signal("numden_full", 4)
        rden_done = signal("rden_done", 4)
        att0_done = signal("att0_done", 4)
        wo_full = signal("wo_full", 4)
        add1_done = signal("add1_done", 4)
        h_full = signal("h_full", 2 * FT)
        h_done = signal("h_done", 2 * FT)
        w2_full = signal("w2_full", 4)
        t1_done = signal("t1_done", 4)
        gelu_done = signal("gelu_done", 4)
        x_add1_done = signal("x_add1_done", 1)
        x1_done = signal("x1_done", 4)
        s_full = signal("s_full", 2)
        s_done = signal("s_done", 2)
        relu_done = signal("relu_done", PAIRS)
        g_done = signal("g_done", PAIRS)
        x_bout_done = signal("x_bout_done", 1)
        fo_full = signal("fo_full", 4)
        x2_done = signal("x2_done", 4)
        lat_full = signal("lat_full", 2)
        lat_hi_done = signal("lat_hi_done", 2)
        lat_lo_done = signal("lat_lo_done", 2)
        k1_full = signal("k1_full", 4)
        k1_hi_done = signal("k1_hi_done", 4)
        k1_lo_done = signal("k1_lo_done", 4)
        q1_full = signal("q1_full", 4)
        q1_hi_done = signal("q1_hi_done", 4)
        q1_lo_done = signal("q1_lo_done", 4)
        v1_full = signal("v1_full", 4)
        v1_done = signal("v1_done", 4)
        v_ones_done = signal("v_ones_done", 1)
        late_slots_ready = signal("late_slots_ready", 4)
        q_loaded = [signal(f"q_loaded{slot}", 16 * 2 * 3 * GH) for slot in range(2)]
        k_loaded = [signal(f"k_loaded{g}", 16 * 3 * GH) for g in range(GROUPS)]
        rows_full = signal("rows_full", UNITS * MAX_TILES)
        rows_max_done = signal("rows_max_done", UNITS * MAX_TILES)
        max_step = signal("max_step", 2 * UNITS)
        m16_done = signal("m16_done", UNITS)
        mT_full = signal("mT_full", UNITS)
        mT_done = signal("mT_done", UNITS)
        m_loaded = signal("m_loaded", 16 * UNITS)
        m_cleared = signal("m_cleared", 16 * GROUPS, at_start=1)
        cols_full = signal("cols_full", UNITS * BURSTS * GH)
        exp_done = signal("exp_done", UNITS * BURSTS * GH)
        av_done = signal("av_done", UNITS * BURSTS)
        o_done = signal("o_done", UNITS)
        den_step = signal("den_step", 2 * UNITS)
        att1_done = signal("att1_done", UNITS)
        o1_full = signal("o1_full", 4)
        x3_done = signal("x3_done", 4)
        route_full = signal("route_full", 1)
        route_step = signal("route_step", ROUTE_STEPS)
        route_exp = signal("route_exp", 3)
        gate_full = signal("gate_full", EXPERTS * 4)
        up_full = signal("up_full", EXPERTS * 4)
        silu_done = signal("silu_done", EXPERTS * 4)
        hmoe_done = signal("hmoe_done", EXPERTS * 4)
        down_full = signal("down_full", EXPERTS * 4)
        moe_done = signal("moe_done", EXPERTS * TT, at_start=1)
        stored = signal("stored", 64, at_start=1)

        def stage(region, start, rows, shape):
            n = math.prod(shape)
            names = "abc"[:len(shape)]
            v = region[0:rows, start:start + n]
            if len(shape) == 1:
                return v
            return v.rearrange(f"p ({' '.join(names)}) -> p {' '.join(names)}", **dict(zip(names, shape)))

        chunk = "(c p) n -> p c n"
        st_kv = stage(r3, 2048, P, [KC, 2 * D])
        st_win = stage(r0, 0, P, [KC, 2 * M0])
        split_plan = [
            ([(stage(r1, 0, P, [EXPERTS, KC, EI]), a["L1_ffn_Wg"].rearrange("e (c p) n -> p e c n", p=P))],
             stage(r1, 0, P, [EXPERTS, KC, EI]), wg),
            ([(stage(r2, 0, P, [EXPERTS, KC, EI]), a["L1_ffn_Wu"].rearrange("e (c p) n -> p e c n", p=P))],
             stage(r2, 0, P, [EXPERTS, KC, EI]), wu),
            ([(stage(r3, 0, P, [KC, FF]), a["L0_attn_w1"].rearrange(chunk, p=P))],
             stage(r3, 0, P, [KC, FF]), w1),
            ([(st_kv[:, :, 0:D], a["L0_attn_wk"].rearrange("(c p) h d -> p c (h d)", p=P)),
              (st_kv[:, :, D:2 * D], a["L0_attn_wv"].rearrange("(c p) h d -> p c (h d)", p=P))],
             st_kv, wkv0),
            ([(stage(r3, 3072, P, [KC, D]), a["L0_attn_wq"].rearrange("(c p) h d -> p c (h d)", p=P))],
             stage(r3, 3072, P, [KC, D]), wq0),
            ([(stage(r3, 3584, P, [KC, D]), a["L1_attn_Wq"].rearrange(chunk, p=P))],
             stage(r3, 3584, P, [KC, D]), wq1),
            ([(st_win[:, :, s * M0:(s + 1) * M0], a["L0_ffn_Win"].rearrange(chunk, p=P)) for s in range(2)],
             st_win, win),
            ([(stage(r0, 256, P, [KC, LATENT]), a["L1_attn_Wl"].rearrange(chunk, p=P))],
             stage(r0, 256, P, [KC, LATENT]), wl),
            ([(stage(r0, 512, LATENT, [D]), a["L1_attn_Wk"])], stage(r0, 512, LATENT, [D]), wk1),
            ([(stage(r0, 768, LATENT, [D]), a["L1_attn_Wv"])], stage(r0, 768, LATENT, [D]), wv1),
            ([(stage(r0, 1024, P, [KC, EXPERTS]), a["L1_ffn_Wr"].rearrange(chunk, p=P))],
             stage(r0, 1024, P, [KC, EXPERTS]), wr),
        ]

        def column(vec, rows):
            return vec.rearrange("(c p) -> p c", p=rows)

        def halves(m):
            return m.rearrange("m (k two) -> two m k", two=2)

        def row_for_all(vec):
            return vec.partition_broadcast(P)

        plain_loads = [
            (wo0[:], a["L0_attn_wo"].rearrange("(c h) d n -> (h d) c n", c=KC)),
            (w2[:], a["L0_attn_w2"].rearrange(chunk, p=P)),
            (wout[0:M0, :], a["L0_ffn_Wout"]), (wout[M0:P, :], a["L0_ffn_Wout"]),
            (wd[:, 0:4], a["L1_ffn_Wd"][0:4].rearrange("e (m p) n -> p e m n", p=P)),
            (wd[:, 4:8], a["L1_ffn_Wd"][4:8].rearrange("e (m p) n -> p e m n", p=P)),
            (gamma[:], column(a["L0_attn_gamma1"], P)), (beta[:], column(a["L0_attn_beta1"], P)),
            (b1[:], column(a["L0_attn_b1"], P)), (bq[:], column(a["L1_attn_bq"], P)),
            (bk[:], column(a["L1_attn_bk"], P)), (bl[:], column(a["L1_attn_bl"], LATENT)),
            (b2_all[:], row_for_all(a["L0_attn_b2"])), (bout_all[:], row_for_all(a["L0_ffn_bout"])),
            (bv_all[:], row_for_all(a["L1_attn_bv"])), (temp_all[:], row_for_all(a["L1_ffn_temperature"])),
        ]
        for s in range(2):
            rows = slice(s * M0, (s + 1) * M0)
            plain_loads += [
                (bin2[rows, :], column(a["L0_ffn_bin_"], M0)),
                (w1p[rows, :], halves(a["L0_ffn_W1"])[s]), (b1p[rows, :], halves(a["L0_ffn_b1"])[s]),
                (w2p[rows, :], halves(a["L0_ffn_W2"])[s]),
            ]
        zeroed_loads = [(wo1[32 * c:32 * c + DH, :, :],
                         a["L1_attn_Wo"].rearrange("(g c r) n -> c r g n", g=GROUPS, c=GH)[c])
                        for c in range(GH)]
        zeroed_loads.append((wo1[DH:DH + 1, 0, :], a["L1_attn_bo"].rearrange("(a n) -> a n", a=1)))
        zeroed_loads.append((b2p[0:M0, :], column(a["L0_ffn_b2"], M0)))
        N_LOADS = sum(len(x[0]) for x in split_plan) + len(plain_loads) + len(zeroed_loads)
        N_SPLIT = len(split_plan)

        x_view = a["L0_attn_x"].rearrange("b (t p) d -> b p t d", p=P)
        out_view = out.rearrange("b (t p) d -> b p t d", p=P)

        def stack_rows(g, hh, part):
            row, at = HALF * (g % 2) + DH * hh, HALF * (g // 2) + DH * part
            return slice(row, row + DH), slice(at, at + DH)

        def load_q(eng, g):
            for hh in range(GH):
                for part in range(3):
                    rows, at = stack_rows(g, hh, part)
                    eng.dma_start(qs[at, g % 2, hh, :], (qT_hi, qT_lo, qT_hi)[part][rows, g // 2, :])\
                       .then_inc(q_loaded[g % 2].sem, 16)

        def load_k(eng, g):
            for hh in range(GH):
                for part in range(3):
                    rows, at = stack_rows(g, hh, part)
                    eng.dma_start(k_stack[g][at, hh, :], (kT_hi, kT_hi, kT_lo)[part][rows, g // 2, :])\
                       .then_inc(k_loaded[g].sem, 16)

        def load_maxima(eng, u):
            g, ib = divmod(u, IB)
            at = HALF * (g // 2) + SPLIT_ROWS
            eng.dma_start(qs[at:at + 2 * GH, g % 2, :, ib * NB:(ib + 1) * NB],
                          mT[:].unsqueeze(1).to_broadcast([2 * GH, GH, NB])).then_inc(m_loaded.sem, 16)

        block = ctx.enter_context(nc.Block())

        @block.sync
        def _(sp):
            for loads, _, _ in split_plan:
                for dst, src in loads:
                    sp.dma_start(dst, src).then_inc(weights_loaded.sem, 16)
            with nc.allow_non_contiguous_dma(reason="a few KB of per-partition vectors, once"):
                for dst, src in plain_loads:
                    sp.dma_start(dst, src).then_inc(weights_loaded.sem, 16)
            sp.wait_ge(setup_step.sem, 2)
            with nc.allow_non_contiguous_dma(reason="one of them is a per-partition vector"):
                for dst, src in zeroed_loads:
                    sp.dma_start(dst, src).then_inc(weights_loaded.sem, 16)

            with sp.Fori(0, BATCH) as b:
                sp.wait_ge(m_cleared.sem, m_cleared.at(b, 0))
                sp.wait_ge(k1_lo_done.sem, k1_lo_done.at(b, 2))
                load_k(sp, 0)
                sp.wait_ge(q1_lo_done.sem, q1_lo_done.at(b, 2))
                load_q(sp, 1)
                sp.wait_ge(q1_lo_done.sem, q1_lo_done.at(b, 4))
                load_q(sp, 3)
                load_k(sp, 1)
                sp.wait_ge(k1_lo_done.sem, k1_lo_done.at(b, 4))
                sp.wait_ge(late_slots_ready.sem, late_slots_ready.at(b, 4))
                load_k(sp, 2)
                load_k(sp, 3)
                for u in range(1, UNITS):
                    sp.wait_ge(mT_done.sem, mT_done.at(b, u + 1))
                    load_maxima(sp, u)
                sp.wait_ge(exp_done.sem, exp_done.at(b, UNITS * BURSTS * GH))
                for g in range(GROUPS):
                    at = HALF * (g // 2) + SPLIT_ROWS
                    sp.dma_start(qs[at:at + 2 * GH, g % 2], qs[at + 2 * GH:at + 4 * GH, g % 2])\
                      .then_inc(m_cleared.sem, 16)
                for tp in range(4):
                    sp.wait_ge(moe_done.sem, moe_done.at(b, (EXPERTS - 1) * TT + 2 * tp + 2))
                    sp.dma_start(out_view[b, :, 2 * tp:2 * tp + 2, :], moe_acc[:, 2 * tp:2 * tp + 2, :])\
                      .then_inc(stored.sem, 16)
            sp.wait_ge(stored.sem, BATCH * stored.per_batch + stored.at_start)
            sp.wait_ge(m_cleared.sem, BATCH * m_cleared.per_batch + m_cleared.at_start)

        @block.gpsimd
        def _(pool):
            pool.memset(wo1[:], 0.0).then_inc(setup_step.sem, 1)
            pool.memset(b2p[:], 0.0).then_inc(setup_step.sem, 1)
            pool.memset(ident[:], 0.0).then_inc(setup_step.sem, 1)
            pool.memset(head_mask[:], 1.0).then_inc(setup_step.sem, 1)
            pool.memset(before[:], 0.0).then_inc(setup_step.sem, 1)
            pool.memset(ks[:], 0.0).then_inc(setup_step.sem, 1)
            pool.memset(qs[:], 0.0).then_inc(setup_step.sem, 1)
            pool.memset(ones_tok[:], 1.0).then_inc(setup_step.sem, 1)
            pool.memset(eps[:, 0, :], 1e-5).then_inc(setup_step.sem, 1)
            pool.memset(eps[:, 1, :], 1e-6).then_inc(setup_step.sem, 1)
            pool.memset(neg_half[:], -0.5).then_inc(setup_step.sem, 1)
            pool.memset(zero_cell[:], 0.0).then_inc(setup_step.sem, 1)
            pair = float(struct.unpack("f", struct.pack("I", PAIR_OF_UNITS))[0])
            pool.memset(max_rows[:], pair).then_inc(setup_step.sem, 1)
            pool.wait_ge(setup_step.sem, 13)
            for s in range(2):
                half = max_rows[HALF * s:HALF * (s + 1), :]
                pool.affine_select(out=half, in_=half, compare_op=ALU.is_ge, fill=0.0, base=-SPLIT_ROWS,
                                   pattern=[[-2, GH]], channel_multiplier=1).then_inc(setup_step.sem, 1)
            pool.wait_ge(setup_step.sem, 15)
            for s in range(2):
                half = max_rows[HALF * s:HALF * (s + 1), :]
                pool.affine_select(out=half, in_=half, compare_op=ALU.is_ge, fill=0.0, base=SPLIT_ROWS + 1,
                                   pattern=[[2, GH]], channel_multiplier=-1).then_inc(setup_step.sem, 1)
            pool.wait_ge(setup_step.sem, 17)
            for slot in range(2):
                pool.tensor_copy(ks[0:HALF, slot].bitcast(F32), max_rows[0:HALF, :].unsqueeze(2)
                                 .to_broadcast([HALF, GH, TOKENS // 2])).then_inc(setup_step.sem, 1)
            pool.affine_select(out=ident[:], in_=ident[:], compare_op=ALU.not_equal, fill=1.0, base=0,
                               pattern=[[-1, P]], channel_multiplier=1).then_inc(setup_step.sem, 1)
            pool.affine_select(out=before[:], in_=before[:], compare_op=ALU.is_ge, fill=1.0, base=0,
                               pattern=[[-1, EXPERTS], [1, EXPERTS]], channel_multiplier=0)\
                .then_inc(setup_step.sem, 1)
            mask = head_mask[:].rearrange("p a (h d) -> p a h d", d=DH)
            pool.affine_select(out=mask, in_=mask, compare_op=ALU.is_ge, fill=0.0, base=0,
                               pattern=[[0, 2], [-DH, P // DH], [0, DH]], channel_multiplier=1)\
                .then_inc(setup_step.sem, 1)
            pool.wait_ge(setup_step.sem, 22)
            pool.affine_select(out=mask, in_=mask, compare_op=ALU.is_ge, fill=0.0, base=DH - 1,
                               pattern=[[0, 2], [DH, P // DH], [0, DH]], channel_multiplier=-1)\
                .then_inc(setup_step.sem, 1)
            pool.tensor_copy(ident16[:], ident[:]).then_inc(setup_step.sem, 1)
            pool.wait_ge(setup_step.sem, 24)
            pool.wait_ge(weights_loaded.sem, 16 * N_LOADS)
            pool.memset(eps[:, 0, :], 1e-5).then_inc(consts_made.sem, 1)

            def rstds(b, norm, which_eps):
                for s in range(2):
                    half = slice(s * TT // 2, (s + 1) * TT // 2)
                    pool.wait_ge(stats_done.sem, stats_done.at(b, norm * TT + (s + 1) * TT // 2))
                    pool.tensor_tensor(var_eps[:, half], mv[:, half, 1], eps[:, which_eps, :], ALU.add)\
                        .then_inc(eps_added.sem, 1)
                    pool.wait_ge(eps_added.sem, eps_added.at(b, norm * 2 + s + 1))
                    pool.tensor_tensor(rstd[:, half], var_eps[:, half], neg_half[:], ALU.pow)\
                        .then_inc(rstd_done.sem, 1)

            with pool.Fori(0, BATCH) as b:
                pool.wait_ge(moe_done.sem, moe_done.at(b, 0))
                for s in range(2):
                    half = slice(s * TT // 2, (s + 1) * TT // 2)
                    pool.dma_start(x_tok[:, half, :], x_view[b, :, half, :]).then_inc(x_loaded.sem, 16)
                rstds(b, 0, 0)
                rstds(b, 1, 1)
                rstds(b, 2, 1)
                pool.wait_ge(add1_done.sem, add1_done.at(b, 4))
                pool.tensor_tensor(x_tok[:], x_tok[:], add1, ALU.add).then_inc(x_add1_done.sem, 1)
                pool.memset(v_aug[:, :, :, DH:32], 1.0).then_inc(v_ones_done.sem, 1)
                rstds(b, 3, 0)
                pool.wait_ge(norm_done.sem, norm_done.at(b, 4 * TT))
                pool.tensor_tensor(x_tok[:], x_tok[:], bout_all[:].unsqueeze(1).to_broadcast([P, TT, D]),
                                   ALU.add).then_inc(x_bout_done.sem, 1)
                rstds(b, 4, 0)
                rstds(b, 5, 0)

        @block.scalar
        def _(act):
            act.wait_ge(weights_loaded.sem, 16 * N_LOADS)
            for _, staged, (hi, _) in split_plan:
                act.activation(hi[:], staged, ACT.Copy).then_inc(hi_split.sem, 1)

            def xT_his(b, n, affine):
                for k in range(4):
                    i, c = divmod(k, KC)
                    dst = xT[0][:, c, i * NB:(i + 1) * NB]
                    act.wait_ge(xT_full.sem, xT_full.at(b, 4 * n + k + 1))
                    if affine:
                        act.activation(dst, bank[XT_BANK[n] + k][:], ACT.Identity, bias=beta[:, c:c + 1],
                                       scale=gamma[:, c:c + 1]).then_inc(xT_hi_done.sem, 1)
                    else:
                        act.activation(dst, bank[XT_BANK[n] + k][:], ACT.Copy).then_inc(xT_hi_done.sem, 1)

            with act.Fori(0, BATCH) as b:
                xT_his(b, 0, True)
                xT_his(b, 1, True)
                for i in range(IB):
                    for f in range(FT):
                        n = i * FT + f
                        act.wait_ge(h_full.sem, h_full.at(b, n + 1))
                        if i and f == 0:
                            act.wait_ge(w2_full.sem, w2_full.at(b, 2))
                        act.activation(h_ff[:, f, :], bank[4 + f % 4][:], ACT.Gelu, bias=b1[:, f:f + 1])\
                            .then_inc(h_done.sem, 1)
                    for tp in range(2):
                        n = 2 * i + tp
                        act.wait_ge(t1_done.sem, t1_done.at(b, n + 1))
                        act.activation(t1[:, 2 * n:2 * n + 2, :], t1[:, 2 * n:2 * n + 2, :], ACT.Gelu)\
                            .then_inc(gelu_done.sem, 1)
                xT_his(b, 2, False)
                for i in range(IB):
                    act.wait_ge(s_full.sem, s_full.at(b, i + 1))
                    act.activation(s_dup[:, i * NB:(i + 1) * NB], bank[4 + i][:], ACT.Identity, bias=bin2[:])\
                        .then_inc(s_done.sem, 1)
                act.wait_ge(s_done.sem, s_done.at(b, 2))
                for k in range(PAIRS):
                    if k >= 2:
                        act.wait_ge(g_done.sem, g_done.at(b, k - 1))
                    act.activation(relu_s[:, k % 2, :], s_dup, ACT.Relu, bias=b1p[:, k:k + 1],
                                   scale=w1p[:, k:k + 1]).then_inc(relu_done.sem, 1)
                xT_his(b, 3, False)
                for i in range(IB):
                    act.wait_ge(lat_full.sem, lat_full.at(b, i + 1))
                    act.activation(latT[0][:, i * NB:(i + 1) * NB], bank[i][0:LATENT, :], ACT.Identity,
                                   bias=bl[:]).then_inc(lat_hi_done.sem, 1)
                for m in range(KC):
                    for k in (2 * m, 2 * m + 1):
                        i = k % IB
                        act.wait_ge(k1_full.sem, k1_full.at(b, k + 1))
                        act.activation(kT_hi[:, m, i * NB:(i + 1) * NB], bank[4 + k][:], ACT.Identity,
                                       bias=bk[:, m:m + 1]).then_inc(k1_hi_done.sem, 1)
                    for k in (2 * m, 2 * m + 1):
                        i = k % IB
                        act.wait_ge(q1_full.sem, q1_full.at(b, k + 1))
                        act.activation(qT_hi[:, m, i * NB:(i + 1) * NB], bank[k][:], ACT.Identity,
                                       bias=bq[:, m:m + 1]).then_inc(q1_hi_done.sem, 1)

                act.wait_ge(m_cleared.sem, m_cleared.at(b, 0))
                act.wait_ge(q1_lo_done.sem, q1_lo_done.at(b, 2))
                load_q(act, 0)
                act.wait_ge(q1_lo_done.sem, q1_lo_done.at(b, 4))
                load_q(act, 2)

                for g in (2, 3):
                    words = late_words[g]
                    act.activation(words[0:HALF, :], zero_cell[0:HALF, :].to_broadcast([HALF, 2048]),
                                   ACT.Copy).then_inc(late_slots_ready.sem, 1)
                    act.activation(words[HALF + 32:P, :].rearrange("p (h n) -> p h n", h=GH),
                                   max_rows[HALF + 32:P, :].unsqueeze(2).to_broadcast([32, GH, 512]),
                                   ACT.Copy).then_inc(late_slots_ready.sem, 1)

                def maxima_to_rows(u):
                    act.wait_ge(mT_full.sem, mT_full.at(b, u + 1))
                    if u:
                        act.wait_ge(m_loaded.sem, m_loaded.at(b, 16 * u))
                    act.activation(mT[:], bank[5][:].bitcast(F16)[0:2 * GH, 0:NB], ACT.Copy)\
                        .then_inc(mT_done.sem, 1)

                def out_of_unit(u):
                    g, ib = divmod(u, IB)
                    act.wait_ge(av_done.sem, av_done.at(b, BURSTS * (u + 1)))
                    if u == 0:
                        for slot in range(2):
                            act.wait_ge(q_loaded[slot].sem, q_loaded[slot].at(b, 16 * 2 * 3 * GH))
                        for q in range(GROUPS):
                            act.wait_ge(k_loaded[q].sem, k_loaded[q].at(b, 16 * 3 * GH))
                    act.activation(oT[:, g, ib * NB:(ib + 1) * NB], bank[6 + ib][:], ACT.Copy)\
                        .then_inc(o_done.sem, 1)

                maxima_to_rows(0)
                act.wait_ge(mT_done.sem, mT_done.at(b, 1))
                load_maxima(act, 0)
                for n in range(UNITS * BURSTS):
                    u, r = divmod(n, BURSTS)
                    if r == BURSTS - 2 and u + 1 < UNITS:
                        maxima_to_rows(u + 1)
                    for hh in range(GH):
                        tile = n * GH + hh
                        act.wait_ge(cols_full.sem, cols_full.at(b, tile + 1))
                        if n >= 2 and hh == 0:
                            act.wait_ge(av_done.sem, av_done.at(b, n - 1))
                        act.activation(probs[:, tile % P_SLOTS, :], bank[2 + tile % 3][:], ACT.Exp,
                                       scale=SCALE).then_inc(exp_done.sem, 1)
                    if r == 0 and u:
                        out_of_unit(u - 1)
                out_of_unit(UNITS - 1)
                xT_his(b, 4, False)
                act.wait_ge(route_step.sem, route_step.at(b, ROUTE_Z))
                act.activation(rt[:, 1], rt[:, 0], ACT.Exp, scale=-1.0).then_inc(route_exp.sem, 1)
                act.wait_ge(route_step.sem, route_step.at(b, ROUTE_DIST))
                act.activation(rt[:, 6], rt[:, 5], ACT.Exp, scale=-1.0 / 0.1).then_inc(route_exp.sem, 1)
                act.activation(rt[:, 7], rt[:, 5], ACT.Exp, scale=-1.0 / 0.3).then_inc(route_exp.sem, 1)
                for j in range(EXPERTS * 4):
                    act.wait_ge(gate_full.sem, gate_full.at(b, j + 1))
                    if j >= 2:
                        act.wait_ge(hmoe_done.sem, hmoe_done.at(b, j - 1))
                    act.activation(silu[:, j % 2, :], bank[4 + 2 * (j % 2)][:], ACT.Silu)\
                        .then_inc(silu_done.sem, 1)

        @block.tensor
        def _(pe):
            pe.wait_ge(lo_split.sem, N_SPLIT)
            pe.wait_ge(consts_made.sem, 1)

            def split_product(out_ap, stationary, moving):
                chunks = stationary[1]
                terms = [(c, ps, pm) for c in range(chunks) for ps, pm in ((0, 0), (1, 0), (0, 1))]
                for k, (c, ps, pm) in enumerate(terms):
                    last = pe.matmul(out_ap, stationary[0](ps, c), moving(pm, c),
                                     start=(k == 0), stop=(k == len(terms) - 1))
                return last

            def transposes(b, norm, n):
                for k in range(4):
                    i, c = divmod(k, KC)
                    pe.wait_ge(norm_done.sem, norm_done.at(b, norm * TT + 4 * (i + 1)))
                    for t in range(4):
                        last = pe.transpose(bank[XT_BANK[n] + k][:, t * P:(t + 1) * P],
                                            n_tok[:, 4 * i + t, c * P:(c + 1) * P], ident[:])
                    last.then_inc(xT_full.sem, 1)

            def cols(w, lo, hi):
                return (lambda part, c: w[part][:, c, lo:hi], KC)

            def x_cols(lo, hi):
                return lambda part, c: xT[part][:, c, lo:hi]

            with pe.Fori(0, BATCH) as b:
                transposes(b, 1, 0)
                for t in range(TT):
                    pe.wait_ge(xT_lo_done.sem, xT_lo_done.at(b, 2 * (t // 4 + 1)))
                    if t >= 4:
                        pe.wait_ge(kv_done.sem, kv_done.at(b, t - 3))
                    split_product(bank[4 + t % 4][:],
                                  (lambda part, c: xT[part][:, c, t * P:(t + 1) * P], KC),
                                  lambda part, c: wkv0[part][:, c, :]).then_inc(kv_full.sem, 1)
                for k in range(4):
                    m, i = divmod(k, IB)
                    split_product(bank[k][:], cols(wq0, m * P, (m + 1) * P),
                                  x_cols(i * NB, (i + 1) * NB)).then_inc(q_full.sem, 1)
                pe.wait_ge(kv_done.sem, kv_done.at(b, TT))
                for m in range(KC):
                    for t in range(TT):
                        pe.matmul(bank[4 + m][:, 0:P], kv_tok[:, t, m * P:(m + 1) * P],
                                  kv_tok[:, t, D + m * P:D + (m + 1) * P], start=(t == 0), stop=(t == TT - 1))
                    for t in range(TT):
                        last = pe.matmul(bank[4 + m][:, P:2 * P], kv_tok[:, t, m * P:(m + 1) * P],
                                         ones_tok[:], start=(t == 0), stop=(t == TT - 1))
                    last.then_inc(kvs_full.sem, 1)
                for k in range(4):
                    m, i = divmod(k, IB)
                    pe.wait_ge(kvs_done.sem, kvs_done.at(b, m + 1))
                    pe.wait_ge(q_done.sem, q_done.at(b, 4 if k == 0 else k + 1))
                    if k >= 2:
                        pe.wait_ge(att0_done.sem, att0_done.at(b, k - 1))
                    for part in range(2):
                        last = pe.matmul(bank[2 * (k % 2) + part][:], kvsB[:, m, part, :],
                                         qpT[:, m, i * NB:(i + 1) * NB], start=True, stop=True)
                    last.then_inc(numden_full.sem, 1)
                pe.wait_ge(att0_done.sem, att0_done.at(b, 4))
                for tp in range(4):
                    for t in range(2):
                        for c in range(KC):
                            at = (2 * tp + t) * P
                            last = pe.matmul(bank[4 + tp][:, t * D:(t + 1) * D], attT0[:, c, at:at + P],
                                             wo0[:, c, :], start=(c == 0), stop=(c == KC - 1))
                    last.then_inc(wo_full.sem, 1)
                transposes(b, 2, 1)
                pe.wait_ge(add1_done.sem, add1_done.at(b, 4))
                for i in range(IB):
                    pe.wait_ge(xT_lo_done.sem, xT_lo_done.at(b, 8))
                    for f in range(FT):
                        n = i * FT + f
                        if n >= 4:
                            pe.wait_ge(h_done.sem, h_done.at(b, n - 3))
                        split_product(bank[4 + f % 4][:], cols(w1, f * P, (f + 1) * P),
                                      x_cols(i * NB, (i + 1) * NB)).then_inc(h_full.sem, 1)
                    pe.wait_ge(h_done.sem, h_done.at(b, (i + 1) * FT))
                    for tp in range(2):
                        for t in range(2):
                            for f in range(FT):
                                at = (2 * tp + t) * P
                                last = pe.matmul(bank[2 * i + tp][:, t * D:(t + 1) * D], h_ff[:, f, at:at + P],
                                                 w2[:, f, :], start=(f == 0), stop=(f == FT - 1))
                        last.then_inc(w2_full.sem, 1)
                pe.wait_ge(t1_done.sem, t1_done.at(b, 4))
                transposes(b, 3, 2)
                for i in range(IB):
                    pe.wait_ge(xT_lo_done.sem, xT_lo_done.at(b, 8 + 2 * (i + 1)))
                    split_product(bank[4 + i][:], cols(win, 0, 2 * M0),
                                  x_cols(i * NB, (i + 1) * NB)).then_inc(s_full.sem, 1)
                pe.wait_ge(g_done.sem, g_done.at(b, PAIRS))
                for tp in range(4):
                    for t in range(2):
                        at = (2 * tp + t) * P
                        last = pe.matmul(bank[tp][:, t * D:(t + 1) * D], g_acc[:, at:at + P], wout[:],
                                         start=True, stop=True)
                    last.then_inc(fo_full.sem, 1)
                transposes(b, 4, 3)
                pe.wait_ge(x2_done.sem, x2_done.at(b, 4))
                for i in range(IB):
                    pe.wait_ge(xT_lo_done.sem, xT_lo_done.at(b, 12 + 2 * (i + 1)))
                    split_product(bank[i][0:LATENT, :], (lambda part, c: wl[part][:, c, :], KC),
                                  x_cols(i * NB, (i + 1) * NB)).then_inc(lat_full.sem, 1)
                pe.wait_ge(lat_lo_done.sem, lat_lo_done.at(b, 2))
                for m in range(KC):
                    for i in range(IB):
                        split_product(bank[4 + 2 * m + i][:], (lambda part, c: wk1[part][:, m * P:(m + 1) * P], 1),
                                      lambda part, c: latT[part][:, i * NB:(i + 1) * NB]).then_inc(k1_full.sem, 1)
                    for i in range(IB):
                        split_product(bank[2 * m + i][:], cols(wq1, m * P, (m + 1) * P),
                                      x_cols(i * NB, (i + 1) * NB)).then_inc(q1_full.sem, 1)
                for tp in range(4):
                    pe.wait_ge(k1_lo_done.sem, k1_lo_done.at(b, tp + 1))
                    for t in range(2):
                        at = (2 * tp + t) * P
                        last = split_product(bank[4 + tp][:, t * D:(t + 1) * D],
                                             (lambda part, c: latT[part][:, at:at + P], 1),
                                             lambda part, c: wv1[part][:])
                    last.then_inc(v1_full.sem, 1)
                pe.wait_ge(q1_lo_done.sem, q1_lo_done.at(b, 4))
                pe.wait_ge(v1_done.sem, v1_done.at(b, 4))
                pe.wait_ge(v_ones_done.sem, v_ones_done.at(b, 1))

                def row_tile(n):
                    u, r = divmod(n, MAX_TILES)
                    g, ib = divmod(u, IB)
                    it, hh, jb = (TT // IB) * ib + r // (GH * IB), (r // IB) % GH, r % IB
                    if r == 0 and ib == 0:
                        pe.wait_ge(q_loaded[g % 2].sem, q_loaded[g % 2].at(b, 16 * 2 * 3 * GH))
                        pe.wait_ge(k_loaded[g].sem, k_loaded[g].at(b, 16 * 3 * GH))
                    if n >= 2:
                        pe.wait_ge(rows_max_done.sem, rows_max_done.at(b, n - 1))
                    pe.matmul(bank[n % 2][:], qs[:, g % 2, hh, it * P:(it + 1) * P],
                              k_stack[g][:, hh, jb * NB:(jb + 1) * NB],
                              start=True, stop=True).then_inc(rows_full.sem, 1)

                def maxima(u):
                    pe.wait_ge(m16_done.sem, m16_done.at(b, u + 1))
                    if u:
                        pe.wait_ge(mT_done.sem, mT_done.at(b, u))
                    for it in range(TT // IB):
                        last = pe.transpose(bank[5][:].bitcast(F16)[0:2 * GH, it * P:(it + 1) * P],
                                            m16[:, it].rearrange("p h s -> p (h s)"), ident16[:])
                    last.then_inc(mT_full.sem, 1)

                def column_tile(n, hh):
                    u, jt = divmod(n, BURSTS)
                    g, ib = divmod(u, IB)
                    tile = n * GH + hh
                    if tile >= 3:
                        pe.wait_ge(exp_done.sem, exp_done.at(b, tile - 2))
                    pe.matmul(bank[2 + tile % 3][:], k_stack[g][:, hh, jt * P:(jt + 1) * P],
                              qs[:, g % 2, hh, ib * NB:(ib + 1) * NB],
                              start=True, stop=True).then_inc(cols_full.sem, 1)

                def values(n):
                    u, jt = divmod(n, BURSTS)
                    g, ib = divmod(u, IB)
                    if jt == 0 and u >= 2:
                        pe.wait_ge(o_done.sem, o_done.at(b, u - 1))
                    pe.wait_ge(exp_done.sem, exp_done.at(b, (n + 1) * GH))
                    for hh in range(GH):
                        last = pe.matmul(bank[6 + ib][32 * hh:32 * hh + 32, :], v_aug[:, jt, GH * g + hh, :],
                                         probs[:, (n * GH + hh) % P_SLOTS, :], start=(jt == 0),
                                         stop=(jt == TT - 1))
                    last.then_inc(av_done.sem, 1)

                pe.wait_ge(m_cleared.sem, m_cleared.at(b, 0))
                for n in range(AHEAD):
                    row_tile(n)
                    if n == MAX_TILES + 5:
                        maxima(0)
                for n in range(UNITS * BURSTS):
                    u, r = divmod(n, BURSTS)
                    if r == 0:
                        pe.wait_ge(m_loaded.sem, m_loaded.at(b, 16 * (u + 1)))
                    if r == BURSTS - 2 and u + 1 < UNITS:
                        maxima(u + 1)
                    for hh in range(GH):
                        column_tile(n, hh)
                        if AHEAD + 4 * n + hh < UNITS * MAX_TILES:
                            row_tile(AHEAD + 4 * n + hh)
                    if n:
                        values(n - 1)
                values(UNITS * BURSTS - 1)
                pe.wait_ge(rows_max_done.sem, rows_max_done.at(b, UNITS * MAX_TILES))
                pe.wait_ge(exp_done.sem, exp_done.at(b, UNITS * BURSTS * GH))
                pe.wait_ge(att1_done.sem, att1_done.at(b, UNITS))
                for tp in range(4):
                    for t in range(2):
                        for g in range(GROUPS):
                            at = (2 * tp + t) * P
                            last = pe.matmul(bank[tp][:, t * D:(t + 1) * D], oT[:, g, at:at + P], wo1[:, g, :],
                                             start=(g == 0), stop=(g == GROUPS - 1))
                    last.then_inc(o1_full.sem, 1)
                transposes(b, 5, 4)
                pe.wait_ge(x3_done.sem, x3_done.at(b, 4))
                for t in range(TT):
                    pe.wait_ge(xT_lo_done.sem, xT_lo_done.at(b, 16 + 2 * (t // 4 + 1)))
                    last = split_product(bank[0][:, t * EXPERTS:(t + 1) * EXPERTS],
                                         (lambda part, c: xT[part][:, c, t * P:(t + 1) * P], KC),
                                         lambda part, c: wr[part][:, c, :])
                last.then_inc(route_full.sem, 1)

                def gate_up(e):
                    for k in range(4):
                        m, i = divmod(k, IB)
                        j = 4 * e + k
                        if j >= 2:
                            pe.wait_ge(hmoe_done.sem, hmoe_done.at(b, j - 1))
                        for w, at, sig in ((wg, 4, gate_full), (wu, 5, up_full)):
                            split_product(bank[at + 2 * (j % 2)][:],
                                          (lambda part, c: w[part][:, e, c, m * P:(m + 1) * P], KC),
                                          x_cols(i * NB, (i + 1) * NB)).then_inc(sig.sem, 1)

                def down(e):
                    pe.wait_ge(hmoe_done.sem, hmoe_done.at(b, 4 * e + 4))
                    for tp in range(4):
                        if e:
                            pe.wait_ge(moe_done.sem, moe_done.at(b, (e - 1) * TT + 2 * tp + 2))
                        elif tp == 0:
                            pe.wait_ge(route_step.sem, route_step.at(b, ROUTE_Z))
                        for t in range(2):
                            for m in range(ET):
                                at = (2 * tp + t) * P
                                last = pe.matmul(bank[tp][:, t * D:(t + 1) * D],
                                                 h_moe[:, e % 2, m, at:at + P], wd[:, e, m, :],
                                                 start=(m == 0), stop=(m == ET - 1))
                        last.then_inc(down_full.sem, 1)

                gate_up(0)
                for e in range(1, EXPERTS):
                    gate_up(e)
                    down(e - 1)
                down(EXPERTS - 1)

        @block.vector
        def _(dve):
            dve.wait_ge(consts_made.sem, 1)
            for k, (_, staged, (hi, lo)) in enumerate(split_plan):
                dve.wait_ge(hi_split.sem, k + 1)
                dve.tensor_tensor(lo[:], staged, hi[:], ALU.subtract).then_inc(lo_split.sem, 1)
            dve.memset(wait_cell[:, 1:2], 0.0).then_inc(moe_done.sem, moe_done.at_start)
            dve.memset(wait_cell[:, 2:3], 0.0).then_inc(stored.sem, stored.at_start)
            dve.memset(wait_cell[:, 3:4], 0.0).then_inc(m_cleared.sem, m_cleared.at_start)
            dve.reciprocal(rtemp[:], temp_all[:]).then_inc(setup_step.sem, 1)
            dve.wait_ge(lo_split.sem, N_SPLIT)
            dve.wait_ge(setup_step.sem, 25)

            def carry_wait():
                dve.memset(wait_cell[:, 0:1], 0.0)

            def norm(b, n, src, dst, ready, per_tile):
                for s in range(2):
                    half = range(s * TT // 2, (s + 1) * TT // 2)
                    for t in half:
                        dve.wait_ge(ready.sem, ready.at(b, math.ceil((t + 1) * per_tile)))
                        dve.bn_stats(bn[:, t, :], src[:, t, :]).then_inc(bn_done.sem, 1)
                    dve.wait_ge(bn_done.sem, bn_done.at(b, n * TT + half[-1] + 1))
                    carry_wait()
                    for t in half:
                        dve.bn_aggr(mv[:, t, :], bn[:, t, :]).then_inc(stats_done.sem, 1)
                for t in range(TT):
                    if t % 4 == 0:
                        dve.wait_ge(rstd_done.sem, rstd_done.at(b, n * 2 + t // 4 + 1))
                    dve.tensor_scalar(dst[:, t, :], src[:, t, :], mv[:, t, 0:1], rstd[:, t:t + 1],
                                      ALU.subtract, ALU.mult).then_inc(norm_done.sem, 1)

            def xT_los(b, n, affine):
                for k in range(4):
                    i, c = divmod(k, KC)
                    src = bank[XT_BANK[n] + k][:]
                    at = slice(i * NB, (i + 1) * NB)
                    dve.wait_ge(xT_hi_done.sem, xT_hi_done.at(b, 4 * n + k + 1))
                    if affine:
                        if k >= 2:
                            dve.wait_ge(xT_lo_done.sem, xT_lo_done.at(b, 4 * n + k - 1))
                        dve.tensor_scalar(gtmp[:, k % 2, :], src, gamma[:, c:c + 1], beta[:, c:c + 1],
                                          ALU.mult, ALU.add).then_inc(xT_affine.sem, 1)
                        dve.wait_ge(xT_affine.sem, xT_affine.at(b, 4 * n + k + 1))
                        src = gtmp[:, k % 2, :]
                    dve.tensor_tensor(xT[1][:, c, at], src, xT[0][:, c, at], ALU.subtract)\
                       .then_inc(xT_lo_done.sem, 1)

            with dve.Fori(0, BATCH) as b:
                dve.wait_ge(x_loaded.sem, x_loaded.at(b, 32))
                norm(b, 0, x_tok, y_tok, x_loaded, 4)
                norm(b, 1, y_tok, n_tok, norm_done, 1)
                xT_los(b, 0, True)
                for t in range(TT):
                    dve.wait_ge(kv_full.sem, kv_full.at(b, t + 1))
                    dve.tensor_scalar(kv_tok[:, t, 0:D], bank[4 + t % 4][:, 0:D], 0.0, 1e-3, ALU.max, ALU.add)
                    dve.tensor_copy(kv_tok[:, t, D:2 * D], bank[4 + t % 4][:, D:2 * D]).then_inc(kv_done.sem, 1)
                dve.wait_ge(stored.sem, stored.at(b, 0))
                for k in range(4):
                    m, i = divmod(k, IB)
                    dve.wait_ge(q_full.sem, q_full.at(b, k + 1))
                    dve.tensor_scalar(qpT[:, m, i * NB:(i + 1) * NB], bank[k][:], 0.0, 1e-3, ALU.max, ALU.add)\
                       .then_inc(q_done.sem, 1)
                for m in range(KC):
                    dve.wait_ge(kvs_full.sem, kvs_full.at(b, m + 1))
                    dve.tensor_tensor(kvsB[:, m], bank[4 + m][:, 0:2 * P].rearrange("p (a n) -> p a n", a=2),
                                      head_mask[:], ALU.mult).then_inc(kvs_done.sem, 1)
                for k in range(4):
                    m, i = divmod(k, IB)
                    dve.wait_ge(numden_full.sem, numden_full.at(b, k + 1))
                    if k >= 2:
                        dve.wait_ge(att0_done.sem, att0_done.at(b, k - 1))
                    dve.reciprocal(den0[:, k % 2, :], bank[2 * (k % 2) + 1][:]).then_inc(rden_done.sem, 1)
                    dve.wait_ge(rden_done.sem, rden_done.at(b, k + 1))
                    dve.tensor_tensor(attT0[:, m, i * NB:(i + 1) * NB], bank[2 * (k % 2)][:],
                                      den0[:, k % 2, :], ALU.mult).then_inc(att0_done.sem, 1)
                for tp in range(4):
                    dve.wait_ge(wo_full.sem, wo_full.at(b, tp + 1))
                    dve.tensor_tensor(add1[:, 2 * tp:2 * tp + 2, :],
                                      bank[4 + tp][:].rearrange("p (t d) -> p t d", d=D),
                                      y_tok[:, 2 * tp:2 * tp + 2, :], ALU.add).then_inc(add1_done.sem, 1)
                norm(b, 2, add1, n_tok, add1_done, 0.5)
                xT_los(b, 1, True)
                for n in range(4):
                    dve.wait_ge(w2_full.sem, w2_full.at(b, n + 1))
                    dve.tensor_tensor(t1[:, 2 * n:2 * n + 2, :], bank[n][:].rearrange("p (t d) -> p t d", d=D),
                                      b2_all[:].unsqueeze(1).to_broadcast([P, 2, D]), ALU.add)\
                       .then_inc(t1_done.sem, 1)
                dve.wait_ge(x_add1_done.sem, x_add1_done.at(b, 1))
                for n in range(4):
                    pair = slice(2 * n, 2 * n + 2)
                    dve.wait_ge(gelu_done.sem, gelu_done.at(b, n + 1))
                    dve.tensor_tensor(x_tok[:, pair, :], x_tok[:, pair, :], t1[:, pair, :], ALU.add)\
                       .then_inc(x1_done.sem, 1)
                norm(b, 3, x_tok, n_tok, x1_done, 0.5)
                xT_los(b, 2, False)
                for k in range(PAIRS):
                    dve.wait_ge(relu_done.sem, relu_done.at(b, k + 1))
                    if k == 0:
                        dve.tensor_scalar(g_acc, relu_s[:, 0, :], w2p[:, 0:1], b2p[:], ALU.mult, ALU.add)\
                           .then_inc(g_done.sem, 1)
                        continue
                    dve.wait_ge(g_done.sem, g_done.at(b, k))
                    dve.scalar_tensor_tensor(out=g_acc, in0=relu_s[:, k % 2, :], scalar=w2p[:, k:k + 1],
                                             in1=g_acc, op0=ALU.mult, op1=ALU.add).then_inc(g_done.sem, 1)
                dve.wait_ge(x_bout_done.sem, x_bout_done.at(b, 1))
                for tp in range(4):
                    pair = slice(2 * tp, 2 * tp + 2)
                    dve.wait_ge(fo_full.sem, fo_full.at(b, tp + 1))
                    dve.tensor_tensor(x_tok[:, pair, :], bank[tp][:].rearrange("p (t d) -> p t d", d=D),
                                      x_tok[:, pair, :], ALU.add).then_inc(x2_done.sem, 1)
                norm(b, 4, x_tok, n_tok, x2_done, 0.5)
                xT_los(b, 3, False)
                for i in range(IB):
                    at = slice(i * NB, (i + 1) * NB)
                    dve.wait_ge(lat_hi_done.sem, lat_hi_done.at(b, i + 1))
                    dve.scalar_tensor_tensor(out=latT[1][:, at], in0=bank[i][0:LATENT, :], scalar=bl[:],
                                             in1=latT[0][:, at], op0=ALU.add, op1=ALU.subtract)\
                       .then_inc(lat_lo_done.sem, 1)
                for m, (hi, lo, bias, first, hi_done, lo_done) in [
                        (m, x) for m in range(KC) for x in ((kT_hi, kT_lo, bk, 4, k1_hi_done, k1_lo_done),
                                                            (qT_hi, qT_lo, bq, 0, q1_hi_done, q1_lo_done))]:
                    for i in range(IB):
                        k = 2 * m + i
                        at = slice(i * NB, (i + 1) * NB)
                        dve.wait_ge(hi_done.sem, hi_done.at(b, k + 1))
                        dve.scalar_tensor_tensor(out=lo[:, m, at], in0=bank[first + k][:], scalar=bias[:, m:m + 1],
                                                 in1=hi[:, m, at], op0=ALU.add, op1=ALU.subtract)\
                           .then_inc(lo_done.sem, 1)
                for tp in range(4):
                    dve.wait_ge(v1_full.sem, v1_full.at(b, tp + 1))
                    dve.tensor_tensor(v_aug[:, 2 * tp:2 * tp + 2, :, 0:DH],
                                      bank[4 + tp][:].rearrange("p (t h c) -> p t h c", t=2, c=DH),
                                      bv_all[:].rearrange("p (h c) -> p h c", c=DH).unsqueeze(1)
                                      .to_broadcast([P, 2, HEADS, DH]), ALU.add).then_inc(v1_done.sem, 1)

                def unit_maxima(u):
                    dve.wait_ge(rows_max_done.sem, rows_max_done.at(b, MAX_TILES * (u + 1)))
                    if u:
                        dve.wait_ge(mT_full.sem, mT_full.at(b, u))
                    dve.tensor_reduce(head_max[:], row_max[:, u % 2], AX_X, ALU.max).then_inc(max_step.sem, 1)
                    dve.wait_ge(max_step.sem, max_step.at(b, 2 * u + 1))
                    dve.tensor_scalar(m16[:, :, :, 0], head_max[:], -1.0 / MAX_UNIT, None, ALU.mult)\
                       .then_inc(max_step.sem, 1)
                    dve.wait_ge(max_step.sem, max_step.at(b, 2 * u + 2))
                    dve.scalar_tensor_tensor(out=m16[:, :, :, 1], in0=head_max[:], scalar=-1.0 / MAX_UNIT,
                                             in1=m16[:, :, :, 0], op0=ALU.mult, op1=ALU.subtract)\
                       .then_inc(m16_done.sem, 1)

                def normalise(u):
                    g, ib = divmod(u, IB)
                    o = oT[:, g, ib * NB:(ib + 1) * NB]
                    dve.wait_ge(o_done.sem, o_done.at(b, u + 1))
                    if u:
                        dve.wait_ge(att1_done.sem, att1_done.at(b, u))
                    carry_wait()
                    dve.stream_shuffle(den1[:, 0, :], o, mask=[DH] * 32).then_inc(den_step.sem, 1)
                    dve.wait_ge(den_step.sem, den_step.at(b, 2 * u + 1))
                    dve.reciprocal(den1[:, 1, :], den1[:, 0, :]).then_inc(den_step.sem, 1)
                    dve.wait_ge(den_step.sem, den_step.at(b, 2 * u + 2))
                    dve.tensor_tensor(o, o, den1[:, 1, :], ALU.mult).then_inc(att1_done.sem, 1)

                for n in range(UNITS * MAX_TILES):
                    u, r = divmod(n, MAX_TILES)
                    it, hh, jb = r // (GH * IB), (r // IB) % GH, r % IB
                    dve.wait_ge(rows_full.sem, rows_full.at(b, n + 1))
                    if r == 0 and u >= 2:
                        dve.wait_ge(m16_done.sem, m16_done.at(b, u - 1))
                    dve.tensor_reduce(row_max[:, u % 2, it, hh, jb:jb + 1], bank[n % 2][:], AX_X, ALU.max)\
                       .then_inc(rows_max_done.sem, 1)
                    if r == MAX_TILES - 1:
                        unit_maxima(u)
                for u in range(UNITS):
                    normalise(u)
                for tp in range(4):
                    pair = slice(2 * tp, 2 * tp + 2)
                    dve.wait_ge(o1_full.sem, o1_full.at(b, tp + 1))
                    dve.tensor_tensor(x_tok[:, pair, :], bank[tp][:].rearrange("p (t d) -> p t d", d=D),
                                      x_tok[:, pair, :], ALU.add).then_inc(x3_done.sem, 1)
                norm(b, 5, x_tok, n_tok, x3_done, 0.5)
                xT_los(b, 4, False)
                steps = 0

                def step(instruction):
                    nonlocal steps
                    steps += 1
                    instruction.then_inc(route_step.sem, 1)
                    dve.wait_ge(route_step.sem, route_step.at(b, steps))

                def per_expert(v):
                    return v.unsqueeze(2).to_broadcast([P, TT, EXPERTS])

                z, inh, zone, low, dist, w, fb = rt[:, 0], rt[:, 2], rt[:, 3], rt[:, 4], rt[:, 5], rt[:, 6], rt[:, 7]
                rank, chosen, none, rsum = rt[:, 8], rt[:, 9], rt1[:, 0], rt1[:, 1]
                dve.wait_ge(route_full.sem, route_full.at(b, 1))
                step(dve.tensor_scalar(z, bank[0][:, 0:TT * EXPERTS].rearrange("p (t e) -> p t e", e=EXPERTS),
                                       rtemp[:], None, ALU.mult))
                assert steps == ROUTE_Z
                dve.wait_ge(route_exp.sem, route_exp.at(b, 1))
                step(dve.tensor_scalar(rt[:, 10], rt[:, 1], 1.0, None, ALU.add))
                step(dve.reciprocal(inh, rt[:, 10]))
                step(dve.tensor_scalar(low, inh, ZONE_LOWER, None, ALU.is_ge))
                step(dve.scalar_tensor_tensor(out=zone, in0=inh, scalar=ZONE_UPPER, in1=low,
                                              op0=ALU.is_le, op1=ALU.mult))
                step(dve.tensor_scalar(rt[:, 11], inh, ZONE_CENTER, None, ALU.subtract))
                step(dve.scalar_tensor_tensor(out=dist, in0=rt[:, 11], scalar=-1.0, in1=rt[:, 11],
                                              op0=ALU.mult, op1=ALU.max))
                assert steps == ROUTE_DIST
                dve.wait_ge(route_exp.sem, route_exp.at(b, 3))
                step(dve.tensor_tensor(rt[:, 10], w, zone, ALU.mult))
                step(dve.tensor_reduce(rsum, rt[:, 10], AX_X, ALU.add))
                step(dve.tensor_scalar(none, rsum, 1e-8, None, ALU.is_lt))
                ahead, equal = pairs
                mine = fb.unsqueeze(3).to_broadcast([P, TT, EXPERTS, EXPERTS])
                other = fb.unsqueeze(2).to_broadcast([P, TT, EXPERTS, EXPERTS])
                step(dve.tensor_tensor(ahead, other, mine, ALU.is_gt))
                step(dve.tensor_tensor(equal, other, mine, ALU.is_equal))
                step(dve.tensor_tensor(equal, equal, before[:].unsqueeze(1).to_broadcast(
                    [P, TT, EXPERTS, EXPERTS]), ALU.mult))
                step(dve.tensor_tensor(ahead, ahead, equal, ALU.add))
                step(dve.tensor_reduce(rank, ahead, AX_X, ALU.add))
                step(dve.scalar_tensor_tensor(out=chosen, in0=rank, scalar=2.0, in1=fb,
                                              op0=ALU.is_lt, op1=ALU.mult))
                step(dve.tensor_reduce(rt1[:, 2], chosen, AX_X, ALU.add))
                step(dve.tensor_scalar(rt1[:, 3], rt1[:, 2], 1e-8, None, ALU.max))
                step(dve.reciprocal(rt1[:, 4], rt1[:, 3]))
                step(dve.tensor_tensor(chosen, chosen, per_expert(rt1[:, 4]), ALU.mult))
                step(dve.tensor_tensor(chosen, chosen, per_expert(none), ALU.mult))
                step(dve.tensor_scalar(rt1[:, 5], none, -1.0, 1.0, ALU.mult, ALU.add))
                step(dve.tensor_tensor(rt[:, 11], rt[:, 10], per_expert(rt1[:, 5]), ALU.mult))
                step(dve.tensor_tensor(rt[:, 11], rt[:, 11], chosen, ALU.add))
                step(dve.tensor_reduce(rt1[:, 2], rt[:, 11], AX_X, ALU.add))
                step(dve.tensor_scalar(rt1[:, 3], rt1[:, 2], 1e-8, None, ALU.max))
                step(dve.reciprocal(rt1[:, 4], rt1[:, 3]))
                step(dve.tensor_tensor(rt[:, 10], rt[:, 11], per_expert(rt1[:, 4]), ALU.mult))
                route_w = rt[:, 10]
                assert steps == ROUTE_STEPS, steps

                def hidden(e):
                    for k in range(4):
                        m, i = divmod(k, IB)
                        j = 4 * e + k
                        dve.wait_ge(silu_done.sem, silu_done.at(b, j + 1))
                        dve.wait_ge(up_full.sem, up_full.at(b, j + 1))
                        dve.tensor_tensor(h_moe[:, e % 2, m, i * NB:(i + 1) * NB], silu[:, j % 2, :],
                                          bank[5 + 2 * (j % 2)][:], ALU.mult).then_inc(hmoe_done.sem, 1)

                def weigh(e):
                    for t in range(TT):
                        if t % 2 == 0:
                            dve.wait_ge(down_full.sem, down_full.at(b, 4 * e + t // 2 + 1))
                        if e:
                            dve.wait_ge(moe_done.sem, moe_done.at(b, (e - 1) * TT + t + 1))
                        dve.scalar_tensor_tensor(out=moe_acc[:, t, :], in0=bank[t // 2][:, (t % 2) * D:(t % 2 + 1) * D],
                                                 scalar=route_w[:, t, e:e + 1],
                                                 in1=(moe_acc if e else x_tok)[:, t, :],
                                                 op0=ALU.mult, op1=ALU.add).then_inc(moe_done.sem, 1)

                hidden(0)
                for e in range(1, EXPERTS):
                    hidden(e)
                    weigh(e - 1)
                weigh(EXPERTS - 1)


XT_BANK = [0, 0, 0, 4, 4]
ROUTE_Z = 1
ROUTE_DIST = 7

_INS = ['L0_attn_x', 'L0_attn_gamma1', 'L0_attn_beta1', 'L0_attn_wq', 'L0_attn_wk', 'L0_attn_wv', 'L0_attn_wo',
        'L0_attn_w1', 'L0_attn_b1', 'L0_attn_w2', 'L0_attn_b2', 'L0_ffn_Win', 'L0_ffn_bin_', 'L0_ffn_W1',
        'L0_ffn_b1', 'L0_ffn_W2', 'L0_ffn_b2', 'L0_ffn_Wout', 'L0_ffn_bout', 'L1_attn_Wq', 'L1_attn_bq',
        'L1_attn_Wl', 'L1_attn_bl', 'L1_attn_Wk', 'L1_attn_bk', 'L1_attn_Wv', 'L1_attn_bv', 'L1_attn_Wo',
        'L1_attn_bo', 'L1_ffn_Wg', 'L1_ffn_Wu', 'L1_ffn_Wd', 'L1_ffn_Wr', 'L1_ffn_temperature']


def kernel(**inputs):
    import numpy as _np
    import concourse.bacc as _bacc
    from concourse import mybir as _mybir
    from concourse.bass_utils import run_bass_kernel_spmd as _run

    nc = _bacc.Bacc("TRN2", target_bir_lowering=False, num_devices=1)
    arrays, args = {}, {}
    for name in _INS:
        a = _np.ascontiguousarray(inputs[name])
        arrays[f"in_{name}_dram"] = a
        args[name] = nc.dram_tensor(f"in_{name}_dram", a.shape, _mybir.dt.from_np(a.dtype),
                                    kind="ExternalInput").ap()
    out = nc.dram_tensor("out_0_dram", (BATCH, TOKENS, D), F32, kind="ExternalOutput").ap()
    build(nc, args, out)
    r = _run(nc, [arrays], core_ids=[0])
    return r.results[0]["out_0_dram"]
```

```python
import math
import struct
from contextlib import ExitStack

import concourse.bass as bass
from concourse import mybir

ALU = mybir.AluOpType
ACT = mybir.ActivationFunctionType
F32 = mybir.dt.float32
F16 = mybir.dt.float16
AX_X = mybir.AxisListType.X

P = 128
BATCH, TOKENS, D = 8, 1024, 256
TT = TOKENS // P
NB = 512
IB = TOKENS // NB
KC = D // P
HEADS, DH = 16, 16
FF = 1024
FT = FF // P
M0, INNER = 64, 16
PAIRS = INNER // 2
LATENT = 64
EXPERTS, EI = 8, 256
ET = EI // P
GROUPS, GH = 4, 4
HALF = 64
SPLIT_ROWS = 3 * DH
MAX_UNIT = 256.0
PAIR_OF_UNITS = 0x5C005C00
UNITS = GROUPS * IB
P_SLOTS = 8
ROW_BANK = (0, 1, 5)
BURSTS = TT
MAX_TILES = (TT // IB) * GH * IB
AHEAD = MAX_TILES + 5
STREAMED = 1
DIV_AFTER = 3 * MAX_TILES + 4
CATCH_UP = 9
DIV_PARTS = 8
OUT_AFTER = 4
NORM_FFN, NORM_EXPAND, NORM_PROJECT, NORM_ROUTER, NORM_NEXT, NORM_NEXT_LN1, NORMS = range(7)
T_FFN, T_EXPAND, T_PROJECT, T_ROUTER, T_NEXT, T_SETS = range(6)
T_BANK = (0, 0, 4, 0, 4)
T_OF_NORM = {NORM_FFN: T_FFN, NORM_EXPAND: T_EXPAND, NORM_PROJECT: T_PROJECT, NORM_ROUTER: T_ROUTER,
             NORM_NEXT_LN1: T_NEXT}
HT = TT // IB
MH = P // DH
KVS = P + MH
ROUTE_STEPS = 28
SCALE = DH ** -0.5
ZONE_CENTER = 1.0 / math.e
ZONE_LOWER = 0.5 - math.log(4.0 / 3.0)
ZONE_UPPER = 0.5


class Signal:

    def __init__(self, sem, per_batch, at_start=0):
        self.sem, self.per_batch, self.at_start = sem, per_batch, at_start

    def at(self, b, n):
        return b * self.per_batch + self.at_start + n


def build(nc, a, out):
    nc.disable_value_cache = True
    ctx = ExitStack()
    with ctx:
        def sb(name, shape, dt=F32):
            return ctx.enter_context(nc.sbuf_tensor(name, shape, dt))

        def signal(name, per_batch=1, at_start=0):
            return Signal(ctx.enter_context(nc.semaphore(name)), per_batch, at_start)

        def split_weight(name, shape):
            return sb(name + "_hi", shape, F16), sb(name + "_lo", shape, F16)

        wq0 = split_weight("wq0", [P, KC, D])
        wkv0 = split_weight("wkv0", [P, KC, 2 * D])
        w1 = split_weight("w1", [P, KC, FF])
        win = split_weight("win", [P, KC, 2 * M0])
        wl = split_weight("wl", [P, KC, LATENT])
        wq1 = split_weight("wq1", [P, KC, D])
        wk1 = split_weight("wk1", [LATENT, D])
        wv1 = split_weight("wv1", [LATENT, D])
        wr = split_weight("wr", [P, KC, EXPERTS])
        wg = split_weight("wg", [P, EXPERTS, KC, EI])
        wu = split_weight("wu", [P, EXPERTS, KC, EI])
        wo0 = sb("wo0", [P, KC, D])
        w2 = split_weight("w2", [P, FT, D])
        wout = sb("wout", [P, D])
        wo1 = sb("wo1", [P, GROUPS, D])
        wd = split_weight("wd", [P, EXPERTS, ET, D])
        gamma = sb("gamma", [P, KC])
        beta = sb("beta", [P, KC])
        b1 = sb("b1", [P, FT])
        bin2 = sb("bin2", [P, 1])
        w1p = sb("w1p", [P, PAIRS])
        b1p = sb("b1p", [P, PAIRS])
        w2p = sb("w2p", [P, PAIRS])
        b2p = sb("b2p", [P, 1])
        bq = sb("bq", [P, KC])
        bk = sb("bk", [P, KC])
        bl = sb("bl", [LATENT, 1])
        b2_all = sb("b2_all", [P, D])
        bout_all = sb("bout_all", [P, D])
        bv_all = sb("bv_all", [P, D])
        temp_all = sb("temp_all", [P, 1])
        rtemp = sb("rtemp", [P, 1])
        ident = sb("ident", [P, P])
        ident16 = sb("ident16", [P, P], F16)
        head_mask = sb("head_mask", [P, KVS])
        ones_tok = sb("ones_tok", [P, MH])
        before = sb("before", [P, EXPERTS, EXPERTS])
        eps = sb("eps", [P, 2, TT // 2])
        neg_half = sb("neg_half", [P, TT // 2])
        x_tok = sb("x_tok", [P, TT, D])
        r0 = sb("r0", [P, 2 * TT * D])
        r1 = sb("r1", [P, 4096])
        r2 = sb("r2", [P, 4096])
        r3 = sb("r3", [P, 4096])
        xT_both = sb("xT", [P, 2, KC, TOKENS], F16)
        xT = (xT_both[:, 0], xT_both[:, 1])
        qs = sb("q_stack", [P, 2, GH, TOKENS], F16)
        ks = sb("k_stack", [P, 2, GH, TOKENS], F16)
        bn = sb("bn", [P, TT, 6])
        mv = sb("mv", [P, TT, 2])
        var_eps = sb("var_eps", [P, TT])
        rstd = sb("rstd", [P, TT])
        row_max = sb("row_max", [P, 2, TT // IB, GH, IB])
        head_max = sb("head_max", [P, TT // IB, GH])
        m16 = sb("m16", [P, TT // IB, GH, 2], F16)
        mT = sb("mT", [2 * GH, NB], F16)
        max_rows = sb("max_rows", [P, GH])
        zero_cell = sb("zero_cell", [P, 1])
        rt = sb("route", [P, 12, TT, EXPERTS])
        rt1 = sb("route_sums", [P, 6, TT])

        def view(region, start, size, pattern, **kw):
            return region[:, start:start + size].rearrange(pattern, **kw)

        y_tok = view(r0, 0, TT * D, "p (t d) -> p t d", d=D)
        n_tok = view(r0, TT * D, TT * D, "p (t d) -> p t d", d=D)
        probs = view(r0, 0, P_SLOTS * NB, "p (s n) -> p s n", n=NB)
        kv_tok = view(r1, 0, TT * 2 * D, "p (t n) -> p t n", n=2 * D)
        v_aug = view(r1, 0, TT * HEADS * 32, "p (t h c) -> p t h c", h=HEADS, c=32)
        h_ff = [r2[:, 2048 * k:2048 * (k + 1)].bitcast(F16).rearrange("p (f n) -> p f n", n=NB)
                for k in range(2)]
        h_tmp = view(r1, 0, 4 * NB, "p (s n) -> p s n", n=NB)
        attT0 = view(r2, 0, KC * TOKENS, "p (c n) -> p c n", c=KC)
        att_tok = n_tok
        den0 = view(r2, 2048, TT * HEADS, "p (t c h) -> p t c h", c=KC, h=MH)
        gtmp = {T_FFN: view(r0, 0, 2 * NB, "p (s n) -> p s n", n=NB),
                T_NEXT: view(r1, 3072, 2 * NB, "p (s n) -> p s n", n=NB)}
        expand = [view(r0, 0, 4 * NB, "p (s n) -> p s n", n=NB), view(r3, 2048, 4 * NB, "p (s n) -> p s n", n=NB)]
        s_dup = [e[:, 0, :] for e in expand]
        relu_s = [e[:, 1:3, :] for e in expand]
        g_acc = [e[:, 3, :] for e in expand]
        qT_hi, qT_lo, kT_hi, kT_lo = [r3[:, 1024 * k:1024 * (k + 1)].bitcast(F16)
                                      .rearrange("p (c n) -> p c n", c=KC) for k in range(4)]
        latT = [r2[0:LATENT, 512 * k:512 * (k + 1)].bitcast(F16) for k in range(2)]
        den1 = view(r2, 0, 3 * NB, "p (s n) -> p s n", s=3)
        late_words = {2: xT_both[:].bitcast(F32).rearrange("p a c n -> p (a c n)"), 3: r2[:, 2048:4096]}
        k_stack = [ks[:, 0], ks[:, 1]] + [late_words[g].bitcast(F16).rearrange("p (h n) -> p h n", h=GH)
                                          for g in (2, 3)]
        h_moe = [r2[:, 2048 * k:2048 * (k + 1)].bitcast(F16).rearrange("p (s m n) -> p s m n", s=2, m=ET)
                 for k in range(2)]
        qpT = view(r3, 0, KC * TOKENS, "p (c n) -> p c n", c=KC)
        t1 = view(r3, 0, TT * D, "p (t d) -> p t d", d=D)
        add1 = view(r3, 2048, TT * D, "p (t d) -> p t d", d=D)
        oT = view(r3, 0, GROUPS * TOKENS, "p (g n) -> p g n", g=GROUPS)
        moe_acc = view(r3, 0, TT * D, "p (t d) -> p t d", d=D)
        silu = view(r1, 0, 4 * NB, "p (s n) -> p s n", n=NB)
        pairs = [view(r3, 3072 + 512 * k, 512, "p (t e f) -> p t e f", e=EXPERTS, f=EXPERTS)
                 for k in range(2)]
        wait_cell = sb("wait_cell", [P, 4])
        kvsB = view(r3, 2048, KC * KVS, "p (c n) -> p c n", c=KC)

        bank = [ctx.enter_context(nc.psum_tensor(f"bank{k}", [P, NB], F32)) for k in range(8)]

        weights_loaded = signal("weights_loaded")
        hi_split = signal("hi_split")
        lo_split = signal("lo_split")
        setup_step = signal("setup_step")
        consts_made = signal("consts_made")
        x_loaded = signal("x_loaded", 32, at_start=32)
        bn_done = signal("bn_done", NORMS * TT, at_start=2 * TT)
        stats_done = signal("stats_done", NORMS * TT, at_start=2 * TT)
        eps_added = signal("eps_added", NORMS * 2, at_start=2 * 2)
        rstd_done = signal("rstd_done", NORMS * 2, at_start=2 * 2)
        norm_done = signal("norm_done", NORMS * TT, at_start=2 * TT)
        xT_full = signal("xT_full", T_SETS * 4, at_start=4)
        xT_hi_done = signal("xT_hi_done", T_SETS * 4, at_start=4)
        xT_affine = signal("xT_affine", 2 * 4, at_start=4)
        xT_lo_done = signal("xT_lo_done", T_SETS * 4, at_start=4)
        kv_full = signal("kv_full", TT)
        kv_done = signal("kv_done", TT)
        q_full = signal("q_full", 4)
        q_done = signal("q_done", 4)
        kvs_full = signal("kvs_full", KC)
        kvs_done = signal("kvs_done", KC)
        numden_full = signal("numden_full", TT)
        rden_done = signal("rden_done", TT)
        att0_done = signal("att0_done", TT)
        attT0_full = signal("attT0_full", 4)
        attT0_done = signal("attT0_done", 4)
        wo_full = signal("wo_full", 4)
        add1_done = signal("add1_done", 4)
        h_full = signal("h_full", 2 * FT)
        h_done = signal("h_done", 2 * FT)
        h_hi_done = signal("h_hi_done", 2 * FT)
        h_lo_done = signal("h_lo_done", 2 * FT)
        w2_full = signal("w2_full", 4)
        t1_done = signal("t1_done", 4)
        gelu_done = signal("gelu_done", 4)
        x_add1_done = signal("x_add1_done", 1)
        x1_done = signal("x1_done", 4)
        s_full = signal("s_full", 2)
        s_done = signal("s_done", 2)
        relu_done = signal("relu_done", IB * PAIRS)
        g_done = signal("g_done", IB * PAIRS)
        x_bout_done = signal("x_bout_done", IB)
        fo_full = signal("fo_full", 4)
        x2_done = signal("x2_done", 4)
        lat_full = signal("lat_full", 2)
        lat_hi_done = signal("lat_hi_done", 2)
        lat_lo_done = signal("lat_lo_done", 2)
        k1_full = signal("k1_full", 4)
        k1_hi_done = signal("k1_hi_done", 4)
        k1_lo_done = signal("k1_lo_done", 4)
        q1_full = signal("q1_full", 4)
        q1_hi_done = signal("q1_hi_done", 4)
        q1_lo_done = signal("q1_lo_done", 4)
        v1_full = signal("v1_full", 4)
        v1_done = signal("v1_done", 4)
        v_ones_done = signal("v_ones_done", 1)
        late_slots_ready = signal("late_slots_ready", 4)
        head_loaded = [signal(f"head_loaded{hh}", 16 * 2 * 3) for hh in range(GH)]
        q_loaded = [signal(f"q_loaded{g}", 16 * 3 * GH) for g in range(1, GROUPS)]
        k_loaded = [signal(f"k_loaded{g}", 16 * 3 * GH) for g in range(1, GROUPS)]
        rows_full = signal("rows_full", UNITS * MAX_TILES)
        rows_max_done = signal("rows_max_done", UNITS * MAX_TILES)
        max_step = signal("max_step", 2 * UNITS)
        m16_done = signal("m16_done", UNITS)
        mT_full = signal("mT_full", UNITS)
        mT_done = signal("mT_done", UNITS)
        m_loaded = signal("m_loaded", 16 * UNITS)
        m_cleared = signal("m_cleared", 16 * GROUPS, at_start=1)
        cols_full = signal("cols_full", UNITS * BURSTS * GH)
        exp_done = signal("exp_done", UNITS * BURSTS * GH)
        av_done = signal("av_done", UNITS * BURSTS)
        o_done = signal("o_done", UNITS)
        den_step = signal("den_step", (1 + DIV_PARTS) * UNITS)
        att1_done = signal("att1_done", UNITS)
        o1_full = signal("o1_full", 4)
        x3_done = signal("x3_done", 4)
        route_full = signal("route_full", 1)
        route_step = signal("route_step", ROUTE_STEPS)
        route_exp = signal("route_exp", 3)
        gate_full = signal("gate_full", EXPERTS * 4)
        up_full = signal("up_full", EXPERTS * 4)
        silu_done = signal("silu_done", EXPERTS * 4)
        hmoe_done = signal("hmoe_done", EXPERTS * 4)
        hmoe_hi_done = signal("hmoe_hi_done", EXPERTS * 4)
        hmoe_lo_done = signal("hmoe_lo_done", EXPERTS * 4)
        down_full = signal("down_full", EXPERTS * 4)
        moe_done = signal("moe_done", EXPERTS * TT, at_start=1)
        stored = signal("stored", 64, at_start=1)

        def stage(region, start, rows, shape):
            n = math.prod(shape)
            names = "abc"[:len(shape)]
            v = region[0:rows, start:start + n]
            if len(shape) == 1:
                return v
            return v.rearrange(f"p ({' '.join(names)}) -> p {' '.join(names)}", **dict(zip(names, shape)))

        chunk = "(c p) n -> p c n"
        st_kv = stage(r3, 2048, P, [KC, 2 * D])
        st_win = stage(r0, 0, P, [KC, 2 * M0])
        x_tok_flat = x_tok[:].rearrange("p t d -> p (t d)")
        wd_stage = [stage(r0, 2048, P, [EXPERTS // 2, ET, D]),
                    stage(xT_both[:].bitcast(F32).rearrange("p a c n -> p (a c n)"), 0, P, [EXPERTS // 2, ET, D])]
        split_plan = [
            ([(stage(r1, 0, P, [EXPERTS, KC, EI]), a["L1_ffn_Wg"].rearrange("e (c p) n -> p e c n", p=P))],
             stage(r1, 0, P, [EXPERTS, KC, EI]), wg),
            ([(stage(r2, 0, P, [EXPERTS, KC, EI]), a["L1_ffn_Wu"].rearrange("e (c p) n -> p e c n", p=P))],
             stage(r2, 0, P, [EXPERTS, KC, EI]), wu),
            ([(stage(r3, 0, P, [KC, FF]), a["L0_attn_w1"].rearrange(chunk, p=P))],
             stage(r3, 0, P, [KC, FF]), w1),
            ([(st_kv[:, :, 0:D], a["L0_attn_wk"].rearrange("(c p) h d -> p c (h d)", p=P)),
              (st_kv[:, :, D:2 * D], a["L0_attn_wv"].rearrange("(c p) h d -> p c (h d)", p=P))],
             st_kv, wkv0),
            ([(stage(r3, 3072, P, [KC, D]), a["L0_attn_wq"].rearrange("(c p) h d -> p c (h d)", p=P))],
             stage(r3, 3072, P, [KC, D]), wq0),
            ([(stage(r3, 3584, P, [KC, D]), a["L1_attn_Wq"].rearrange(chunk, p=P))],
             stage(r3, 3584, P, [KC, D]), wq1),
            ([(st_win[:, :, s * M0:(s + 1) * M0], a["L0_ffn_Win"].rearrange(chunk, p=P)) for s in range(2)],
             st_win, win),
            ([(stage(r0, 256, P, [KC, LATENT]), a["L1_attn_Wl"].rearrange(chunk, p=P))],
             stage(r0, 256, P, [KC, LATENT]), wl),
            ([(stage(r0, 512, LATENT, [D]), a["L1_attn_Wk"])], stage(r0, 512, LATENT, [D]), wk1),
            ([(stage(r0, 768, LATENT, [D]), a["L1_attn_Wv"])], stage(r0, 768, LATENT, [D]), wv1),
            ([(stage(r0, 1024, P, [KC, EXPERTS]), a["L1_ffn_Wr"].rearrange(chunk, p=P))],
             stage(r0, 1024, P, [KC, EXPERTS]), wr),
            ([(stage(x_tok_flat, 0, P, [FT, D]), a["L0_attn_w2"].rearrange(chunk, p=P))],
             stage(x_tok_flat, 0, P, [FT, D]), w2),
            ([(wd_stage[0], a["L1_ffn_Wd"][0:4].rearrange("e (m p) n -> p e m n", p=P))],
             wd_stage[0], (wd[0][:, 0:4], wd[1][:, 0:4])),
            ([(wd_stage[1], a["L1_ffn_Wd"][4:8].rearrange("e (m p) n -> p e m n", p=P))],
             wd_stage[1], (wd[0][:, 4:8], wd[1][:, 4:8])),
        ]

        def column(vec, rows):
            return vec.rearrange("(c p) -> p c", p=rows)

        def halves(m):
            return m.rearrange("m (k two) -> two m k", two=2)

        def row_for_all(vec):
            return vec.partition_broadcast(P)

        plain_loads = [
            (wo0[:], a["L0_attn_wo"].rearrange("(c h) d n -> (h d) c n", c=KC)),
            (wout[0:M0, :], a["L0_ffn_Wout"]), (wout[M0:P, :], a["L0_ffn_Wout"]),
            (gamma[:], column(a["L0_attn_gamma1"], P)), (beta[:], column(a["L0_attn_beta1"], P)),
            (b1[:], column(a["L0_attn_b1"], P)), (bq[:], column(a["L1_attn_bq"], P)),
            (bk[:], column(a["L1_attn_bk"], P)), (bl[:], column(a["L1_attn_bl"], LATENT)),
            (b2_all[:], row_for_all(a["L0_attn_b2"])), (bout_all[:], row_for_all(a["L0_ffn_bout"])),
            (bv_all[:], row_for_all(a["L1_attn_bv"])), (temp_all[:], row_for_all(a["L1_ffn_temperature"])),
        ]
        for s in range(2):
            rows = slice(s * M0, (s + 1) * M0)
            plain_loads += [
                (bin2[rows, :], column(a["L0_ffn_bin_"], M0)),
                (w1p[rows, :], halves(a["L0_ffn_W1"])[s]), (b1p[rows, :], halves(a["L0_ffn_b1"])[s]),
                (w2p[rows, :], halves(a["L0_ffn_W2"])[s]),
            ]
        zeroed_loads = [(wo1[32 * c:32 * c + DH, :, :],
                         a["L1_attn_Wo"].rearrange("(g c r) n -> c r g n", g=GROUPS, c=GH)[c])
                        for c in range(GH)]
        zeroed_loads.append((wo1[DH:DH + 1, 0, :], a["L1_attn_bo"].rearrange("(a n) -> a n", a=1)))
        zeroed_loads.append((b2p[0:M0, :], column(a["L0_ffn_b2"], M0)))
        N_LOADS = sum(len(x[0]) for x in split_plan) + len(plain_loads) + len(zeroed_loads)
        N_SPLIT = len(split_plan)

        x_view = a["L0_attn_x"].rearrange("b (t p) d -> b p t d", p=P)
        out_view = out.rearrange("b (t p) d -> b p t d", p=P)

        def stack_rows(g, hh, part):
            row, at = HALF * (g % 2) + DH * hh, HALF * (g // 2) + DH * part
            return slice(row, row + DH), slice(at, at + DH)

        def load_head(eng, g, hh, which, loaded):
            sources = (qT_hi, qT_lo, qT_hi) if which == "q" else (kT_hi, kT_hi, kT_lo)
            stack = qs[:, g % 2] if which == "q" else k_stack[g]
            for part in range(3):
                rows, at = stack_rows(g, hh, part)
                eng.dma_start(stack[at, hh, :], sources[part][rows, g // 2, :]).then_inc(loaded.sem, 16)

        def load_group(eng, g, which):
            for hh in range(GH):
                load_head(eng, g, hh, which, (q_loaded if which == "q" else k_loaded)[g - 1])

        def load_maxima(eng, u):
            g, ib = divmod(u, IB)
            at = HALF * (g // 2) + SPLIT_ROWS
            eng.dma_start(qs[at:at + 2 * GH, g % 2, :, ib * NB:(ib + 1) * NB],
                          mT[:].unsqueeze(1).to_broadcast([2 * GH, GH, NB])).then_inc(m_loaded.sem, 16)

        block = ctx.enter_context(nc.Block())

        @block.sync
        def _(sp):
            for loads, _, _ in split_plan:
                for dst, src in loads:
                    sp.dma_start(dst, src).then_inc(weights_loaded.sem, 16)
            with nc.allow_non_contiguous_dma(reason="a few KB of per-partition vectors, once"):
                for dst, src in plain_loads:
                    sp.dma_start(dst, src).then_inc(weights_loaded.sem, 16)
            sp.wait_ge(setup_step.sem, 2)
            with nc.allow_non_contiguous_dma(reason="one of them is a per-partition vector"):
                for dst, src in zeroed_loads:
                    sp.dma_start(dst, src).then_inc(weights_loaded.sem, 16)

            with sp.Fori(0, BATCH) as b:
                sp.wait_ge(m_cleared.sem, m_cleared.at(b, 0))
                sp.wait_ge(k1_lo_done.sem, k1_lo_done.at(b, 3))
                load_head(sp, 0, 0, "k", head_loaded[0])
                sp.wait_ge(q1_lo_done.sem, q1_lo_done.at(b, 3))
                load_head(sp, 0, 0, "q", head_loaded[0])
                for hh in range(1, GH):
                    load_head(sp, 0, hh, "k", head_loaded[hh])
                    load_head(sp, 0, hh, "q", head_loaded[hh])
                sp.wait_ge(q1_lo_done.sem, q1_lo_done.at(b, 4))
                load_group(sp, 2, "q")
                load_group(sp, 1, "q")
                load_group(sp, 3, "q")
                load_group(sp, 1, "k")
                sp.wait_ge(k1_lo_done.sem, k1_lo_done.at(b, 4))
                sp.wait_ge(late_slots_ready.sem, late_slots_ready.at(b, 4))
                for u in range(1, UNITS):
                    sp.wait_ge(mT_done.sem, mT_done.at(b, u + 1))
                    load_maxima(sp, u)
                    if u == 1:
                        load_group(sp, 2, "k")
                        load_group(sp, 3, "k")
                sp.wait_ge(exp_done.sem, exp_done.at(b, UNITS * BURSTS * GH))
                for g in range(GROUPS):
                    at = HALF * (g // 2) + SPLIT_ROWS
                    sp.dma_start(qs[at:at + 2 * GH, g % 2], qs[at + 2 * GH:at + 4 * GH, g % 2])\
                      .then_inc(m_cleared.sem, 16)
                for tp in range(4):
                    sp.wait_ge(moe_done.sem, moe_done.at(b, (EXPERTS - 1) * TT + 2 * tp + 2))
                    sp.dma_start(out_view[b, :, 2 * tp:2 * tp + 2, :], moe_acc[:, 2 * tp:2 * tp + 2, :])\
                      .then_inc(stored.sem, 16)
            sp.wait_ge(stored.sem, BATCH * stored.per_batch + stored.at_start)
            sp.wait_ge(m_cleared.sem, BATCH * m_cleared.per_batch + m_cleared.at_start)

        @block.gpsimd
        def _(pool):
            pool.memset(wo1[:], 0.0).then_inc(setup_step.sem, 1)
            pool.memset(b2p[:], 0.0).then_inc(setup_step.sem, 1)
            pool.memset(ident[:], 0.0).then_inc(setup_step.sem, 1)
            pool.memset(head_mask[:], 1.0).then_inc(setup_step.sem, 1)
            pool.memset(before[:], 0.0).then_inc(setup_step.sem, 1)
            pool.memset(ks[:], 0.0).then_inc(setup_step.sem, 1)
            pool.memset(qs[:], 0.0).then_inc(setup_step.sem, 1)
            pool.memset(ones_tok[:], 1.0).then_inc(setup_step.sem, 1)
            pool.memset(eps[:, 0, :], 1e-5).then_inc(setup_step.sem, 1)
            pool.memset(eps[:, 1, :], 1e-6).then_inc(setup_step.sem, 1)
            pool.memset(neg_half[:], -0.5).then_inc(setup_step.sem, 1)
            pool.memset(zero_cell[:], 0.0).then_inc(setup_step.sem, 1)
            pair = float(struct.unpack("f", struct.pack("I", PAIR_OF_UNITS))[0])
            pool.memset(max_rows[:], pair).then_inc(setup_step.sem, 1)
            pool.wait_ge(setup_step.sem, 13)
            for s in range(2):
                half = max_rows[HALF * s:HALF * (s + 1), :]
                pool.affine_select(out=half, in_=half, compare_op=ALU.is_ge, fill=0.0, base=-SPLIT_ROWS,
                                   pattern=[[-2, GH]], channel_multiplier=1).then_inc(setup_step.sem, 1)
            pool.wait_ge(setup_step.sem, 15)
            for s in range(2):
                half = max_rows[HALF * s:HALF * (s + 1), :]
                pool.affine_select(out=half, in_=half, compare_op=ALU.is_ge, fill=0.0, base=SPLIT_ROWS + 1,
                                   pattern=[[2, GH]], channel_multiplier=-1).then_inc(setup_step.sem, 1)
            pool.wait_ge(setup_step.sem, 17)
            for slot in range(2):
                pool.tensor_copy(ks[0:HALF, slot].bitcast(F32), max_rows[0:HALF, :].unsqueeze(2)
                                 .to_broadcast([HALF, GH, TOKENS // 2])).then_inc(setup_step.sem, 1)
            pool.affine_select(out=ident[:], in_=ident[:], compare_op=ALU.not_equal, fill=1.0, base=0,
                               pattern=[[-1, P]], channel_multiplier=1).then_inc(setup_step.sem, 1)
            pool.affine_select(out=before[:], in_=before[:], compare_op=ALU.is_ge, fill=1.0, base=0,
                               pattern=[[-1, EXPERTS], [1, EXPERTS]], channel_multiplier=0)\
                .then_inc(setup_step.sem, 1)
            blocks = head_mask[:, 0:P].rearrange("p (h d) -> p h d", d=DH)
            heads = head_mask[:, P:KVS]
            pool.affine_select(out=blocks, in_=blocks, compare_op=ALU.is_ge, fill=0.0, base=0,
                               pattern=[[-DH, MH], [0, DH]], channel_multiplier=1)\
                .then_inc(setup_step.sem, 1)
            pool.affine_select(out=heads, in_=heads, compare_op=ALU.is_ge, fill=0.0, base=0,
                               pattern=[[-DH, MH]], channel_multiplier=1).then_inc(setup_step.sem, 1)
            pool.wait_ge(setup_step.sem, 23)
            pool.affine_select(out=blocks, in_=blocks, compare_op=ALU.is_ge, fill=0.0, base=DH - 1,
                               pattern=[[DH, MH], [0, DH]], channel_multiplier=-1)\
                .then_inc(setup_step.sem, 1)
            pool.affine_select(out=heads, in_=heads, compare_op=ALU.is_ge, fill=0.0, base=DH - 1,
                               pattern=[[DH, MH]], channel_multiplier=-1).then_inc(setup_step.sem, 1)
            pool.tensor_copy(ident16[:], ident[:]).then_inc(setup_step.sem, 1)
            pool.wait_ge(setup_step.sem, 26)
            pool.wait_ge(weights_loaded.sem, 16 * N_LOADS)
            pool.memset(eps[:, 0, :], 1e-5).then_inc(consts_made.sem, 1)

            def rstds(b, norm, s, which_eps):
                half = slice(s * HT, (s + 1) * HT)
                pool.wait_ge(stats_done.sem, stats_done.at(b, norm * TT + (s + 1) * HT))
                pool.tensor_tensor(var_eps[:, half], mv[:, half, 1], eps[:, which_eps, :], ALU.add)\
                    .then_inc(eps_added.sem, 1)
                pool.wait_ge(eps_added.sem, eps_added.at(b, norm * 2 + s + 1))
                pool.tensor_tensor(rstd[:, half], var_eps[:, half], neg_half[:], ALU.pow)\
                    .then_inc(rstd_done.sem, 1)

            def load_x(b_next):
                for s in range(2):
                    half = slice(s * HT, (s + 1) * HT)
                    pool.dma_start(x_tok[:, half, :], x_view[b_next, :, half, :]).then_inc(x_loaded.sem, 16)

            def hidden_lo(b, i, units):
                for f in units:
                    n = i * FT + f
                    pool.wait_ge(h_hi_done.sem, h_hi_done.at(b, n + 1))
                    pool.tensor_tensor(h_ff[1][:, f, :], h_tmp[:, n % 4, :], h_ff[0][:, f, :], ALU.subtract)\
                        .then_inc(h_lo_done.sem, 1)

            pool.wait_ge(lo_split.sem, N_SPLIT)
            load_x(0)
            for s in range(2):
                rstds(-1, NORM_NEXT, s, 0)
            for s in range(2):
                rstds(-1, NORM_NEXT_LN1, s, 1)
            with pool.Fori(0, BATCH) as b:
                for s in range(2):
                    rstds(b, NORM_FFN, s, 1)
                hidden_lo(b, 0, range(FT))
                pool.wait_ge(add1_done.sem, add1_done.at(b, 4))
                pool.tensor_tensor(x_tok[:], x_tok[:], add1, ALU.add).then_inc(x_add1_done.sem, 1)
                def add_bout(s):
                    half = slice(s * HT, (s + 1) * HT)
                    pool.wait_ge(norm_done.sem, norm_done.at(b, NORM_EXPAND * TT + (s + 1) * HT))
                    pool.tensor_tensor(x_tok[:, half, :], x_tok[:, half, :],
                                       bout_all[:].unsqueeze(1).to_broadcast([P, HT, D]), ALU.add)\
                        .then_inc(x_bout_done.sem, 1)

                hidden_lo(b, 1, range(2))
                rstds(b, NORM_EXPAND, 0, 0)
                hidden_lo(b, 1, range(2, FT))
                add_bout(0)
                rstds(b, NORM_EXPAND, 1, 0)
                add_bout(1)
                rstds(b, NORM_PROJECT, 0, 0)
                pool.memset(v_aug[:, :, :, DH:32], 1.0).then_inc(v_ones_done.sem, 1)
                rstds(b, NORM_PROJECT, 1, 0)
                for u in range(UNITS):
                    g, ib = divmod(u, IB)
                    o = oT[:, g, ib * NB:(ib + 1) * NB]
                    pool.wait_ge(den_step.sem, den_step.at(b, (1 + DIV_PARTS) * (u + 1)))
                    pool.tensor_tensor(o, o, den1[:, 1 + u % 2, :], ALU.mult).then_inc(att1_done.sem, 1)
                for s in range(2):
                    rstds(b, NORM_ROUTER, s, 0)
                for e in range(EXPERTS):
                    for j in range(4 * e, 4 * e + 4):
                        i, m = divmod(j % 4, ET)
                        at = slice(i * NB, (i + 1) * NB)
                        pool.wait_ge(hmoe_hi_done.sem, hmoe_hi_done.at(b, j + 1))
                        pool.tensor_tensor(h_moe[1][:, e % 2, m, at], silu[:, j % 4, :],
                                           h_moe[0][:, e % 2, m, at], ALU.subtract).then_inc(hmoe_lo_done.sem, 1)
                    if e == 1:
                        pool.wait_ge(moe_done.sem, moe_done.at(b, TT))
                        load_x((b + 1) % BATCH)
                    if e == 2:
                        for s in range(2):
                            rstds(b, NORM_NEXT, s, 0)
                    if e == 4:
                        for s in range(2):
                            rstds(b, NORM_NEXT_LN1, s, 1)

        @block.scalar
        def _(act):
            act.wait_ge(weights_loaded.sem, 16 * N_LOADS)
            for _, staged, (hi, _) in split_plan:
                act.activation(hi[:], staged, ACT.Copy).then_inc(hi_split.sem, 1)

            def xT_his(b, n, i):
                for c in range(KC):
                    k = KC * i + c
                    dst = xT[0][:, c, i * NB:(i + 1) * NB]
                    act.wait_ge(xT_full.sem, xT_full.at(b, 4 * n + k + 1))
                    if n in (T_FFN, T_NEXT):
                        act.activation(dst, bank[T_BANK[n] + k][:], ACT.Identity, bias=beta[:, c:c + 1],
                                       scale=gamma[:, c:c + 1]).then_inc(xT_hi_done.sem, 1)
                    else:
                        act.activation(dst, bank[T_BANK[n] + k][:], ACT.Copy).then_inc(xT_hi_done.sem, 1)

            for i in range(IB):
                xT_his(-1, T_NEXT, i)
            with act.Fori(0, BATCH) as b:
                for k in range(4):
                    i, c = divmod(k, KC)
                    act.wait_ge(attT0_full.sem, attT0_full.at(b, k + 1))
                    act.activation(attT0[:, c, i * NB:(i + 1) * NB], bank[4 + k][:], ACT.Copy)\
                        .then_inc(attT0_done.sem, 1)
                xT_his(b, T_FFN, 0)

                def gelu_out(n):
                    act.wait_ge(t1_done.sem, t1_done.at(b, n + 1))
                    act.activation(t1[:, 2 * n:2 * n + 2, :], t1[:, 2 * n:2 * n + 2, :], ACT.Gelu)\
                        .then_inc(gelu_done.sem, 1)

                def relus(i, pairs_of_units):
                    if pairs_of_units[0] == 0:
                        act.wait_ge(s_full.sem, s_full.at(b, i + 1))
                        act.activation(s_dup[i], bank[2 * i][:], ACT.Identity, bias=bin2[:])\
                            .then_inc(s_done.sem, 1)
                        act.wait_ge(s_done.sem, s_done.at(b, i + 1))
                    for k in pairs_of_units:
                        if k >= 2:
                            act.wait_ge(g_done.sem, g_done.at(b, i * PAIRS + k - 1))
                        act.activation(relu_s[i][:, k % 2, :], s_dup[i], ACT.Relu, bias=b1p[:, k:k + 1],
                                       scale=w1p[:, k:k + 1]).then_inc(relu_done.sem, 1)

                def hidden_hi(n):
                    act.wait_ge(h_done.sem, h_done.at(b, n + 1))
                    if n == FT:
                        act.wait_ge(w2_full.sem, w2_full.at(b, 2))
                    act.activation(h_ff[0][:, n % FT, :], h_tmp[:, n % 4, :], ACT.Copy).then_inc(h_hi_done.sem, 1)

                for i in range(IB):
                    for f in range(FT):
                        n = i * FT + f
                        act.wait_ge(h_full.sem, h_full.at(b, n + 1))
                        if n >= 4:
                            act.wait_ge(h_lo_done.sem, h_lo_done.at(b, n - 3))
                        act.activation(h_tmp[:, n % 4, :], bank[4 + f % 4][:], ACT.Gelu, bias=b1[:, f:f + 1])\
                            .then_inc(h_done.sem, 1)
                        if f:
                            hidden_hi(n - 1)
                    hidden_hi(i * FT + FT - 1)
                    if i == 0:
                        xT_his(b, T_FFN, 1)
                        gelu_out(0)
                        gelu_out(1)
                xT_his(b, T_EXPAND, 0)
                relus(0, range(3))
                gelu_out(2)
                relus(0, range(3, PAIRS))
                gelu_out(3)
                xT_his(b, T_EXPAND, 1)
                relus(1, range(4))
                xT_his(b, T_PROJECT, 0)
                relus(1, range(4, PAIRS))

                def latent_hi(i):
                    act.wait_ge(lat_full.sem, lat_full.at(b, i + 1))
                    act.activation(latT[0][:, i * NB:(i + 1) * NB], bank[2 * i][0:LATENT, :], ACT.Identity,
                                   bias=bl[:]).then_inc(lat_hi_done.sem, 1)

                def qk_his(i):
                    for m in range(KC):
                        act.wait_ge(k1_full.sem, k1_full.at(b, KC * i + m + 1))
                        act.activation(kT_hi[:, m, i * NB:(i + 1) * NB], bank[4 + KC * i + m][:], ACT.Identity,
                                       bias=bk[:, m:m + 1]).then_inc(k1_hi_done.sem, 1)
                    for m in range(KC):
                        act.wait_ge(q1_full.sem, q1_full.at(b, KC * i + m + 1))
                        act.activation(qT_hi[:, m, i * NB:(i + 1) * NB], bank[KC * i + m][:], ACT.Identity,
                                       bias=bq[:, m:m + 1]).then_inc(q1_hi_done.sem, 1)

                latent_hi(0)
                qk_his(0)
                xT_his(b, T_PROJECT, 1)
                latent_hi(1)
                qk_his(1)

                for g in (2, 3):
                    words = late_words[g]
                    act.activation(words[0:HALF, :], zero_cell[0:HALF, :].to_broadcast([HALF, 2048]),
                                   ACT.Copy).then_inc(late_slots_ready.sem, 1)
                    act.activation(words[HALF + 32:P, :].rearrange("p (h n) -> p h n", h=GH),
                                   max_rows[HALF + 32:P, :].unsqueeze(2).to_broadcast([32, GH, 512]),
                                   ACT.Copy).then_inc(late_slots_ready.sem, 1)

                def maxima_to_rows(u):
                    act.wait_ge(mT_full.sem, mT_full.at(b, u + 1))
                    if u:
                        act.wait_ge(m_loaded.sem, m_loaded.at(b, 16 * u))
                    act.activation(mT[:], bank[6 + u % IB][:].bitcast(F16)[0:2 * GH, 0:NB], ACT.Copy)\
                        .then_inc(mT_done.sem, 1)

                def out_of_unit(u):
                    g, ib = divmod(u, IB)
                    act.wait_ge(av_done.sem, av_done.at(b, BURSTS * (u + 1)))
                    if u == 0:
                        for hh in range(GH):
                            act.wait_ge(head_loaded[hh].sem, head_loaded[hh].at(b, 16 * 2 * 3))
                        for k in range(GROUPS - 1):
                            act.wait_ge(q_loaded[k].sem, q_loaded[k].at(b, 16 * 3 * GH))
                            act.wait_ge(k_loaded[k].sem, k_loaded[k].at(b, 16 * 3 * GH))
                    act.activation(oT[:, g, ib * NB:(ib + 1) * NB], bank[6 + ib][:], ACT.Copy)\
                        .then_inc(o_done.sem, 1)

                maxima_to_rows(0)
                act.wait_ge(mT_done.sem, mT_done.at(b, 1))
                load_maxima(act, 0)
                for n in range(UNITS * BURSTS):
                    u, r = divmod(n, BURSTS)
                    if r == BURSTS - 2 and u + 1 < UNITS:
                        maxima_to_rows(u + 1)
                    for hh in range(GH):
                        tile = n * GH + hh
                        act.wait_ge(cols_full.sem, cols_full.at(b, tile + 1))
                        if n >= 2 and hh == 0:
                            act.wait_ge(av_done.sem, av_done.at(b, n - 1))
                        act.activation(probs[:, tile % P_SLOTS, :], bank[2 + tile % 3][:], ACT.Exp,
                                       scale=SCALE).then_inc(exp_done.sem, 1)
                    if r == OUT_AFTER and u:
                        out_of_unit(u - 1)
                out_of_unit(UNITS - 1)
                def silu_of(j):
                    if j < EXPERTS * 4:
                        act.wait_ge(gate_full.sem, gate_full.at(b, j + 1))
                        if j >= 4:
                            act.wait_ge(hmoe_lo_done.sem, hmoe_lo_done.at(b, j - 3))
                        act.activation(silu[:, j % 4, :], bank[4 + 2 * (j % 2)][:], ACT.Silu)\
                            .then_inc(silu_done.sem, 1)
                    if j:
                        e, k = divmod(j - 1, 4)
                        i, m = divmod(k, ET)
                        act.wait_ge(hmoe_done.sem, hmoe_done.at(b, j))
                        if e >= 2 and k == 0:
                            act.wait_ge(down_full.sem, down_full.at(b, 4 * (e - 1)))
                        act.activation(h_moe[0][:, e % 2, m, i * NB:(i + 1) * NB], silu[:, (j - 1) % 4, :],
                                       ACT.Copy).then_inc(hmoe_hi_done.sem, 1)

                xT_his(b, T_ROUTER, 0)
                silu_of(0)
                silu_of(1)
                xT_his(b, T_ROUTER, 1)
                act.wait_ge(route_step.sem, route_step.at(b, ROUTE_Z))
                act.activation(rt[:, 1], rt[:, 0], ACT.Exp, scale=-1.0).then_inc(route_exp.sem, 1)
                act.wait_ge(route_step.sem, route_step.at(b, ROUTE_DIST))
                act.activation(rt[:, 6], rt[:, 5], ACT.Exp, scale=-1.0 / 0.1).then_inc(route_exp.sem, 1)
                act.activation(rt[:, 7], rt[:, 5], ACT.Exp, scale=-1.0 / 0.3).then_inc(route_exp.sem, 1)
                for j in range(2, EXPERTS * 4 + 1):
                    silu_of(j)
                for i in range(IB):
                    xT_his(b, T_NEXT, i)

        @block.tensor
        def _(pe):
            pe.wait_ge(lo_split.sem, N_SPLIT)
            pe.wait_ge(consts_made.sem, 1)

            def split_product(out_ap, stationary, moving, xT_counts=None):
                chunks = stationary[1]
                terms = [(c, ps, pm) for c in range(chunks) for ps, pm in ((0, 0), (1, 0), (0, 1))]
                for k, (c, ps, pm) in enumerate(terms):
                    if xT_counts is not None and k % 3 == 0:
                        pe.wait_ge(xT_lo_done.sem, xT_counts[c])
                    last = pe.matmul(out_ap, stationary[0](ps, c), moving(pm, c),
                                     start=(k == 0), stop=(k == len(terms) - 1))
                return last

            def lows(b, n, i):
                return [xT_lo_done.at(b, 4 * n + KC * i + c + 1) for c in range(KC)]

            def transposes(b, norm, i):
                n = T_OF_NORM[norm]
                pe.wait_ge(norm_done.sem, norm_done.at(b, norm * TT + HT * (i + 1)))
                for c in range(KC):
                    for t in range(HT):
                        last = pe.transpose(bank[T_BANK[n] + KC * i + c][:, t * P:(t + 1) * P],
                                            n_tok[:, HT * i + t, c * P:(c + 1) * P], ident[:])
                    last.then_inc(xT_full.sem, 1)

            def cols(w, lo, hi):
                return (lambda part, c: w[part][:, c, lo:hi], KC)

            def x_cols(lo, hi):
                return lambda part, c: xT[part][:, c, lo:hi]

            for i in range(IB):
                transposes(-1, NORM_NEXT_LN1, i)
            with pe.Fori(0, BATCH) as b:
                for t in range(TT):
                    pe.wait_ge(xT_lo_done.sem, xT_lo_done.at(b - 1, 4 * T_NEXT + (2 if t < 2 else 4)))
                    if t >= 4:
                        pe.wait_ge(kv_done.sem, kv_done.at(b, t - 3))
                    split_product(bank[4 + t % 4][:],
                                  (lambda part, c: xT[part][:, c, t * P:(t + 1) * P], KC),
                                  lambda part, c: wkv0[part][:, c, :]).then_inc(kv_full.sem, 1)
                pe.wait_ge(moe_done.sem, moe_done.at(b, 0))
                for k in range(4):
                    m, i = divmod(k, IB)
                    split_product(bank[k][:], cols(wq0, m * P, (m + 1) * P),
                                  x_cols(i * NB, (i + 1) * NB)).then_inc(q_full.sem, 1)
                pe.wait_ge(kv_done.sem, kv_done.at(b, TT))
                for m in range(KC):
                    for t in range(TT):
                        pe.matmul(bank[4 + m][:, 0:P], kv_tok[:, t, m * P:(m + 1) * P],
                                  kv_tok[:, t, D + m * P:D + (m + 1) * P], start=(t == 0), stop=(t == TT - 1))
                    for t in range(TT):
                        last = pe.matmul(bank[4 + m][:, P:KVS], kv_tok[:, t, m * P:(m + 1) * P],
                                         ones_tok[:], start=(t == 0), stop=(t == TT - 1))
                    last.then_inc(kvs_full.sem, 1)
                pe.wait_ge(kvs_done.sem, kvs_done.at(b, KC))
                pe.wait_ge(q_done.sem, q_done.at(b, 4))
                for t in range(TT):
                    if t >= 4:
                        pe.wait_ge(att0_done.sem, att0_done.at(b, t - 3))
                    for m in range(KC):
                        last = pe.matmul(bank[t % 4][:, m * KVS:(m + 1) * KVS], qpT[:, m, t * P:(t + 1) * P],
                                         kvsB[:, m, :], start=True, stop=True)
                    last.then_inc(numden_full.sem, 1)
                for k in range(4):
                    i, c = divmod(k, KC)
                    pe.wait_ge(att0_done.sem, att0_done.at(b, HT * (i + 1)))
                    for t in range(HT):
                        last = pe.transpose(bank[4 + k][:, t * P:(t + 1) * P],
                                            att_tok[:, HT * i + t, c * P:(c + 1) * P], ident[:])
                    last.then_inc(attT0_full.sem, 1)
                for tp in range(4):
                    pe.wait_ge(attT0_done.sem, attT0_done.at(b, 2 * (tp // 2 + 1)))
                    for t in range(2):
                        for c in range(KC):
                            at = (2 * tp + t) * P
                            last = pe.matmul(bank[tp][:, t * D:(t + 1) * D], attT0[:, c, at:at + P],
                                             wo0[:, c, :], start=(c == 0), stop=(c == KC - 1))
                    last.then_inc(wo_full.sem, 1)

                def hidden_ffn(i):
                    for f in range(FT):
                        n = i * FT + f
                        if n >= 4:
                            pe.wait_ge(h_done.sem, h_done.at(b, n - 3))
                        split_product(bank[4 + f % 4][:], cols(w1, f * P, (f + 1) * P),
                                      x_cols(i * NB, (i + 1) * NB),
                                      lows(b, T_FFN, i) if f == 0 else None).then_inc(h_full.sem, 1)

                def out_ffn(n, t):
                    i, tp = divmod(n, 2)
                    at = (2 * tp + t) * P
                    for f in range(FT):
                        if tp == 0 and t == 0:
                            pe.wait_ge(h_lo_done.sem, h_lo_done.at(b, i * FT + f + 1))
                        for ph, pw in ((0, 0), (1, 0), (0, 1)):
                            last = pe.matmul(bank[n][:, t * D:(t + 1) * D], h_ff[ph][:, f, at:at + P],
                                             w2[pw][:, f, :], start=(f == 0 and ph == pw),
                                             stop=(f == FT - 1 and pw == 1))
                    if t == 1:
                        last.then_inc(w2_full.sem, 1)

                def expand_in(i):
                    split_product(bank[2 * i][:], cols(win, 0, 2 * M0),
                                  x_cols(i * NB, (i + 1) * NB), lows(b, T_EXPAND, i)).then_inc(s_full.sem, 1)

                def expand_out(i):
                    pe.wait_ge(g_done.sem, g_done.at(b, (i + 1) * PAIRS))
                    for tp in (2 * i, 2 * i + 1):
                        for t in range(2):
                            at = (2 * (tp % 2) + t) * P
                            last = pe.matmul(bank[tp][:, t * D:(t + 1) * D], g_acc[i][:, at:at + P], wout[:],
                                             start=True, stop=True)
                        last.then_inc(fo_full.sem, 1)

                def latent(i):
                    split_product(bank[2 * i][0:LATENT, :], (lambda part, c: wl[part][:, c, :], KC),
                                  x_cols(i * NB, (i + 1) * NB), lows(b, T_PROJECT, i)).then_inc(lat_full.sem, 1)

                def keys_and_queries(i):
                    pe.wait_ge(lat_lo_done.sem, lat_lo_done.at(b, i + 1))
                    for m in range(KC):
                        split_product(bank[4 + KC * i + m][:],
                                      (lambda part, c: wk1[part][:, m * P:(m + 1) * P], 1),
                                      lambda part, c: latT[part][:, i * NB:(i + 1) * NB]).then_inc(k1_full.sem, 1)
                    for m in range(KC):
                        split_product(bank[KC * i + m][:], cols(wq1, m * P, (m + 1) * P),
                                      x_cols(i * NB, (i + 1) * NB)).then_inc(q1_full.sem, 1)

                def values_of(i):
                    for tp in (2 * i, 2 * i + 1):
                        pe.wait_ge(k1_lo_done.sem, k1_lo_done.at(b, tp + 1))
                        for t in range(2):
                            at = (2 * tp + t) * P
                            last = split_product(bank[4 + tp][:, t * D:(t + 1) * D],
                                                 (lambda part, c: latT[part][:, at:at + P], 1),
                                                 lambda part, c: wv1[part][:])
                        last.then_inc(v1_full.sem, 1)

                transposes(b, NORM_FFN, 0)
                hidden_ffn(0)
                transposes(b, NORM_FFN, 1)
                for n in (0, 1):
                    out_ffn(n, 0)
                    out_ffn(n, 1)
                hidden_ffn(1)
                transposes(b, NORM_EXPAND, 0)
                out_ffn(2, 0)
                expand_in(0)
                out_ffn(2, 1)
                out_ffn(3, 0)
                out_ffn(3, 1)
                expand_out(0)
                transposes(b, NORM_EXPAND, 1)
                expand_in(1)
                transposes(b, NORM_PROJECT, 0)
                latent(0)
                expand_out(1)
                keys_and_queries(0)
                transposes(b, NORM_PROJECT, 1)
                values_of(0)
                latent(1)
                keys_and_queries(1)
                values_of(1)
                pe.wait_ge(q1_lo_done.sem, q1_lo_done.at(b, 4))
                pe.wait_ge(v1_done.sem, v1_done.at(b, 4))
                pe.wait_ge(v_ones_done.sem, v_ones_done.at(b, 1))

                def row_tile(n):
                    u, r = divmod(n, MAX_TILES)
                    g, ib = divmod(u, IB)
                    hh, it, jb = r // TT, (TT // IB) * ib + (r // IB) % (TT // IB), r % IB
                    if r % TT == 0 and u == 0:
                        pe.wait_ge(head_loaded[hh].sem, head_loaded[hh].at(b, 16 * 2 * 3))
                    if r == 0 and g and ib == 0:
                        pe.wait_ge(q_loaded[g - 1].sem, q_loaded[g - 1].at(b, 16 * 3 * GH))
                        pe.wait_ge(k_loaded[g - 1].sem, k_loaded[g - 1].at(b, 16 * 3 * GH))
                    if r == 0 and g == 1 and ib == 0:
                        pe.wait_ge(q_loaded[2].sem, q_loaded[2].at(b, 16 * 3 * GH))
                    if n >= 3:
                        pe.wait_ge(rows_max_done.sem, rows_max_done.at(b, n - 2))
                    rows = slice(0, HALF) if n < AHEAD else slice(0, P)
                    pe.matmul(bank[ROW_BANK[n % 3]][:], qs[rows, g % 2, hh, it * P:(it + 1) * P],
                              k_stack[g][rows, hh, jb * NB:(jb + 1) * NB],
                              start=True, stop=True).then_inc(rows_full.sem, 1)

                def maxima(u):
                    pe.wait_ge(m16_done.sem, m16_done.at(b, u + 1))
                    if u:
                        pe.wait_ge(mT_done.sem, mT_done.at(b, u))
                    if u >= 2:
                        pe.wait_ge(o_done.sem, o_done.at(b, u - 1))
                    for it in range(TT // IB):
                        last = pe.transpose(bank[6 + u % IB][:].bitcast(F16)[0:2 * GH, it * P:(it + 1) * P],
                                            m16[:, it].rearrange("p h s -> p (h s)"), ident16[:])
                    last.then_inc(mT_full.sem, 1)

                def column_tile(n, hh):
                    u, jt = divmod(n, BURSTS)
                    g, ib = divmod(u, IB)
                    tile = n * GH + hh
                    if tile >= 3:
                        pe.wait_ge(exp_done.sem, exp_done.at(b, tile - 2))
                    pe.matmul(bank[2 + tile % 3][:], k_stack[g][:, hh, jt * P:(jt + 1) * P],
                              qs[:, g % 2, hh, ib * NB:(ib + 1) * NB],
                              start=True, stop=True).then_inc(cols_full.sem, 1)

                def values(n):
                    u, jt = divmod(n, BURSTS)
                    g, ib = divmod(u, IB)
                    if jt == 0 and u >= 2:
                        pe.wait_ge(o_done.sem, o_done.at(b, u - 1))
                    pe.wait_ge(exp_done.sem, exp_done.at(b, (n + 1) * GH))
                    for hh in range(GH):
                        last = pe.matmul(bank[6 + ib][32 * hh:32 * hh + 32, :], v_aug[:, jt, GH * g + hh, :],
                                         probs[:, (n * GH + hh) % P_SLOTS, :], start=(jt == 0),
                                         stop=(jt == TT - 1))
                    last.then_inc(av_done.sem, 1)

                pe.wait_ge(m_cleared.sem, m_cleared.at(b, 0))
                for n in range(AHEAD):
                    row_tile(n)
                    if n == MAX_TILES + 1:
                        maxima(0)
                row = AHEAD
                for n in range(UNITS * BURSTS):
                    u, r = divmod(n, BURSTS)
                    if n == 0:
                        pe.wait_ge(q_loaded[1].sem, q_loaded[1].at(b, 16 * 3 * GH))
                    if r == 0:
                        pe.wait_ge(m_loaded.sem, m_loaded.at(b, 16 * (u + 1)))
                    if r == BURSTS - 2 and u + 1 < UNITS:
                        maxima(u + 1)
                    for hh in range(GH):
                        column_tile(n, hh)
                        if row < UNITS * MAX_TILES:
                            row_tile(row)
                            row += 1
                    if n < CATCH_UP:
                        row_tile(row)
                        row += 1
                    if n:
                        values(n - 1)
                values(UNITS * BURSTS - 1)
                pe.wait_ge(rows_max_done.sem, rows_max_done.at(b, UNITS * MAX_TILES))
                pe.wait_ge(exp_done.sem, exp_done.at(b, UNITS * BURSTS * GH))
                for tp in range(4):
                    if tp % 2 == 0:
                        pe.wait_ge(att1_done.sem, att1_done.at(b, UNITS - IB + 1 + tp // 2))
                    for t in range(2):
                        for g in range(GROUPS):
                            at = (2 * tp + t) * P
                            last = pe.matmul(bank[tp][:, t * D:(t + 1) * D], oT[:, g, at:at + P], wo1[:, g, :],
                                             start=(g == 0), stop=(g == GROUPS - 1))
                    last.then_inc(o1_full.sem, 1)
                def gate_up(j):
                    e, k = divmod(j, 4)
                    i, m = divmod(k, ET)
                    if j >= 2:
                        pe.wait_ge(hmoe_done.sem, hmoe_done.at(b, j - 1))
                    for w, at, sig in ((wg, 4, gate_full), (wu, 5, up_full)):
                        split_product(bank[at + 2 * (j % 2)][:],
                                      (lambda part, c: w[part][:, e, c, m * P:(m + 1) * P], KC),
                                      x_cols(i * NB, (i + 1) * NB),
                                      lows(b, T_ROUTER, 0) if j == 0 else None).then_inc(sig.sem, 1)

                transposes(b, NORM_ROUTER, 0)
                gate_up(0)
                gate_up(1)
                transposes(b, NORM_ROUTER, 1)
                pe.wait_ge(xT_lo_done.sem, xT_lo_done.at(b, 4 * T_ROUTER + 4))
                for t in range(TT):
                    last = split_product(bank[0][:, t * EXPERTS:(t + 1) * EXPERTS],
                                         (lambda part, c: xT[part][:, c, t * P:(t + 1) * P], KC),
                                         lambda part, c: wr[part][:, c, :])
                last.then_inc(route_full.sem, 1)
                gate_up(2)
                gate_up(3)

                def down(e):
                    pe.wait_ge(hmoe_lo_done.sem, hmoe_lo_done.at(b, 4 * e + 4))
                    for tp in range(4):
                        if e:
                            pe.wait_ge(moe_done.sem, moe_done.at(b, (e - 1) * TT + 2 * tp + 2))
                        elif tp == 0:
                            pe.wait_ge(route_step.sem, route_step.at(b, ROUTE_Z))
                        for t in range(2):
                            at = (2 * tp + t) * P
                            last = split_product(bank[tp][:, t * D:(t + 1) * D],
                                                 (lambda part, m: h_moe[part][:, e % 2, m, at:at + P], ET),
                                                 lambda part, m: wd[part][:, e, m, :])
                        last.then_inc(down_full.sem, 1)

                for e in range(1, EXPERTS):
                    for j in range(4 * e, 4 * e + 4):
                        gate_up(j)
                    down(e - 1)
                for i in range(IB):
                    pe.wait_ge(hmoe_done.sem, hmoe_done.at(b, EXPERTS * 4))
                    transposes(b, NORM_NEXT_LN1, i)
                down(EXPERTS - 1)

        @block.vector
        def _(dve):
            dve.wait_ge(consts_made.sem, 1)
            for k, (_, staged, (hi, lo)) in enumerate(split_plan):
                dve.wait_ge(hi_split.sem, k + 1)
                dve.tensor_tensor(lo[:], staged, hi[:], ALU.subtract).then_inc(lo_split.sem, 1)
            dve.memset(wait_cell[:, 1:2], 0.0).then_inc(moe_done.sem, moe_done.at_start)
            dve.memset(wait_cell[:, 2:3], 0.0).then_inc(stored.sem, stored.at_start)
            dve.memset(wait_cell[:, 3:4], 0.0).then_inc(m_cleared.sem, m_cleared.at_start)
            dve.reciprocal(rtemp[:], temp_all[:]).then_inc(setup_step.sem, 1)
            dve.wait_ge(lo_split.sem, N_SPLIT)
            dve.wait_ge(setup_step.sem, 27)

            def carry_wait():
                dve.memset(wait_cell[:, 0:1], 0.0)

            def norm_bn(b, n, tp, src):
                for t in (2 * tp, 2 * tp + 1):
                    dve.bn_stats(bn[:, t, :], src[:, t, :]).then_inc(bn_done.sem, 1)

            def norm_aggr(b, n, s):
                dve.wait_ge(bn_done.sem, bn_done.at(b, n * TT + (s + 1) * HT))
                carry_wait()
                for t in range(s * HT, (s + 1) * HT):
                    dve.bn_aggr(mv[:, t, :], bn[:, t, :]).then_inc(stats_done.sem, 1)

            def norm_stats(b, n, s, src):
                norm_bn(b, n, 2 * s, src)
                norm_bn(b, n, 2 * s + 1, src)
                norm_aggr(b, n, s)

            def norm_apply(b, n, s, src, dst):
                dve.wait_ge(rstd_done.sem, rstd_done.at(b, n * 2 + s + 1))
                for t in range(s * HT, (s + 1) * HT):
                    dve.tensor_scalar(dst[:, t, :], src[:, t, :], mv[:, t, 0:1], rstd[:, t:t + 1],
                                      ALU.subtract, ALU.mult).then_inc(norm_done.sem, 1)

            def xT_los(b, n, i):
                for c in range(KC):
                    k = KC * i + c
                    src = bank[T_BANK[n] + k][:]
                    at = slice(i * NB, (i + 1) * NB)
                    dve.wait_ge(xT_hi_done.sem, xT_hi_done.at(b, 4 * n + k + 1))
                    if n in gtmp:
                        tmp = gtmp[n][:, k % 2, :]
                        if k >= 2:
                            dve.wait_ge(xT_lo_done.sem, xT_lo_done.at(b, 4 * n + k - 1))
                        dve.tensor_scalar(tmp, src, gamma[:, c:c + 1], beta[:, c:c + 1],
                                          ALU.mult, ALU.add).then_inc(xT_affine.sem, 1)
                        dve.wait_ge(xT_affine.sem, xT_affine.at(b, 4 * (n == T_NEXT) + k + 1))
                        src = tmp
                    dve.tensor_tensor(xT[1][:, c, at], src, xT[0][:, c, at], ALU.subtract)\
                       .then_inc(xT_lo_done.sem, 1)

            def next_stats(b):
                dve.wait_ge(x_loaded.sem, x_loaded.at(b, 32))
                for s in range(2):
                    norm_stats(b, NORM_NEXT, s, x_tok)

            def next_apply(b):
                for s in range(2):
                    norm_apply(b, NORM_NEXT, s, x_tok, y_tok)

            def next_ln1_stats(b):
                for s in range(2):
                    dve.wait_ge(norm_done.sem, norm_done.at(b, NORM_NEXT * TT + (s + 1) * HT))
                    norm_stats(b, NORM_NEXT_LN1, s, y_tok)

            def next_ln1_apply(b):
                for s in range(2):
                    norm_apply(b, NORM_NEXT_LN1, s, y_tok, n_tok)

            next_stats(-1)
            next_apply(-1)
            next_ln1_stats(-1)
            next_ln1_apply(-1)
            for i in range(IB):
                xT_los(-1, T_NEXT, i)
            with dve.Fori(0, BATCH) as b:
                for t in range(TT):
                    dve.wait_ge(kv_full.sem, kv_full.at(b, t + 1))
                    dve.tensor_scalar(kv_tok[:, t, 0:D], bank[4 + t % 4][:, 0:D], 0.0, 1e-3, ALU.max, ALU.add)
                    dve.tensor_copy(kv_tok[:, t, D:2 * D], bank[4 + t % 4][:, D:2 * D]).then_inc(kv_done.sem, 1)
                dve.wait_ge(stored.sem, stored.at(b, 0))
                for k in range(4):
                    m, i = divmod(k, IB)
                    dve.wait_ge(q_full.sem, q_full.at(b, k + 1))
                    dve.tensor_scalar(qpT[:, m, i * NB:(i + 1) * NB], bank[k][:], 0.0, 1e-3, ALU.max, ALU.add)\
                       .then_inc(q_done.sem, 1)
                for m in range(KC):
                    dve.wait_ge(kvs_full.sem, kvs_full.at(b, m + 1))
                    dve.tensor_tensor(kvsB[:, m], bank[4 + m][:, 0:KVS], head_mask[:], ALU.mult).then_inc(kvs_done.sem, 1)
                for t in range(TT):
                    numden = bank[t % 4][:, 0:KC * KVS].rearrange("p (c n) -> p c n", c=KC)
                    dve.wait_ge(numden_full.sem, numden_full.at(b, t + 1))
                    dve.reciprocal(den0[:, t], numden[:, :, P:KVS]).then_inc(rden_done.sem, 1)
                    dve.wait_ge(rden_done.sem, rden_done.at(b, t + 1))
                    dve.tensor_tensor(att_tok[:, t, :].rearrange("p (c h d) -> p c h d", c=KC, d=DH),
                                      numden[:, :, 0:P].rearrange("p c (h d) -> p c h d", d=DH),
                                      den0[:, t].unsqueeze(3).to_broadcast([P, KC, MH, DH]), ALU.mult)\
                       .then_inc(att0_done.sem, 1)
                for tp in range(4):
                    dve.wait_ge(wo_full.sem, wo_full.at(b, tp + 1))
                    dve.tensor_tensor(add1[:, 2 * tp:2 * tp + 2, :],
                                      bank[tp][:].rearrange("p (t d) -> p t d", d=D),
                                      y_tok[:, 2 * tp:2 * tp + 2, :], ALU.add).then_inc(add1_done.sem, 1)
                    dve.wait_ge(add1_done.sem, add1_done.at(b, tp + 1))
                    norm_bn(b, NORM_FFN, tp, add1)
                    if tp % 2:
                        norm_aggr(b, NORM_FFN, tp // 2)
                    if tp == 2:
                        norm_apply(b, NORM_FFN, 0, add1, n_tok)

                def ffn_out(n):
                    dve.wait_ge(w2_full.sem, w2_full.at(b, n + 1))
                    dve.tensor_tensor(t1[:, 2 * n:2 * n + 2, :], bank[n][:].rearrange("p (t d) -> p t d", d=D),
                                      b2_all[:].unsqueeze(1).to_broadcast([P, 2, D]), ALU.add)\
                       .then_inc(t1_done.sem, 1)

                def residual1(n):
                    pair = slice(2 * n, 2 * n + 2)
                    if n == 0:
                        dve.wait_ge(x_add1_done.sem, x_add1_done.at(b, 1))
                    dve.wait_ge(gelu_done.sem, gelu_done.at(b, n + 1))
                    dve.tensor_tensor(x_tok[:, pair, :], x_tok[:, pair, :], t1[:, pair, :], ALU.add)\
                       .then_inc(x1_done.sem, 1)
                    dve.wait_ge(x1_done.sem, x1_done.at(b, n + 1))
                    norm_bn(b, NORM_EXPAND, n, x_tok)
                    if n % 2:
                        norm_aggr(b, NORM_EXPAND, n // 2)

                def sums(i, pairs_of_units):
                    for k in pairs_of_units:
                        dve.wait_ge(relu_done.sem, relu_done.at(b, i * PAIRS + k + 1))
                        if k == 0:
                            dve.tensor_scalar(g_acc[i], relu_s[i][:, 0, :], w2p[:, 0:1], b2p[:], ALU.mult, ALU.add)\
                               .then_inc(g_done.sem, 1)
                            continue
                        dve.wait_ge(g_done.sem, g_done.at(b, i * PAIRS + k))
                        dve.scalar_tensor_tensor(out=g_acc[i], in0=relu_s[i][:, k % 2, :], scalar=w2p[:, k:k + 1],
                                                 in1=g_acc[i], op0=ALU.mult, op1=ALU.add).then_inc(g_done.sem, 1)

                def residual2(s):
                    dve.wait_ge(x_bout_done.sem, x_bout_done.at(b, s + 1))
                    for tp in (2 * s, 2 * s + 1):
                        pair = slice(2 * tp, 2 * tp + 2)
                        dve.wait_ge(fo_full.sem, fo_full.at(b, tp + 1))
                        dve.tensor_tensor(x_tok[:, pair, :], bank[tp][:].rearrange("p (t d) -> p t d", d=D),
                                          x_tok[:, pair, :], ALU.add).then_inc(x2_done.sem, 1)
                        dve.wait_ge(x2_done.sem, x2_done.at(b, tp + 1))
                        norm_bn(b, NORM_PROJECT, tp, x_tok)
                    norm_aggr(b, NORM_PROJECT, s)

                def latent_lo(i):
                    at = slice(i * NB, (i + 1) * NB)
                    dve.wait_ge(lat_hi_done.sem, lat_hi_done.at(b, i + 1))
                    dve.scalar_tensor_tensor(out=latT[1][:, at], in0=bank[2 * i][0:LATENT, :], scalar=bl[:],
                                             in1=latT[0][:, at], op0=ALU.add, op1=ALU.subtract)\
                       .then_inc(lat_lo_done.sem, 1)

                def k_los(i):
                    at = slice(i * NB, (i + 1) * NB)
                    for m in range(KC):
                        dve.wait_ge(k1_hi_done.sem, k1_hi_done.at(b, KC * i + m + 1))
                        dve.scalar_tensor_tensor(out=kT_lo[:, m, at], in0=bank[4 + KC * i + m][:],
                                                 scalar=bk[:, m:m + 1], in1=kT_hi[:, m, at],
                                                 op0=ALU.add, op1=ALU.subtract).then_inc(k1_lo_done.sem, 1)

                def q_los(i):
                    at = slice(i * NB, (i + 1) * NB)
                    for m in range(KC):
                        dve.wait_ge(q1_hi_done.sem, q1_hi_done.at(b, KC * i + m + 1))
                        dve.scalar_tensor_tensor(out=qT_lo[:, m, at], in0=bank[KC * i + m][:],
                                                 scalar=bq[:, m:m + 1], in1=qT_hi[:, m, at],
                                                 op0=ALU.add, op1=ALU.subtract).then_inc(q1_lo_done.sem, 1)

                def values_out(i):
                    for tp in (2 * i, 2 * i + 1):
                        dve.wait_ge(v1_full.sem, v1_full.at(b, tp + 1))
                        dve.tensor_tensor(v_aug[:, 2 * tp:2 * tp + 2, :, 0:DH],
                                          bank[4 + tp][:].rearrange("p (t h c) -> p t h c", t=2, c=DH),
                                          bv_all[:].rearrange("p (h c) -> p h c", c=DH).unsqueeze(1)
                                          .to_broadcast([P, 2, HEADS, DH]), ALU.add).then_inc(v1_done.sem, 1)

                xT_los(b, T_FFN, 0)
                norm_apply(b, NORM_FFN, 1, add1, n_tok)
                xT_los(b, T_FFN, 1)
                ffn_out(0)
                residual1(0)
                ffn_out(1)
                residual1(1)
                norm_apply(b, NORM_EXPAND, 0, x_tok, n_tok)
                xT_los(b, T_EXPAND, 0)
                sums(0, range(2))
                ffn_out(2)
                sums(0, range(2, 5))
                residual1(2)
                sums(0, range(5, 7))
                ffn_out(3)
                sums(0, range(7, PAIRS))
                residual1(3)
                norm_apply(b, NORM_EXPAND, 1, x_tok, n_tok)
                residual2(0)
                xT_los(b, T_EXPAND, 1)
                norm_apply(b, NORM_PROJECT, 0, x_tok, n_tok)
                sums(1, range(4))
                xT_los(b, T_PROJECT, 0)
                sums(1, range(4, PAIRS))
                latent_lo(0)
                residual2(1)
                k_los(0)
                norm_apply(b, NORM_PROJECT, 1, x_tok, n_tok)
                q_los(0)
                xT_los(b, T_PROJECT, 1)
                latent_lo(1)
                values_out(0)
                k_los(1)
                q_los(1)
                values_out(1)
                def unit_maxima(u):
                    dve.wait_ge(rows_max_done.sem, rows_max_done.at(b, MAX_TILES * (u + 1)))
                    if u:
                        dve.wait_ge(mT_full.sem, mT_full.at(b, u))
                    dve.tensor_reduce(head_max[:], row_max[:, u % 2], AX_X, ALU.max).then_inc(max_step.sem, 1)
                    dve.wait_ge(max_step.sem, max_step.at(b, 2 * u + 1))
                    dve.tensor_scalar(m16[:, :, :, 0], head_max[:], -1.0 / MAX_UNIT, None, ALU.mult)\
                       .then_inc(max_step.sem, 1)
                    dve.wait_ge(max_step.sem, max_step.at(b, 2 * u + 2))
                    dve.scalar_tensor_tensor(out=m16[:, :, :, 1], in0=head_max[:], scalar=-1.0 / MAX_UNIT,
                                             in1=m16[:, :, :, 0], op0=ALU.mult, op1=ALU.subtract)\
                       .then_inc(m16_done.sem, 1)

                def sums_of_heads(u):
                    g, ib = divmod(u, IB)
                    dve.wait_ge(o_done.sem, o_done.at(b, u + 1))
                    if u:
                        dve.wait_ge(den_step.sem, den_step.at(b, (1 + DIV_PARTS) * u))
                    carry_wait()
                    dve.stream_shuffle(den1[:, 0, :], oT[:, g, ib * NB:(ib + 1) * NB], mask=[DH] * 32)\
                       .then_inc(den_step.sem, 1)

                def reciprocals(u, first, parts):
                    at = slice(first * NB // DIV_PARTS, (first + parts) * NB // DIV_PARTS)
                    if first == 0:
                        dve.wait_ge(den_step.sem, den_step.at(b, (1 + DIV_PARTS) * u + 1))
                        if u >= 2:
                            dve.wait_ge(att1_done.sem, att1_done.at(b, u - 1))
                    dve.reciprocal(den1[:, 1 + u % 2, at], den1[:, 0, at]).then_inc(den_step.sem, parts)

                for n in range(UNITS * MAX_TILES):
                    u, r = divmod(n, MAX_TILES)
                    hh, it, jb = r // TT, (r // IB) % (TT // IB), r % IB
                    dve.wait_ge(rows_full.sem, rows_full.at(b, n + 1))
                    if r == 0 and u >= 2:
                        dve.wait_ge(m16_done.sem, m16_done.at(b, u - 1))
                    dve.tensor_reduce(row_max[:, u % 2, it, hh, jb:jb + 1], bank[ROW_BANK[n % 3]][:], AX_X, ALU.max)\
                       .then_inc(rows_max_done.sem, 1)
                    if r == MAX_TILES - 1:
                        unit_maxima(u)
                    done, step_in = divmod(n - DIV_AFTER, MAX_TILES)
                    if 0 <= done < STREAMED and step_in % 4 == 0:
                        if step_in == 0:
                            sums_of_heads(done)
                        reciprocals(done, step_in // 4, 1)
                for u in range(STREAMED, UNITS):
                    sums_of_heads(u)
                    reciprocals(u, 0, DIV_PARTS)
                for tp in range(4):
                    pair = slice(2 * tp, 2 * tp + 2)
                    dve.wait_ge(o1_full.sem, o1_full.at(b, tp + 1))
                    dve.tensor_tensor(x_tok[:, pair, :], bank[tp][:].rearrange("p (t d) -> p t d", d=D),
                                      x_tok[:, pair, :], ALU.add).then_inc(x3_done.sem, 1)
                    dve.wait_ge(x3_done.sem, x3_done.at(b, tp + 1))
                    norm_bn(b, NORM_ROUTER, tp, x_tok)
                    if tp % 2:
                        norm_aggr(b, NORM_ROUTER, tp // 2)
                        norm_apply(b, NORM_ROUTER, tp // 2, x_tok, n_tok)
                    if tp == 2:
                        xT_los(b, T_ROUTER, 0)
                def hidden(j):
                    dve.wait_ge(silu_done.sem, silu_done.at(b, j + 1))
                    dve.wait_ge(up_full.sem, up_full.at(b, j + 1))
                    dve.tensor_tensor(silu[:, j % 4, :], silu[:, j % 4, :],
                                      bank[5 + 2 * (j % 2)][:], ALU.mult).then_inc(hmoe_done.sem, 1)

                hidden(0)
                hidden(1)
                xT_los(b, T_ROUTER, 1)
                steps = 0

                def step(instruction):
                    nonlocal steps
                    steps += 1
                    instruction.then_inc(route_step.sem, 1)
                    dve.wait_ge(route_step.sem, route_step.at(b, steps))

                def per_expert(v):
                    return v.unsqueeze(2).to_broadcast([P, TT, EXPERTS])

                z, inh, zone, low, dist, w, fb = rt[:, 0], rt[:, 2], rt[:, 3], rt[:, 4], rt[:, 5], rt[:, 6], rt[:, 7]
                rank, chosen, none, rsum = rt[:, 8], rt[:, 9], rt1[:, 0], rt1[:, 1]
                dve.wait_ge(route_full.sem, route_full.at(b, 1))
                step(dve.tensor_scalar(z, bank[0][:, 0:TT * EXPERTS].rearrange("p (t e) -> p t e", e=EXPERTS),
                                       rtemp[:], None, ALU.mult))
                assert steps == ROUTE_Z
                dve.wait_ge(route_exp.sem, route_exp.at(b, 1))
                step(dve.tensor_scalar(rt[:, 10], rt[:, 1], 1.0, None, ALU.add))
                step(dve.reciprocal(inh, rt[:, 10]))
                step(dve.tensor_scalar(low, inh, ZONE_LOWER, None, ALU.is_ge))
                step(dve.scalar_tensor_tensor(out=zone, in0=inh, scalar=ZONE_UPPER, in1=low,
                                              op0=ALU.is_le, op1=ALU.mult))
                step(dve.tensor_scalar(rt[:, 11], inh, ZONE_CENTER, None, ALU.subtract))
                step(dve.scalar_tensor_tensor(out=dist, in0=rt[:, 11], scalar=-1.0, in1=rt[:, 11],
                                              op0=ALU.mult, op1=ALU.max))
                assert steps == ROUTE_DIST
                dve.wait_ge(route_exp.sem, route_exp.at(b, 3))
                step(dve.tensor_tensor(rt[:, 10], w, zone, ALU.mult))
                step(dve.tensor_reduce(rsum, rt[:, 10], AX_X, ALU.add))
                step(dve.tensor_scalar(none, rsum, 1e-8, None, ALU.is_lt))
                hidden(2)
                ahead, equal = pairs
                mine = fb.unsqueeze(3).to_broadcast([P, TT, EXPERTS, EXPERTS])
                other = fb.unsqueeze(2).to_broadcast([P, TT, EXPERTS, EXPERTS])
                step(dve.tensor_tensor(ahead, other, mine, ALU.is_gt))
                step(dve.tensor_tensor(equal, other, mine, ALU.is_equal))
                step(dve.tensor_tensor(equal, equal, before[:].unsqueeze(1).to_broadcast(
                    [P, TT, EXPERTS, EXPERTS]), ALU.mult))
                step(dve.tensor_tensor(ahead, ahead, equal, ALU.add))
                hidden(3)
                step(dve.tensor_reduce(rank, ahead, AX_X, ALU.add))
                step(dve.scalar_tensor_tensor(out=chosen, in0=rank, scalar=2.0, in1=fb,
                                              op0=ALU.is_lt, op1=ALU.mult))
                step(dve.tensor_reduce(rt1[:, 2], chosen, AX_X, ALU.add))
                step(dve.tensor_scalar(rt1[:, 3], rt1[:, 2], 1e-8, None, ALU.max))
                step(dve.reciprocal(rt1[:, 4], rt1[:, 3]))
                step(dve.tensor_tensor(chosen, chosen, per_expert(rt1[:, 4]), ALU.mult))
                step(dve.tensor_tensor(chosen, chosen, per_expert(none), ALU.mult))
                step(dve.tensor_scalar(rt1[:, 5], none, -1.0, 1.0, ALU.mult, ALU.add))
                step(dve.tensor_tensor(rt[:, 11], rt[:, 10], per_expert(rt1[:, 5]), ALU.mult))
                step(dve.tensor_tensor(rt[:, 11], rt[:, 11], chosen, ALU.add))
                step(dve.tensor_reduce(rt1[:, 2], rt[:, 11], AX_X, ALU.add))
                step(dve.tensor_scalar(rt1[:, 3], rt1[:, 2], 1e-8, None, ALU.max))
                step(dve.reciprocal(rt1[:, 4], rt1[:, 3]))
                step(dve.tensor_tensor(rt[:, 10], rt[:, 11], per_expert(rt1[:, 4]), ALU.mult))
                route_w = rt[:, 10]
                assert steps == ROUTE_STEPS, steps

                def weigh(e):
                    for t in range(TT):
                        if t % 2 == 0:
                            dve.wait_ge(down_full.sem, down_full.at(b, 4 * e + t // 2 + 1))
                        if e:
                            dve.wait_ge(moe_done.sem, moe_done.at(b, (e - 1) * TT + t + 1))
                        dve.scalar_tensor_tensor(out=moe_acc[:, t, :], in0=bank[t // 2][:, (t % 2) * D:(t % 2 + 1) * D],
                                                 scalar=route_w[:, t, e:e + 1],
                                                 in1=(moe_acc if e else x_tok)[:, t, :],
                                                 op0=ALU.mult, op1=ALU.add).then_inc(moe_done.sem, 1)

                for e in range(1, EXPERTS):
                    for j in range(4 * e, 4 * e + 4):
                        hidden(j)
                    weigh(e - 1)
                    if e == 2:
                        next_stats(b)
                    if e == 3:
                        next_apply(b)
                    if e == 4:
                        next_ln1_stats(b)
                    if e == 5:
                        next_ln1_apply(b)
                for i in range(IB):
                    xT_los(b, T_NEXT, i)
                weigh(EXPERTS - 1)


ROUTE_Z = 1
ROUTE_DIST = 7

_INS = ['L0_attn_x', 'L0_attn_gamma1', 'L0_attn_beta1', 'L0_attn_wq', 'L0_attn_wk', 'L0_attn_wv', 'L0_attn_wo',
        'L0_attn_w1', 'L0_attn_b1', 'L0_attn_w2', 'L0_attn_b2', 'L0_ffn_Win', 'L0_ffn_bin_', 'L0_ffn_W1',
        'L0_ffn_b1', 'L0_ffn_W2', 'L0_ffn_b2', 'L0_ffn_Wout', 'L0_ffn_bout', 'L1_attn_Wq', 'L1_attn_bq',
        'L1_attn_Wl', 'L1_attn_bl', 'L1_attn_Wk', 'L1_attn_bk', 'L1_attn_Wv', 'L1_attn_bv', 'L1_attn_Wo',
        'L1_attn_bo', 'L1_ffn_Wg', 'L1_ffn_Wu', 'L1_ffn_Wd', 'L1_ffn_Wr', 'L1_ffn_temperature']


def kernel(**inputs):
    import numpy as _np
    import concourse.bacc as _bacc
    from concourse import mybir as _mybir
    from concourse.bass_utils import run_bass_kernel_spmd as _run

    nc = _bacc.Bacc("TRN2", target_bir_lowering=False, num_devices=1)
    arrays, args = {}, {}
    for name in _INS:
        a = _np.ascontiguousarray(inputs[name])
        arrays[f"in_{name}_dram"] = a
        args[name] = nc.dram_tensor(f"in_{name}_dram", a.shape, _mybir.dt.from_np(a.dtype),
                                    kind="ExternalInput").ap()
    out = nc.dram_tensor("out_0_dram", (BATCH, TOKENS, D), F32, kind="ExternalOutput").ap()
    build(nc, args, out)
    r = _run(nc, [arrays], core_ids=[0])
    return r.results[0]["out_0_dram"]
```
